# Optimizing a Trainium2 kernel written in Bass

```python
import numpy as np
import jax
import jax.numpy as jnp

def _softmax(x, axis=-1):
    return jax.nn.softmax(x, axis=axis)

def _gelu(x):
    return jax.nn.gelu(x, approximate=True)

def _silu(x):
    return jax.nn.silu(x)

def _sigmoid(x):
    return jax.nn.sigmoid(x)

def _layernorm(x, axis=-1, eps=1e-05):
    m = jnp.mean(x, axis=axis, keepdims=True)
    v = jnp.var(x, axis=axis, keepdims=True)
    return (x - m) / jnp.sqrt(v + eps)

def _scatter_add(tgt, idx, src, axis=0):
    return tgt.at[idx].add(src)

def _segment_sum(src, seg, n):
    return jax.ops.segment_sum(src, seg, n)
kernel_name = 'mk_hybrid_d1_jaxref_r8_5dcdee'

def setup_inputs(seed: int=0):
    np.random.seed(seed)
    _w = jnp.asarray

    def _L0_attn_a_setup():
        import jax, jax.numpy as jnp
        import numpy as np
        DIM = 128
        H = 16
        HD = DIM // H // 2
        LAMBDA_INIT = 0.8 - 0.6 * float(np.exp(-0.3 * 0))
        EPS = 1e-05

        def _rms_norm(x, w, eps):
            return x * jax.lax.rsqrt(jnp.mean(jnp.square(x), axis=-1, keepdims=True) + eps) * w
        key = jax.random.key(seed)
        ks = jax.random.split(key, 9)
        B, N = (4, 512)
        return {'x': jax.random.normal(ks[0], (B, N, DIM), jnp.float32), 'w_qkv': jax.random.normal(ks[1], (3 * DIM, DIM), jnp.float32) * 0.02, 'w_proj': jax.random.normal(ks[2], (DIM, DIM), jnp.float32) * 0.02, 'b_proj': jnp.zeros((DIM,), jnp.float32), 'lambda_q1': jax.random.normal(ks[3], (HD,), jnp.float32) * 0.1, 'lambda_k1': jax.random.normal(ks[4], (HD,), jnp.float32) * 0.1, 'lambda_q2': jax.random.normal(ks[5], (HD,), jnp.float32) * 0.1, 'lambda_k2': jax.random.normal(ks[6], (HD,), jnp.float32) * 0.1, 'sub_norm_w': jnp.ones((2 * HD,), jnp.float32)}
    _L0_attn_a_in = _L0_attn_a_setup()

    def _L0_attn_b_setup():
        import jax, jax.numpy as jnp
        import numpy as np
        HID = 128
        HEADS = 16
        HEAD_DIM = HID // HEADS
        key = jax.random.key(seed)
        ks = jax.random.split(key, 6)
        N, S = (4, 512)
        scale = 1.0 / np.sqrt(HID)
        return {'x': jax.random.normal(ks[0], (N, S, HID), dtype=jnp.float32), 'Wq': jax.random.normal(ks[1], (HID, HID), dtype=jnp.float32) * scale, 'Wk': jax.random.normal(ks[2], (HID, HID), dtype=jnp.float32) * scale, 'Wv': jax.random.normal(ks[3], (HID, HID), dtype=jnp.float32) * scale, 'Wo': jax.random.normal(ks[4], (HID, HID), dtype=jnp.float32) * scale, 'bo': jnp.zeros((HID,), dtype=jnp.float32)}
    _L0_attn_b_in = _L0_attn_b_setup()

    def _L0_ffn_setup():
        import jax, jax.numpy as jnp
        import numpy as np
        TOP_K = 8
        key = jax.random.key(seed)
        ks = jax.random.split(key, 6)
        B, S, D, F, E = (2, 128, 128, 64, 64)
        x = jax.random.normal(ks[0], (B, S, D), dtype=jnp.float32)
        centroids = jax.random.normal(ks[1], (E, D), dtype=jnp.float32) * 0.05
        expert_biases = jnp.zeros((E,), dtype=jnp.float32)
        Ws_up = jax.random.normal(ks[2], (D, F), dtype=jnp.float32) / np.sqrt(D)
        Ws_down = jax.random.normal(ks[3], (F, D), dtype=jnp.float32) / np.sqrt(F)
        W_up = jax.random.normal(ks[4], (E, D, F), dtype=jnp.float32) / np.sqrt(D)
        W_down = jax.random.normal(ks[5], (E, F, D), dtype=jnp.float32) / np.sqrt(F)
        return {'x': x, 'centroids': centroids, 'expert_biases': expert_biases, 'Ws_up': Ws_up, 'Ws_down': Ws_down, 'W_up': W_up, 'W_down': W_down}
    _L0_ffn_in = _L0_ffn_setup()
    _d = {'L0_attn_a_x': _L0_attn_a_in['x'], 'L0_attn_a_w_qkv': _L0_attn_a_in['w_qkv'], 'L0_attn_a_w_proj': _L0_attn_a_in['w_proj'], 'L0_attn_a_b_proj': _L0_attn_a_in['b_proj'], 'L0_attn_a_lambda_q1': _L0_attn_a_in['lambda_q1'], 'L0_attn_a_lambda_k1': _L0_attn_a_in['lambda_k1'], 'L0_attn_a_lambda_q2': _L0_attn_a_in['lambda_q2'], 'L0_attn_a_lambda_k2': _L0_attn_a_in['lambda_k2'], 'L0_attn_a_sub_norm_w': _L0_attn_a_in['sub_norm_w'], 'L0_attn_b_Wq': _L0_attn_b_in['Wq'], 'L0_attn_b_Wk': _L0_attn_b_in['Wk'], 'L0_attn_b_Wv': _L0_attn_b_in['Wv'], 'L0_attn_b_Wo': _L0_attn_b_in['Wo'], 'L0_attn_b_bo': _L0_attn_b_in['bo'], 'L0_ffn_centroids': _L0_ffn_in['centroids'], 'L0_ffn_expert_biases': _L0_ffn_in['expert_biases'], 'L0_ffn_Ws_up': _L0_ffn_in['Ws_up'], 'L0_ffn_Ws_down': _L0_ffn_in['Ws_down'], 'L0_ffn_W_up': _L0_ffn_in['W_up'], 'L0_ffn_W_down': _L0_ffn_in['W_down']}
    _x0 = _d['L0_attn_a_x']
    _d['L0_attn_a_x'] = jax.random.normal(jax.random.fold_in(jax.random.key(seed), 1), (2, 1024, 128), dtype=_x0.dtype)
    del _x0
    return _d

def reference(L0_attn_a_x, L0_attn_a_w_qkv, L0_attn_a_w_proj, L0_attn_a_b_proj, L0_attn_a_lambda_q1, L0_attn_a_lambda_k1, L0_attn_a_lambda_q2, L0_attn_a_lambda_k2, L0_attn_a_sub_norm_w, L0_attn_b_Wq, L0_attn_b_Wk, L0_attn_b_Wv, L0_attn_b_Wo, L0_attn_b_bo, L0_ffn_centroids, L0_ffn_expert_biases, L0_ffn_Ws_up, L0_ffn_Ws_down, L0_ffn_W_up, L0_ffn_W_down):

    def _L0_attn_a_ref(x, w_qkv, w_proj, b_proj, lambda_q1, lambda_k1, lambda_q2, lambda_k2, sub_norm_w):
        import jax, jax.numpy as jnp
        import numpy as np
        DIM = 128
        H = 16
        HD = DIM // H // 2
        LAMBDA_INIT = 0.8 - 0.6 * float(np.exp(-0.3 * 0))
        EPS = 1e-05

        def _rms_norm(x, w, eps):
            return x * jax.lax.rsqrt(jnp.mean(jnp.square(x), axis=-1, keepdims=True) + eps) * w
        B, N, C = x.shape
        scale = HD ** (-0.5)
        qkv = x @ w_qkv.T
        q, k, v = jnp.split(qkv, 3, axis=-1)
        q = q.reshape(B, N, H, 2, HD)
        k = k.reshape(B, N, H, 2, HD)
        v = v.reshape(B, N, H, 2 * HD)
        lam = jnp.exp(jnp.sum(lambda_q1 * lambda_k1)) - jnp.exp(jnp.sum(lambda_q2 * lambda_k2)) + LAMBDA_INIT

        def sdpa(qi, ki):
            s = jnp.einsum('bnhd,bmhd->bhnm', qi, ki) * scale
            p = jax.nn.softmax(s, axis=-1)
            return jnp.einsum('bhnm,bmhe->bhne', p, v)
        a1 = sdpa(q[:, :, :, 0], k[:, :, :, 0])
        a2 = sdpa(q[:, :, :, 1], k[:, :, :, 1])
        o = a1 - lam * a2
        o = _rms_norm(o, sub_norm_w, EPS) * (1.0 - LAMBDA_INIT)
        o = o.transpose(0, 2, 1, 3).reshape(B, N, C)
        return o @ w_proj.T + b_proj

    def _L0_attn_b_ref(x, Wq, Wk, Wv, Wo, bo):
        import jax, jax.numpy as jnp
        import numpy as np
        HID = 128
        HEADS = 16
        HEAD_DIM = HID // HEADS
        N, S, _ = x.shape
        q = (x @ Wq).reshape(N, S, HEADS, HEAD_DIM)
        k = (x @ Wk).reshape(N, S, HEADS, HEAD_DIM)
        v = (x @ Wv).reshape(N, S, HEADS, HEAD_DIM)
        q = jnp.swapaxes(q, 1, 2)
        k = jnp.swapaxes(k, 1, 2)
        v = jnp.swapaxes(v, 1, 2)
        energy = jnp.einsum('nahd,nbhd->nab', q, k)
        attention = jax.nn.softmax(energy / np.sqrt(HEAD_DIM), axis=2)
        out = jnp.einsum('nab,nbsd->nasd', attention, v)
        out = out.reshape(N, S, HID)
        return out @ Wo + bo

    def _L0_ffn_ref(x, centroids, expert_biases, Ws_up, Ws_down, W_up, W_down):
        import jax, jax.numpy as jnp
        import numpy as np
        TOP_K = 8
        B, S, D = x.shape
        E = centroids.shape[0]
        T = B * S
        xf = x.reshape(T, D)
        shared = jax.nn.silu(xf @ Ws_up) @ Ws_down
        aff = xf @ centroids.T
        biased = aff + expert_biases
        _, idx = jax.lax.top_k(biased, TOP_K)
        sel = jnp.take_along_axis(aff, idx, axis=1)
        w = jax.nn.sigmoid(sel)
        w = w / (jnp.sum(w, axis=-1, keepdims=True) + 1e-08)
        cw = jnp.zeros((T, E), dtype=x.dtype).at[jnp.arange(T)[:, None], idx].add(w)
        h = jax.nn.silu(jnp.einsum('td,edf->etf', xf, W_up))
        y = jnp.einsum('etf,efd->etd', h, W_down)
        routed = jnp.einsum('etd,te->td', y, cw)
        return (shared + routed).reshape(B, S, D)
    x = L0_attn_a_x
    x = x + _L0_attn_a_ref(_layernorm(x, axis=-1), L0_attn_a_w_qkv, L0_attn_a_w_proj, L0_attn_a_b_proj, L0_attn_a_lambda_q1, L0_attn_a_lambda_k1, L0_attn_a_lambda_q2, L0_attn_a_lambda_k2, L0_attn_a_sub_norm_w)
    x = x + _L0_ffn_ref(_layernorm(x, axis=-1), L0_ffn_centroids, L0_ffn_expert_biases, L0_ffn_Ws_up, L0_ffn_Ws_down, L0_ffn_W_up, L0_ffn_W_down)
    x = x + _L0_attn_b_ref(_layernorm(x, axis=-1), L0_attn_b_Wq, L0_attn_b_Wk, L0_attn_b_Wv, L0_attn_b_Wo, L0_attn_b_bo)
    x = x + _L0_ffn_ref(_layernorm(x, axis=-1), L0_ffn_centroids, L0_ffn_expert_biases, L0_ffn_Ws_up, L0_ffn_Ws_down, L0_ffn_W_up, L0_ffn_W_down)
    return x

_drawn_inputs = setup_inputs


def setup_inputs(seed=0):
    import zlib

    import numpy as np

    out = dict(_drawn_inputs(seed))
    spreads = {'L0_attn_a_b_proj': (0.0, 0.1),
     'L0_attn_a_sub_norm_w': (1.0, 0.2),
     'L0_attn_b_bo': (0.0, 0.1),
     'L0_ffn_expert_biases': (0.0, 0.1)}
    factors = {'L0_attn_a_lambda_q1': 8.0,
     'L0_attn_a_lambda_k1': 8.0,
     'L0_attn_a_lambda_q2': 8.0,
     'L0_attn_a_lambda_k2': 8.0}
    for name, (base, spread) in spreads.items():
        noise = np.random.default_rng([zlib.crc32(name.encode()), seed]).standard_normal(out[name].shape)
        drawn = base * np.exp(spread * noise) if base else spread * noise
        out[name] = jnp.asarray(drawn.astype(out[name].dtype))
    for name, factor in factors.items():
        out[name] = (out[name] * factor).astype(out[name].dtype)
    return out
```

```python
from contextlib import ExitStack

import numpy as np

import concourse.bass as bass
from concourse import mybir

F32 = mybir.dt.float32
F32R = mybir.dt.float32r
BF16 = mybir.dt.bfloat16
ALU = mybir.AluOpType
ACT = mybir.ActivationFunctionType
AX_X = mybir.AxisListType.X

P = 128
BATCH, SEQ, DIM = 2, 1024, 128
NT = BATCH * SEQ // P
TB = SEQ // P
TOK = BATCH * SEQ
BANK = 512
NCH = TOK // BANK
LN_EPS = 1e-5

HEADS_A = 16
HD_A = DIM // HEADS_A // 2
SUBS = 2 * HEADS_A
R = 4
GPB = SUBS // R
NG = BATCH * GPB
VD = 2 * HD_A
SCALE_A = HD_A ** -0.5
LAMBDA_INIT = 0.8 - 0.6 * float(np.exp(-0.3 * 0))
EPS_A = 1e-5
Q_SLOTS = (0, 0, 0, 1, 1, 2)
K_SLOTS = (0, 1, 2, 0, 1, 0)
SHIFT_ROW = HD_A * len(Q_SLOTS)
STRIP = 32

QPG = 2 * TB
NQ = NG * QPG
LEAD = 20
BODY = 2 * QPG
HEAD_Q = 4
LOOPS = (NQ - BODY) // BODY
PRING = 4

HEADS_B = 16
HD_B = DIM // HEADS_B
SCALE_B = float(1.0 / np.sqrt(HD_B))
S0 = HEADS_B
S1 = SEQ // S0

E, F, TOPK = 64, 64, 8
PAIRS = E // 2
UNITS = PAIRS + 1
LAG = 3


def max_pass_items():
    index = {}
    for g in range(-LEAD, NQ + 4):
        for key in quad_items(g):
            index[key] = len(index)
    return index


def quad_items(g):
    items = []
    if 0 <= g + LEAD < NQ:
        items.append(("max", g + LEAD, 0))
    if (g + 3) % QPG == 0 and 0 <= (g + 3) // QPG < NG:
        items.append(("shift", (g + 3) // QPG))
    if g >= 10 and (g - 10) % TB == 0 and (g - 10) // TB < 2 * NG:
        items.append(("out", (g - 10) // TB // 2, (g - 10) // TB % 2))
    if 0 <= g + LEAD < NQ:
        items.append(("max", g + LEAD, 1))
    return items


ITEM = max_pass_items()
ITEMS_PER_BODY = 2 * BODY + 2 + 4


def ring_order(names):
    return {n: i for i, n in enumerate(names)}


A_ITEM = ring_order(
    ["wT", "centT"] + [("xT", 0, c) for c in range(NCH)] + [("va", c) for c in range(NCH)]
    + [("oT", c) for c in range(NCH)]
    + [("xT", 1, c) for c in range(NCH)] + [("cwT", 0, c) for c in range(NCH)]
    + [("xT", 2, c) for c in range(NCH)]
    + [("vp", c) for c in range(NCH)]
    + [("xT", 3, c) for c in range(NCH)] + [("cwT", 1, c) for c in range(NCH)])
D_ITEM = ring_order(
    [("qk", j, c) for c in range(NCH) for j in range(2)] + [("proj", c) for c in range(NCH)]
    + [("aff", 0, h) for h in range(2)] + [("out_b", c) for c in range(NCH)] + [("aff", 1, h) for h in range(2)])


def hybrid_layer(nc, x, w_qkv, w_proj, b_proj, lam_q1, lam_k1, lam_q2, lam_k2, sub_w,
                 w_q, w_k, w_v, w_o, b_o, cent, e_bias, ws_up, ws_down, w_up, w_down, out):
    ctx = ExitStack()
    with ctx:
        names = [0]

        def sb(name, shape, dt=F32, where=ctx):
            return where.enter_context(nc.sbuf_tensor(name, shape, dt))

        def sem(name):
            return ctx.enter_context(nc.semaphore(name))

        X = sb("X", [P, NT, DIM])
        XC = sb("XC", [P, NT, DIM])
        SQ = sb("SQ", [P, NT, DIM])
        XT = sb("XT", [P, TOK])
        ln_s = sb("ln_s", [P, NT]); ln_m = sb("ln_m", [P, NT]); ln_v = sb("ln_v", [P, NT])
        ln_sd = sb("ln_sd", [P, NT]); ln_r = sb("ln_r", [P, NT]); ln_t = sb("ln_t", [P, NT])
        WUH = sb("WUH", [P, E * F], F32R); WUL = sb("WUL", [P, E * F], F32R)
        WDH = sb("WDH", [P, PAIRS * DIM], F32R); WDL = sb("WDL", [P, PAIRS * DIM], F32R)
        WSUH = sb("WSUH", [P, P], F32R); WSUL = sb("WSUL", [P, P], F32R)
        WSDH = sb("WSDH", [P, DIM], F32R); WSDL = sb("WSDL", [P, DIM], F32R)
        SEL = sb("SEL", [P, PAIRS * P], F32R)
        ident = sb("ident", [P, P]); identb = sb("identb", [P, P], BF16)
        WQKV = sb("WQKV", [P, 3, DIM]); WPRJ = sb("WPRJ", [P, DIM]); CENT = sb("CENT", [E, DIM])
        WT = sb("WT", [P, 4, DIM])
        CT = sb("CT", [P, E]); WVT = sb("WVT", [P, DIM])
        T8 = sb("T8", [P, HD_B]); H16 = sb("H16", [P, HEADS_B])
        BLK = sb("BLK", [P, DIM])
        WB = sb("WB", [P, 4, DIM])
        BPROJ = sb("BPROJ", [P, DIM]); BO = sb("BO", [P, DIM]); EBIAS = sb("EBIAS", [P, E])
        SUBW = sb("SUBW", [P, VD])
        LAM = sb("LAM", [P, 4, HD_A]); lam_p = sb("lam_p", [P, 2, HD_A]); lam_s = sb("lam_s", [P, 2])
        lam_e = sb("lam_e", [P, 2]); neg_lam = sb("neg_lam", [P, 1])

        VALL = XC[:].rearrange("p t c -> p (t c)").rearrange("p (g t v) -> p g t v", g=NG, t=TB)
        O = XT[:].rearrange("p (g t v) -> p g t v", g=NG, t=TB)

        prep = ExitStack()
        RAWU = sb("RAWU", [P, E * F], where=prep); RAWD = sb("RAWD", [P, PAIRS * DIM], where=prep)
        PARTS = sb("PARTS", [P, 3, 2, TOK], BF16, where=prep)
        R1 = XC[:, 0:2 * BANK // DIM, :].rearrange("p t c -> p (t c)").rearrange("p (j n) -> p j n", j=2)
        SELF = SQ
        RAWSU = sb("RAWSU", [P, P], where=prep); RAWSD = sb("RAWSD", [P, DIM], where=prep)
        ZEROS = sb("ZEROS", [P, SEQ], BF16, where=prep); ONES = sb("ONES", [P, SEQ], BF16, where=prep)
        prep.close()

        attn = ExitStack()
        PR = sb("PR", [P, PRING, R, BANK], where=attn)
        KB = sb("KB", [P, 2, R, SEQ], BF16, where=attn)
        QB = sb("QB", [P, 2, SEQ], BF16, where=attn)
        VG = sb("VG", [P, 2, TB, 2, STRIP], where=attn)
        OTS = sb("OTS", [P, 2, BANK], where=attn)
        SHP = sb("SHP", [P, 2, 3 * R * TB], BF16, where=attn)
        SHT = sb("SHT", [3 * R * TB, 2, P], BF16, where=attn)
        ZERO = sb("ZERO", [P, R * TB], where=attn)
        QA = sb("QA", [P, 2, R, SEQ], BF16, where=attn)
        KA = sb("KA", [P, 2, SEQ], BF16, where=attn)
        NEGMAX = sb("NEGMAX", [P, 2, R * TB], where=attn); SHR = sb("SHR", [P, R * TB], where=attn)
        RD = sb("RD", [P, 4 * R], where=attn); TM = sb("TM", [P, 4 * R, VD], where=attn)
        attn.close()
        rms_s, rms_sd, rms_r, rms_t = (PR[:, 0, j, 0:NG * TB * 2] for j in range(4))

        bctx = ExitStack()
        GRAM = sb("GRAM", [P, BATCH, DIM], where=bctx); GK = sb("GK", [P, BATCH, DIM], where=bctx)
        QK = sb("QK", [P, BATCH, DIM], where=bctx); QKR = sb("QKR", [P, BATCH * HEADS_B], where=bctx)
        EN = sb("EN", [P, BATCH, HEADS_B], where=bctx); en_m = sb("en_m", [P, BATCH], where=bctx)
        en_s = sb("en_s", [P, BATCH], where=bctx); en_r = sb("en_r", [P, BATCH], where=bctx)
        MIXT = sb("MIXT", [P, BATCH, DIM], where=bctx); MIX = sb("MIX", [P, BATCH, DIM], where=bctx)
        VMIX = sb("VMIX", [P, BATCH, DIM], where=bctx)
        VP = sb("VP", [P, BATCH, S0, S1], where=bctx); RT = sb("RT", [P, BATCH, SEQ], where=bctx)
        bctx.close()

        XH = sb("XH", [P, TOK], F32R); XL = sb("XL", [P, TOK], F32R)
        CWT = sb("CWT", [P, TOK], F32R)
        AFF = sb("AFF", [P, NT, E]); BI = sb("BI", [P, NT, E]); BR = sb("BR", [P, NT, E])
        EX, CH = AFF, SQ
        CWH = sb("CWH", [P, NT, E], F32R); CWL = sb("CWL", [P, NT, E], F32R)
        top8 = sb("top8", [P, NT, TOPK]); wsum = sb("wsum", [P, NT]); wrec = sb("wrec", [P, NT])
        SI = sb("SI", [P, 3, BANK]); HF = sb("HF", [P, 3, BANK])
        HH = sb("HH", [P, 3, BANK], F32R); HL = sb("HL", [P, 3, BANK], F32R)
        YS = sb("YS", [P, BANK])

        PS = ctx.enter_context(nc.psum_tensor("PS", [P, 8, BANK], F32))

        q_stack = nc.dram_tensor("q_stack", (NG, R, STRIP, SEQ), BF16, kind="Internal").ap()
        k_stack = nc.dram_tensor("k_stack", (NG, R, STRIP, SEQ), BF16, kind="Internal").ap()
        mixed_d = nc.dram_tensor("mixed_d", (BATCH, S0, HEADS_B, HD_B, S1), F32, kind="Internal").ap()
        shift_d = nc.dram_tensor("shift_d", (2, 3, R, SEQ), BF16, kind="Internal").ap()

        ld_x, ld_w, ld_mix, ld_exp, ld_b = (sem(n) for n in ("ld_x", "ld_w", "ld_mix", "ld_exp", "ld_b"))
        ident_ok, identb_ok, const_ok, sel_f, sel_r = (sem(n) for n in ("ident_ok", "identb_ok", "const_ok", "sel_f", "sel_r"))
        a_full, a_free, d_full, d_free = (sem(n) for n in ("a_full", "a_free", "d_full", "d_free"))
        dve_step = sem("dve_step")
        pool_step = sem("pool_step")
        xc_ok, sq_ok, ve_ok, sd_ok, xn_ok = (sem(n) for n in ("xc_ok", "sq_ok", "ve_ok", "sd_ok", "xn_ok"))
        lam_in, lam_exp = sem("lam_in"), sem("lam_exp")
        qk_hi, qk_r1, qk_mid, qk_lo = (sem(n) for n in ("qk_hi", "qk_r1", "qk_mid", "qk_lo"))
        st_w = [sem(f"st_w{b}") for b in range(BATCH)]
        w_hi, w_lo = sem("w_hi"), sem("w_lo")
        xb_ok = sem("xb_ok")
        qa_ld = [sem(f"qa_ld{u}") for u in range(2)]
        kb_ld = [sem(f"kb_ld{u}") for u in range(2)]
        m_full, m_free, s_full, p_ready = (sem(n) for n in ("m_full", "m_free", "s_full", "p_ready"))
        av_done, o_evac, o_done, v_cp = (sem(n) for n in ("av_done", "o_evac", "o_done", "v_cp"))
        rd_ok, zeroed = sem("rd_ok"), sem("zeroed")
        sh_split, sh_w, sh_r = sem("sh_split"), sem("sh_w"), sem("sh_r")
        rms_sq, rms_ve, rms_sq2, rms_on = (sem(n) for n in ("rms_sq", "rms_ve", "rms_sq2", "rms_on"))
        xh_ok, xl_ok = sem("xh_ok"), sem("xl_ok")
        aff_ok, ex_ok, ch_ok = sem("aff_ok"), sem("ex_ok"), sem("ch_ok")
        z_full, silu_ok, c_full, hf_ok = (sem(n) for n in ("z_full", "silu_ok", "c_full", "hf_ok"))
        hh_ok, hl_ok, down_ok = sem("hh_ok"), sem("hl_ok"), sem("down_ok")
        y_evac, t_full, t_done = sem("y_evac"), sem("t_full"), sem("t_done")
        blk_ok, b_pe, b_dve, b_exp = (sem(n) for n in ("blk_ok", "b_pe", "b_dve", "b_exp"))
        mix_w = [sem(f"mix_w{b}") for b in range(BATCH)]
        mix_r = [sem(f"mix_r{b}") for b in range(BATCH)]
        stored = sem("stored")

        block = ctx.enter_context(nc.Block())


        @block.sync
        def _(sp):
            sp.dma_start(X[:], x.rearrange("b (n p) c -> p (b n) c", p=P)).then_inc(ld_x, 16)
            sp.dma_start(WQKV[:], w_qkv.rearrange("(j p) c -> p j c", p=P)).then_inc(ld_w, 16)
            sp.dma_start(WPRJ[:], w_proj).then_inc(ld_w, 16)
            sp.dma_start(CENT[:], cent).then_inc(ld_w, 16)
            for j, v in enumerate((lam_q1, lam_k1, lam_q2, lam_k2)):
                sp.dma_start(LAM[:, j, :], v.partition_broadcast(P)).then_inc(ld_mix, 16)
            sp.dma_start(BPROJ[:], b_proj.partition_broadcast(P)).then_inc(ld_mix, 16)
            sp.dma_start(BO[:], b_o.partition_broadcast(P)).then_inc(ld_mix, 16)
            sp.dma_start(EBIAS[:], e_bias.partition_broadcast(P)).then_inc(ld_mix, 16)
            sp.dma_start(SUBW[:], sub_w.partition_broadcast(P)).then_inc(ld_mix, 16)

            for b in range(BATCH):
                sp.wait_ge(qk_mid, 4 * (b + 1))
                sp.wait_ge(qk_lo, 4 * (b + 1))
                if b == 0:
                    sp.wait_ge(const_ok, 2)
                gs = slice(b * GPB, (b + 1) * GPB)
                for j, (stack, slots) in enumerate(((q_stack, Q_SLOTS), (k_stack, K_SLOTS))):
                    def rows(lo):
                        return stack[gs, :, lo:lo + HD_A, :].rearrange("g r d n -> (g r) d n")
                    for c, part in enumerate(slots):
                        sp.dma_start(rows(HD_A * c), PARTS[:, part, j, b * SEQ:(b + 1) * SEQ]).then_inc(st_w[b], 16)
                    fill = ZEROS if j == 0 else ONES
                    sp.dma_start(rows(SHIFT_ROW), fill[:]).then_inc(st_w[b], 16)
                    sp.dma_start(rows(SHIFT_ROW + HD_A), ZEROS[:]).then_inc(st_w[b], 16)

            def load(stack, tile, u, g, there):
                if not isinstance(g, int) or g in (0, GPB):
                    b = 0 if isinstance(g, int) and g < GPB else 1
                    sp.wait_ge(st_w[b], STW)
                if tile is QB or tile is KA:
                    src = stack[bass.ds(g, 1), :, :, :].rearrange("o r s n -> (o r s) n")
                    sp.dma_start(tile[:, u, :], src).then_inc(there, 16)
                    return
                for r in range(R):
                    src = stack[bass.ds(g, 1), r, :, :].rearrange("o s n -> (o s) n")
                    sp.dma_start(tile[STRIP * r:STRIP * (r + 1), u, r, :], src).then_inc(there, 16)

            STW = 16 * 2 * (len(Q_SLOTS) + 2)
            sp.wait_ge(zeroed, 1)
            for u in range(2):
                load(q_stack, QA, u, u, qa_ld[u])
                load(k_stack, KA, u, u, qa_ld[u])
            sp.wait_ge(st_w[1], STW)
            sp.wait_ge(zeroed, 2)
            load(q_stack, QB, 0, 0, sh_w)
            load(k_stack, KB, 0, 0, kb_ld[0])

            def shift_rows(i, s):
                u = s % 2
                sp.wait_ge(m_free, i * ITEMS_PER_BODY + (ITEM["shift", s] + 1))
                sp.dma_start(shift_d[u].rearrange("a r (t n) -> (a r t) n", n=P), SHT[:, u, :]).then_inc(sh_w, 16)
                sp.wait_ge(sh_w, i * 64 + 32 * (s + 1))
                for r in range(R):
                    lo = STRIP * r + SHIFT_ROW
                    sp.dma_start(QB[lo:lo + 3, u, :], shift_d[u, :, r, :]).then_inc(sh_r, 16)

            def group_loads(i, s, more=True):
                u = s % 2
                if s >= 2:
                    sp.wait_ge(s_full, i * (R * BODY) + R * QPG * (s - 1))
                if s:
                    load(q_stack, QB, u, i * 2 + s, sh_w)
                    load(k_stack, KB, u, i * 2 + s, kb_ld[u])
                shift_rows(i, s)
                if more:
                    sp.wait_ge(m_full, i * ITEMS_PER_BODY + (ITEM["max", QPG * s + QPG - 1, 1] + 1))
                    load(q_stack, QA, u, i * 2 + (s + 2), qa_ld[u])
                    load(k_stack, KA, u, i * 2 + (s + 2), qa_ld[u])

            group_loads(0, 0)
            group_loads(0, 1)
            with sp.Fori(0, NG // 2 - 2) as i:
                for s in (2, 3):
                    group_loads(i, s)
            for s in (NG - 2, NG - 1):
                group_loads(0, s, False)
            for b in range(BATCH):
                sp.wait_ge(a_free, A_ITEM["vp", 2 * b + 1] + 1)
                sp.dma_start(mixed_d[b].rearrange("i a d j -> (a d) i j"), VP[:, b, :, :]).then_inc(mix_w[b], 16)
            for b in range(BATCH):
                sp.wait_ge(mix_w[b], 16)
                for i in range(S0):
                    sp.dma_start(RT[HD_B * i:HD_B * (i + 1), b, :].rearrange("d (a j) -> d a j", j=S1),
                                 mixed_d[b, i].rearrange("a d j -> d a j")).then_inc(mix_r[b], 16)
            sp.wait_ge(t_done, 2 * NCH)
            sp.dma_start(out.rearrange("b (n p) c -> p (b n) c", p=P), X[:]).then_inc(stored, 16)
            sp.wait_ge(stored, 16)

        @block.gpsimd
        def _(pool):
            nsteps = [0]

            def link(ins):
                nsteps[0] += 1
                ins.then_inc(pool_step, 1)
                pool.wait_ge(pool_step, nsteps[0])

            link(nc.gpsimd.memset(ident[:], 0.0))
            nc.gpsimd.affine_select(out=ident[:], in_=ident[:], compare_op=ALU.not_equal, fill=1.0, base=0,
                                    pattern=[[-1, P]], channel_multiplier=1).then_inc(ident_ok, 1)
            pool.dma_start(RAWU[:].rearrange("d (e f) -> d e f", f=F), w_up.rearrange("e d f -> d e f")).then_inc(ld_exp, 16)
            pool.dma_start(RAWD[:].rearrange("p (j d) -> p j d", d=DIM),
                           w_down.rearrange("(j e) f d -> (e f) j d", e=2)).then_inc(ld_exp, 16)
            link(nc.gpsimd.memset(RAWSU[:], 0.0))
            link(nc.gpsimd.memset(RAWSD[:], 0.0))
            pool.dma_start(RAWSU[:, 0:F], ws_up).then_inc(ld_exp, 16)
            pool.dma_start(RAWSD[0:F, :], ws_down).then_inc(ld_exp, 16)
            for j, w in enumerate((w_q, w_k, w_v, w_o)):
                pool.dma_start(WB[:, j, :], w).then_inc(ld_b, 16)
            pool.wait_ge(ident_ok, 1)
            nc.gpsimd.tensor_copy(identb[:], ident[:]).then_inc(identb_ok, 1)
            nc.gpsimd.memset(ZEROS[:], 0.0).then_inc(const_ok, 1)
            nc.gpsimd.memset(ONES[:], 1.0).then_inc(const_ok, 1)
            nc.gpsimd.memset(QA[:].bitcast(F32), 0.0).then_inc(zeroed, 1)
            pool.wait_ge(ld_mix, 16 * 8)
            pool.wait_ge(xc_ok, 1)
            nc.gpsimd.tensor_tensor(X[:], X[:], BPROJ[:].unsqueeze(1).to_broadcast([P, NT, DIM]), op=ALU.add).then_inc(xb_ok, 1)
            pool.wait_ge(sq_ok, 1)
            pool.wait_ge(ve_ok, 1)
            for h in range(2):
                sel = SELF[:].rearrange("p t c -> p (t c)").rearrange("p (j e f) -> p j e f", e=2, f=F)
                if h:
                    pool.wait_ge(sel_r, 1)
                link(nc.gpsimd.memset(SELF[:], 0.0))
                for base in (0, -E):
                    ins = nc.gpsimd.affine_select(out=sel, in_=sel, compare_op=ALU.not_equal, fill=1.0,
                                                  base=base - h * PAIRS, pattern=[[-2, PAIRS // 2], [-1, 2], [0, F]],
                                                  channel_multiplier=1)
                    if base == 0:
                        link(ins)
                ins.then_inc(sel_f, 1)

            pool.wait_ge(w_lo, 4)
            for b in range(BATCH):
                pool.wait_ge(st_w[b], 16 * 2 * (len(Q_SLOTS) + 2))
            nc.gpsimd.memset(KB[:].bitcast(F32), 0.0).then_inc(zeroed, 1)
            link(nc.gpsimd.memset(ZERO[:], 0.0))
            link(nc.gpsimd.memset(VG[:], 0.0))
            link(nc.gpsimd.memset(VG[:, :, :, :, VD:VD + 1], 1.0))

            def values(u, g):
                pool.wait_ge(a_free, A_ITEM["va", NCH - 1] + 1)
                nc.gpsimd.tensor_copy(
                    VG[:, u, :, :, 0:VD],
                    VALL[:, bass.ds(g, 1), :, :].rearrange("p o t (h d) -> p (o t) h d", d=VD)).then_inc(v_cp, 1)

            def shift_parts(i, s):
                pool.wait_ge(m_free, i * ITEMS_PER_BODY + (ITEM["max", QPG * s + QPG - 1, 1] + 1))
                u, w = s % 2, R * TB
                nc.gpsimd.tensor_tensor(SHP[:, u, 0:w], NEGMAX[:, u, :], ZERO[:], op=ALU.add).then_inc(sh_split, 1)
                pool.wait_ge(sh_split, i * 8 + (4 * s + 1))
                nc.gpsimd.tensor_tensor(SHR[:], NEGMAX[:, u, :], SHP[:, u, 0:w], op=ALU.subtract).then_inc(sh_split, 1)
                pool.wait_ge(sh_split, i * 8 + (4 * s + 2))
                nc.gpsimd.tensor_tensor(SHP[:, u, w:2 * w], SHR[:], ZERO[:], op=ALU.add).then_inc(sh_split, 1)
                pool.wait_ge(sh_split, i * 8 + (4 * s + 3))
                nc.gpsimd.tensor_tensor(SHP[:, u, 2 * w:3 * w], SHR[:], SHP[:, u, w:2 * w], op=ALU.subtract).then_inc(sh_split, 1)
                pool.wait_ge(sh_split, i * 8 + (4 * s + 4))

            values(0, 0)
            values(1, 1)
            shift_parts(0, 0)
            with pool.Fori(0, LOOPS) as i:
                for s in (1, 2):
                    shift_parts(i, s)
                    pool.wait_ge(av_done, i * BODY + QPG * s)
                    values((s + 1) % 2, i * 2 + (s + 1))
            shift_parts(0, NG - 1)

            pool.wait_ge(xc_ok, 3)
            nc.gpsimd.tensor_tensor(X[:], X[:], BO[:].unsqueeze(1).to_broadcast([P, NT, DIM]), op=ALU.add).then_inc(xb_ok, 1)

        @block.scalar
        def _(act):
            def evac(key, dst, src):
                n = A_ITEM[key]
                act.wait_ge(a_full, n + 1)
                nc.scalar.activation(dst, src(n % 4), ACT.Copy).then_inc(a_free, 1)

            def ln_squares(k):
                act.wait_ge(xc_ok, k + 1)
                nc.scalar.activation(SQ[:], XC[:], ACT.Square).then_inc(sq_ok, 1)

            def ln_root(k):
                act.wait_ge(ve_ok, k + 1)
                nc.scalar.activation(ln_sd[:], ln_v[:], ACT.Sqrt).then_inc(sd_ok, 1)

            def ln_transposed(k):
                for c in range(NCH):
                    evac(("xT", k, c), XT[:, c * BANK:(c + 1) * BANK], lambda n: PS[:, n, :])

            evac("wT", WT[:].rearrange("p j c -> p (j c)"), lambda n: PS[:, n, :])
            n = A_ITEM["centT"]
            act.wait_ge(a_full, n + 1)
            nc.scalar.activation(CT[:], PS[:, n % 4, 0:E], ACT.Copy)
            nc.scalar.activation(WVT[:], PS[:, n % 4, E:E + DIM], ACT.Copy).then_inc(a_free, 1)
            act.wait_ge(lam_in, 1)
            nc.scalar.activation(lam_e[:], lam_s[:], ACT.Exp).then_inc(lam_exp, 1)
            ln_squares(0)
            ln_root(0)
            ln_transposed(0)
            for c in range(NCH):
                for j in range(2):
                    n, cols = D_ITEM["qk", j, c], slice(c * BANK, (c + 1) * BANK)
                    act.wait_ge(d_full, n + 1)
                    nc.scalar.activation(PARTS[:, 0, j, cols], PS[:, 4 + n % 4, :], ACT.Copy).then_inc(qk_hi, 1)
                    act.wait_ge(qk_r1, n + 1)
                    nc.scalar.activation(PARTS[:, 1, j, cols], R1[:, n % 2, :], ACT.Copy).then_inc(qk_mid, 1)
            act.wait_ge(qk_lo, 2 * NCH)
            for c in range(NCH):
                b, h = c // 2, c % 2
                evac(("va", c), VALL[:, b * GPB:(b + 1) * GPB, h * 4:(h + 1) * 4, :].rearrange("p g t v -> p t g v"),
                     lambda n: PS[:, n, :].rearrange("p (t g v) -> p t g v", t=4, g=GPB))
            act.wait_ge(ld_exp, 64)
            for dst, src in ((WUH, RAWU), (WDH, RAWD), (WSUH, RAWSU), (WSDH, RAWSD)):
                nc.scalar.activation(dst[:], src[:], ACT.Copy).then_inc(w_hi, 1)
            for h in range(2):
                act.wait_ge(sel_f, h + 1)
                half = PAIRS // 2 * P
                nc.scalar.activation(SEL[:, h * half:(h + 1) * half], SELF[:].rearrange("p t c -> p (t c)"), ACT.Copy).then_inc(sel_r, 1)
            act.wait_ge(w_lo, 4)
            for b in range(BATCH):
                act.wait_ge(st_w[b], 16 * 2 * (len(Q_SLOTS) + 2))

            def exp_quad(i, s):
                g = i * BODY + s
                if s >= HEAD_Q:
                    act.wait_ge(av_done, g - (PRING - 1))
                for r in range(R):
                    n = R * s + r
                    act.wait_ge(s_full, g * R + (r + 1))
                    nc.scalar.activation(PR[:, s % PRING, r, :], PS[:, 4 + n % 3, :], ACT.Exp, scale=SCALE_A).then_inc(p_ready, 1)
                    if r == 1 and s >= 9 and (s - 9) % TB == 0:
                        evac_out(i, s)

            def evac_out(i, s):
                g, half = (s - 9) // QPG, (s - 9) // TB % 2
                act.wait_ge(av_done, i * BODY + (s - 1))
                before = ITEM["out", g - 1, half] + 1 if g else ITEM["out", g + 1, half] + 1 - ITEMS_PER_BODY
                assert before > 0
                act.wait_ge(m_full, i * ITEMS_PER_BODY + before)
                nc.scalar.activation(OTS[:, half, :], PS[:, 7, :], ACT.Copy).then_inc(o_evac, 1)

            for s in range(HEAD_Q):
                exp_quad(0, s)
            with act.Fori(0, LOOPS) as i:
                for s in range(HEAD_Q, HEAD_Q + BODY):
                    exp_quad(i, s)
            for s in range(NQ - BODY + HEAD_Q, NQ):
                exp_quad(0, s)
            evac_out(0, NQ + 1)

            act.wait_ge(o_done, 2 * NG + 1)
            nc.scalar.activation(SQ[:].rearrange("p t c -> p (t c)"), O.rearrange("p g t v -> p (g t v)"), ACT.Square).then_inc(rms_sq, 1)
            act.wait_ge(rms_ve, 1)
            nc.scalar.activation(rms_sd[:], rms_s[:], ACT.Sqrt).then_inc(rms_sq2, 1)
            for c in range(NCH):
                evac(("oT", c), XT[:, c * BANK:(c + 1) * BANK], lambda n: PS[:, n, :])

            def experts(k):
                ln_squares(2 * k + 1)
                ln_root(2 * k + 1)
                ln_transposed(2 * k + 1)
                act.wait_ge(a_free, A_ITEM["xT", 2 * k + 1, NCH - 1] + 1)
                nc.scalar.activation(XH[:], XT[:], ACT.Copy).then_inc(xh_ok, 1)
                act.wait_ge(aff_ok, 2 * (k + 1))
                nc.scalar.activation(EX[:], AFF[:], ACT.Exp, scale=-1.0).then_inc(ex_ok, 1)
                for c in range(NCH):
                    evac(("cwT", k, c), CWT[:, c * BANK:(c + 1) * BANK], lambda n: PS[:, n, :])

                def high(base, hbase, j):
                    if j >= 3:
                        act.wait_ge(down_ok, base + (j - 2))
                    if j < PAIRS:
                        act.wait_ge(hf_ok, hbase + (j + 1))
                    else:
                        act.wait_ge(silu_ok, base + (j + 1))
                    nc.scalar.activation(HH[:, j % 3, :], HF[:, j % 3, :], ACT.Copy).then_inc(hh_ok, 1)

                with act.Fori(0, NCH) as c:
                    base, hbase = c * UNITS + k * NCH * UNITS, c * PAIRS + k * NCH * PAIRS
                    for j in range(UNITS):
                        dst = SI if j < PAIRS else HF
                        act.wait_ge(z_full, base + (j + 1))
                        if j >= 3 and j < PAIRS:
                            act.wait_ge(hf_ok, hbase + (j - 2))
                        if j == PAIRS:
                            act.wait_ge(hl_ok, base + (j - 2))
                            act.wait_ge(hh_ok, base + (j - 2))
                        nc.scalar.activation(dst[:, j % 3, :], PS[:, j % 3, :], ACT.Silu).then_inc(silu_ok, 1)
                        if j:
                            high(base, hbase, j - 1)
                    high(base, hbase, UNITS - 1)
                    act.wait_ge(down_ok, base + UNITS)
                    nc.scalar.activation(YS[:], PS[:, 5, :], ACT.Copy).then_inc(y_evac, 1)

            experts(0)

            ln_squares(2)
            ln_root(2)
            ln_transposed(2)
            act.wait_ge(b_dve, 4)
            nc.scalar.activation(EN[:], EN[:], ACT.Exp, scale=SCALE_B).then_inc(b_exp, 1)
            for c in range(NCH):
                evac(("vp", c), VP[:, c // 2, :, (c % 2) * (S1 // 2):(c % 2 + 1) * (S1 // 2)],
                     lambda n: PS[:, n, :].rearrange("p (j i) -> p i j", i=S0))
            experts(1)

        @block.vector
        def _(dve):
            nsteps = [0]

            def link(ins):
                nsteps[0] += 1
                ins.then_inc(dve_step, 1)
                dve.wait_ge(dve_step, nsteps[0])

            def newton(r, t, v):
                link(nc.vector.tensor_tensor(t, r, r, op=ALU.mult))
                link(nc.vector.tensor_tensor(t, t, v, op=ALU.mult))
                link(nc.vector.tensor_scalar(t, t, -0.5, 1.5, ALU.mult, ALU.add))
                link(nc.vector.tensor_tensor(r, r, t, op=ALU.mult))

            def layernorm(k):
                link(nc.vector.tensor_reduce(ln_s[:], X[:], axis=AX_X, op=ALU.add))
                link(nc.vector.tensor_scalar(ln_m[:], ln_s[:], 1.0 / DIM, None, ALU.mult))
                nc.vector.tensor_tensor(XC[:], X[:], ln_m[:].unsqueeze(2).to_broadcast([P, NT, DIM]), op=ALU.subtract).then_inc(xc_ok, 1)
                dve.wait_ge(sq_ok, k + 1)
                link(nc.vector.tensor_reduce(ln_s[:], SQ[:], axis=AX_X, op=ALU.add))
                nc.vector.tensor_scalar(ln_v[:], ln_s[:], 1.0 / DIM, LN_EPS, ALU.mult, ALU.add).then_inc(ve_ok, 1)
                dve.wait_ge(sd_ok, k + 1)
                link(nc.vector.reciprocal(ln_r[:], ln_sd[:]))
                newton(ln_r[:], ln_t[:], ln_v[:])
                for c in range(NCH):
                    t = XC[:, 4 * c:4 * c + 4, :]
                    nc.vector.tensor_tensor(t, t, ln_r[:, 4 * c:4 * c + 4].unsqueeze(2).to_broadcast([P, 4, DIM]), op=ALU.mult).then_inc(xn_ok, 1)

            dve.wait_ge(ident_ok, 1)
            link(nc.vector.tensor_reduce(T8[:], ident[:].rearrange("p (a d) -> p d a", d=HD_B), axis=AX_X, op=ALU.add))
            link(nc.vector.tensor_reduce(H16[:], ident[:].rearrange("p (a d) -> p a d", d=HD_B), axis=AX_X, op=ALU.add))
            nc.vector.tensor_copy(BLK[:].rearrange("p (a d) -> p a d", d=HD_B),
                                  H16[:].unsqueeze(2).to_broadcast([P, HEADS_B, HD_B])).then_inc(blk_ok, 1)
            dve.wait_ge(ld_mix, 16 * 8)
            for j in range(2):
                link(nc.vector.tensor_tensor(lam_p[:, j, :], LAM[:, 2 * j, :], LAM[:, 2 * j + 1, :], op=ALU.mult))
            nc.vector.tensor_reduce(lam_s[:], lam_p[:], axis=AX_X, op=ALU.add).then_inc(lam_in, 1)
            dve.wait_ge(ld_x, 16)
            layernorm(0)
            dve.wait_ge(lam_exp, 1)
            link(nc.vector.tensor_tensor(neg_lam[:], lam_e[:, 1:2], lam_e[:, 0:1], op=ALU.subtract))
            link(nc.vector.tensor_scalar(neg_lam[:], neg_lam[:], -LAMBDA_INIT, None, ALU.add))
            for c in range(NCH):
                for j in range(2):
                    n, cols = D_ITEM["qk", j, c], slice(c * BANK, (c + 1) * BANK)
                    dve.wait_ge(qk_hi, n + 1)
                    nc.vector.tensor_tensor(R1[:, n % 2, :], PS[:, 4 + n % 4, :], PARTS[:, 0, j, cols], op=ALU.subtract).then_inc(qk_r1, 1)
                    dve.wait_ge(qk_r1, n + 1)
                    dve.wait_ge(qk_mid, n + 1)
                    nc.vector.tensor_tensor(PARTS[:, 2, j, cols], R1[:, n % 2, :], PARTS[:, 1, j, cols], op=ALU.subtract).then_inc(qk_lo, 1)
                    dve.wait_ge(qk_lo, n + 1)
            for n, (dst, src, hi) in enumerate(((WUL, RAWU, WUH), (WDL, RAWD, WDH), (WSUL, RAWSU, WSUH), (WSDL, RAWSD, WSDH))):
                dve.wait_ge(w_hi, n + 1)
                nc.vector.tensor_tensor(dst[:], src[:], hi[:].bitcast(F32), op=ALU.subtract).then_inc(w_lo, 1)
            nc.vector.memset(TM[:], 0.0).then_inc(o_done, 1)
            def slot(it):
                return 2 * (it % 2)

            def max_quad(i, s):
                at = i * ITEMS_PER_BODY
                for key in quad_items(s):
                    it = ITEM[key]
                    e = slot(it)
                    dve.wait_ge(m_full, at + (it + 1))
                    if key[0] == "max":
                        ga, a = key[1] // QPG, 2 * (key[1] % QPG) + key[2]
                        if a == 0 and (ga >= 2):
                            dve.wait_ge(sh_split, i * 8 + 4 * (ga - 1))
                        nc.vector.tensor_reduce(NEGMAX[:, ga % 2, a:a + 1], PS[:, e:e + 2, :].rearrange("p b n -> p (b n)"),
                                                axis=AX_X, op=ALU.max, negate=True).then_inc(m_free, 1)
                    elif key[0] == "shift":
                        ga = key[1]
                        if ga >= 2:
                            dve.wait_ge(sh_w, i * 64 + 32 * (ga - 1))
                        nc.vector.tensor_copy(SHT[:, ga % 2, :], PS[0:3 * R * TB, e, 0:P // 2].bitcast(BF16)).then_inc(m_free, 1)
                    else:
                        gg, half = key[1], key[2]
                        n = 2 * gg + half
                        rows = PS[:, e, :].rearrange("p (m v) -> p m v", v=STRIP)
                        dve.wait_ge(o_done, i * 4 + (n + 1))
                        ob = i * 8 + 2 * n
                        nc.vector.reciprocal(RD[:], rows[:, :, VD]).then_inc(rd_ok, 1)
                        dve.wait_ge(rd_ok, ob + 1)
                        second = RD[:].rearrange("p (m s) -> p m s", s=2)[:, :, 1]
                        nc.vector.tensor_scalar(second, second, neg_lam[:], None, ALU.mult).then_inc(rd_ok, 1)
                        dve.wait_ge(rd_ok, ob + 2)
                        nc.vector.tensor_tensor(TM[:], rows[:, :, 0:VD], RD[:].unsqueeze(2).to_broadcast([P, 4 * R, VD]),
                                                op=ALU.mult).then_inc(m_free, 1)
                        dve.wait_ge(m_free, at + (it + 1))
                        tm = TM[:].rearrange("p (t h s) v -> p t h s v", h=2, s=2)
                        dst = O[:, bass.ds(i * 2 + gg, 1), 4 * half:4 * half + 4, :]
                        nc.vector.tensor_tensor(dst.rearrange("p o t (h v) -> p (o t) h v", v=VD),
                                                tm[:, :, :, 0, :], tm[:, :, :, 1, :], op=ALU.add).then_inc(o_done, 1)

            for s in range(-LEAD, HEAD_Q):
                max_quad(0, s)
            with dve.Fori(0, LOOPS) as i:
                for s in range(HEAD_Q, HEAD_Q + BODY):
                    max_quad(i, s)
            for s in range(NQ - BODY + HEAD_Q, NQ + 4):
                max_quad(0, s)

            dve.wait_ge(rms_sq, 1)
            flat = SQ[:].rearrange("p t c -> p (t c)").rearrange("p (m v) -> p m v", v=VD)
            link(nc.vector.tensor_reduce(rms_s[:], flat, axis=AX_X, op=ALU.add))
            nc.vector.tensor_scalar(rms_s[:], rms_s[:], 1.0 / VD, EPS_A, ALU.mult, ALU.add).then_inc(rms_ve, 1)
            dve.wait_ge(rms_sq2, 1)
            link(nc.vector.reciprocal(rms_r[:], rms_sd[:]))
            newton(rms_r[:], rms_t[:], rms_s[:])
            link(nc.vector.tensor_scalar(rms_r[:], rms_r[:], 1.0 - LAMBDA_INIT, None, ALU.mult))
            heads = O.rearrange("p g t (h v) -> p (g t h) v", v=VD)
            link(nc.vector.tensor_tensor(heads, heads, rms_r[:].unsqueeze(2).to_broadcast([P, NG * TB * 2, VD]), op=ALU.mult))
            link(nc.vector.tensor_tensor(heads, heads, SUBW[:].unsqueeze(1).to_broadcast([P, NG * TB * 2, VD]), op=ALU.mult))
            for b in range(BATCH):
                nc.vector.tensor_copy(
                    XC[:, b * TB:(b + 1) * TB, :].rearrange("p t (g v) -> p t g v", v=2 * VD),
                    O[:, b * GPB:(b + 1) * GPB, :, :].rearrange("p g t v -> p t g v")).then_inc(rms_on, 1)
            dve.wait_ge(xb_ok, 1)
            for c in range(NCH):
                n, t = D_ITEM["proj", c], X[:, 4 * c:4 * c + 4, :].rearrange("p t c -> p (t c)")
                dve.wait_ge(d_full, n + 1)
                nc.vector.tensor_tensor(t, t, PS[:, 4 + n % 4, :], op=ALU.add).then_inc(d_free, 1)
            dve.wait_ge(d_free, NCH)

            def experts(k):
                layernorm(2 * k + 1)
                for h in range(2):
                    n, half = D_ITEM["aff", k, h], slice(8 * h, 8 * h + 8)
                    dve.wait_ge(d_full, n + 1)
                    src = PS[:, 4 + n % 4, :].rearrange("p (t e) -> p t e", e=E)
                    nc.vector.tensor_copy(AFF[:, half, :], src).then_inc(aff_ok, 1)
                    nc.vector.tensor_tensor(BI[:, half, :], src, EBIAS[:].unsqueeze(1).to_broadcast([P, 8, E]), op=ALU.add).then_inc(d_free, 1)
                dve.wait_ge(d_free, D_ITEM["aff", k, 1] - 2 * NCH + 1)
                for t in range(NT):
                    last = nc.vector.max(top8[:, t, :], BI[:, t, :])
                link(last)
                for t in range(NT):
                    last = nc.vector.match_replace(BR[:, t, :], top8[:, t, :], BI[:, t, :], -3.0e38)
                link(last)
                link(nc.vector.tensor_tensor(BR[:], BR[:], BI[:], op=ALU.not_equal))
                dve.wait_ge(ex_ok, k + 1)
                link(nc.vector.tensor_scalar(EX[:], EX[:], 1.0, None, ALU.add))
                link(nc.vector.reciprocal(EX[:], EX[:]))
                link(nc.vector.tensor_tensor(EX[:], EX[:], BR[:], op=ALU.mult))
                link(nc.vector.tensor_reduce(wsum[:], EX[:], axis=AX_X, op=ALU.add))
                link(nc.vector.tensor_scalar(wsum[:], wsum[:], 1e-8, None, ALU.add))
                link(nc.vector.reciprocal(wrec[:], wsum[:]))
                link(nc.vector.tensor_tensor(EX[:], EX[:], wrec[:].unsqueeze(2).to_broadcast([P, NT, E]), op=ALU.mult))
                link(nc.vector.tensor_copy(CWH[:], EX[:]))
                link(nc.vector.tensor_copy(CH[:, :, 0:E], CWH[:].bitcast(F32)))
                link(nc.vector.tensor_tensor(CWL[:], EX[:], CWH[:].bitcast(F32), op=ALU.subtract))
                nc.vector.tensor_copy(CH[:, :, E:2 * E], CWL[:].bitcast(F32)).then_inc(ch_ok, 1)
                dve.wait_ge(xh_ok, k + 1)
                nc.vector.tensor_tensor(XL[:], XT[:], XH[:].bitcast(F32), op=ALU.subtract).then_inc(xl_ok, 1)

                def low(base, hbase, j):
                    if j >= 3:
                        dve.wait_ge(down_ok, base + (j - 2))
                    dve.wait_ge(hh_ok, base + (j + 1))
                    nc.vector.tensor_tensor(HL[:, j % 3, :], HF[:, j % 3, :], HH[:, j % 3, :].bitcast(F32),
                                            op=ALU.subtract).then_inc(hl_ok, 1)

                with dve.Fori(0, NCH) as c:
                    base, hbase = c * UNITS + k * NCH * UNITS, c * PAIRS + k * NCH * PAIRS
                    for j in range(PAIRS):
                        dve.wait_ge(silu_ok, base + (j + 1))
                        dve.wait_ge(c_full, hbase + (j + 1))
                        if j >= 3:
                            dve.wait_ge(hh_ok, base + (j - 2))
                            dve.wait_ge(hl_ok, base + (j - 2))
                        nc.vector.tensor_tensor(HF[:, j % 3, :], SI[:, j % 3, :], PS[:, 3 + j % 2, :], op=ALU.mult).then_inc(hf_ok, 1)
                        if j:
                            dve.wait_ge(hf_ok, hbase + j)
                            low(base, hbase, j - 1)
                    dve.wait_ge(hf_ok, hbase + PAIRS)
                    low(base, hbase, PAIRS - 1)
                    low(base, hbase, UNITS - 1)
                    dve.wait_ge(t_full, c + (k * NCH + 1))
                    dst = X[:, bass.ds(c * 4, 4), :].rearrange("p t c -> p (t c)")
                    nc.vector.tensor_tensor(dst, dst, PS[:, 6, :], op=ALU.add).then_inc(t_done, 1)
                dve.wait_ge(t_done, NCH * (k + 1))

            experts(0)

            layernorm(2)
            dve.wait_ge(xb_ok, 2)
            def step(n, ins):
                ins.then_inc(b_dve, 1)
                dve.wait_ge(b_dve, n)

            pair = [P, BATCH * HEADS_B, HD_B]
            flat = "p b c -> p (b c)"
            two = slice(0, BATCH * DIM)
            dve.wait_ge(b_pe, 1)
            step(1, nc.vector.tensor_copy(GRAM[:].rearrange(flat), PS[:, 4, two]))
            dve.wait_ge(b_pe, 2)
            step(2, nc.vector.tensor_copy(GK[:].rearrange(flat), PS[:, 5, two]))
            dve.wait_ge(b_pe, 3)
            link(nc.vector.tensor_tensor(QK[:].rearrange(flat).rearrange("p (m d) -> p m d", d=HD_B),
                                         PS[:, 6, two].rearrange("p (m d) -> p m d", d=HD_B),
                                         T8[:].unsqueeze(1).to_broadcast(pair), op=ALU.mult))
            step(3, nc.vector.tensor_reduce(QKR[:], QK[:].rearrange(flat).rearrange("p (m d) -> p m d", d=HD_B), axis=AX_X, op=ALU.add))
            dve.wait_ge(b_pe, 4)
            energies = PS[:, 7, 0:BATCH * HEADS_B].rearrange("p (b h) -> p b h", b=BATCH)
            wide = [P, BATCH, HEADS_B]
            link(nc.vector.tensor_reduce(en_m[:], energies, axis=AX_X, op=ALU.max))
            step(4, nc.vector.tensor_tensor(EN[:], energies, en_m[:].unsqueeze(2).to_broadcast(wide), op=ALU.subtract))
            dve.wait_ge(b_exp, 1)
            link(nc.vector.tensor_reduce(en_s[:], EN[:], axis=AX_X, op=ALU.add))
            link(nc.vector.reciprocal(en_r[:], en_s[:]))
            link(nc.vector.tensor_tensor(EN[:], EN[:], en_r[:].unsqueeze(2).to_broadcast(wide), op=ALU.mult))
            step(5, nc.vector.tensor_tensor(MIXT[:].rearrange(flat).rearrange("p (m d) -> p m d", d=HD_B),
                                            EN[:].rearrange("p b h -> p (b h)").unsqueeze(2).to_broadcast(pair),
                                            T8[:].unsqueeze(1).to_broadcast(pair), op=ALU.mult))
            dve.wait_ge(b_pe, 5)
            step(6, nc.vector.tensor_copy(MIX[:].rearrange(flat), PS[:, 4, two]))
            dve.wait_ge(b_pe, 6)
            step(7, nc.vector.tensor_copy(VMIX[:].rearrange(flat), PS[:, 5, two]))
            for c in range(NCH):
                n, t = D_ITEM["out_b", c], X[:, 4 * c:4 * c + 4, :].rearrange("p t c -> p (t c)")
                dve.wait_ge(d_full, n + 1)
                nc.vector.tensor_tensor(t, t, PS[:, 4 + n % 4, :], op=ALU.add).then_inc(d_free, 1)
            dve.wait_ge(d_free, D_ITEM["out_b", NCH - 1] - 2 * NCH + 1)
            experts(1)

        @block.tensor
        def _(pe):
            mm = nc.tensor.matmul

            def ring(key, items, full, free, put):
                n = items[key]
                if n >= 4:
                    pe.wait_ge(free, n - 3)
                put((0 if items is A_ITEM else 4) + n % 4).then_inc(full, 1)

            def transposes(tiles):
                def put(n):
                    for j, t in enumerate(tiles):
                        last = nc.tensor.transpose(PS[:, n, j * P:j * P + t.shape[0]], t, ident[0:t.shape[0], 0:t.shape[0]])
                    return last
                return put

            def ln_transposed(k):
                for c in range(NCH):
                    pe.wait_ge(xn_ok, NCH * k + c + 1)
                    ring(("xT", k, c), A_ITEM, a_full, a_free, transposes([XC[:, 4 * c + j, :] for j in range(4)]))

            pe.wait_ge(ident_ok, 1)
            pe.wait_ge(ld_w, 48)
            ring("wT", A_ITEM, a_full, a_free, transposes([WQKV[:, j, :] for j in range(3)] + [WPRJ[:]]))
            pe.wait_ge(ld_b, 64)

            def centroids(n):
                nc.tensor.transpose(PS[:, n, 0:E], CENT[:], ident[0:E, 0:E])
                return nc.tensor.transpose(PS[:, n, E:E + DIM], WB[:, 2, :], ident[:])

            ring("centT", A_ITEM, a_full, a_free, centroids)
            ln_transposed(0)

            def chunk(w, c):
                return lambda n: mm(PS[:, n, :], w, XT[:, c * BANK:(c + 1) * BANK], start=True, stop=True)

            def tokens(src, w, c):
                def put(n):
                    for j in range(4):
                        t = 4 * c + j
                        last = mm(PS[:, n, j * P:(j + 1) * P], src[:, t * P:(t + 1) * P], w, start=True, stop=True)
                    return last
                return put

            for c in range(NCH):
                pe.wait_ge(a_free, A_ITEM["xT", 0, c] + 1)
                for j in range(2):
                    ring(("qk", j, c), D_ITEM, d_full, qk_r1, chunk(WT[:, j, :], c))
            for c in range(NCH):
                ring(("va", c), A_ITEM, a_full, a_free, tokens(XT, WT[:, 2, :], c))
            pe.wait_ge(qk_r1, 2 * NCH)
            pe.wait_ge(a_free, A_ITEM["va", NCH - 1] + 1)
            pe.wait_ge(identb_ok, 1)

            def m_items(i, which):
                at = i * ITEMS_PER_BODY
                for key in which:
                    it = ITEM[key]
                    e = 2 * (it % 2)
                    if it >= 2:
                        pe.wait_ge(m_free, at + (it - 1))
                    if key[0] == "max":
                        ga, a = key[1] // QPG, 2 * (key[1] % QPG) + key[2]
                        r, nt, u = a // TB, a % TB, ga % 2
                        if a == 0:
                            pe.wait_ge(qa_ld[u], i * (16 * (R + 1)) + 16 * (R + 1) * (ga // 2 + 1))
                        for h in range(2):
                            last = mm(PS[:, e + h, :], QA[:, u, r, nt * P:(nt + 1) * P], KA[:, u, h * BANK:(h + 1) * BANK],
                                      start=True, stop=True)
                    elif key[0] == "shift":
                        ga = key[1]
                        pe.wait_ge(sh_split, i * 8 + 4 * (ga + 1))
                        last = nc.tensor.transpose(PS[0:3 * R * TB, e, 0:P // 2].bitcast(BF16), SHP[:, ga % 2, :], identb[:])
                    else:
                        gg, half = key[1], key[2]
                        pe.wait_ge(o_evac, i * 4 + 2 * gg + half + 1)
                        for j in range(4):
                            last = nc.tensor.transpose(PS[:, e, j * P:(j + 1) * P], OTS[:, half, j * P:(j + 1) * P], ident[:])
                    last.then_inc(m_full, 1)

            def scores(i, s, r):
                g, n, q = i * BODY + s, R * s + r, s % QPG
                half, mt, u = q // TB, q % TB, s // QPG % 2
                if q == 0 and r == 0:
                    grp = s // QPG
                    pe.wait_ge(kb_ld[u], i * (16 * R) + 16 * R * (grp // 2 + 1))
                    pe.wait_ge(sh_r, i * 128 + 64 * (grp + 1))
                if n >= 3:
                    pe.wait_ge(p_ready, g * R + (r - 1 if n in (R * HEAD_Q, R * HEAD_Q + 1) else r - 2))
                mm(PS[:, 4 + n % 3, :], KB[:, u, r, mt * P:(mt + 1) * P], QB[:, u, half * BANK:(half + 1) * BANK],
                   start=True, stop=True).then_inc(s_full, 1)

            def weighted_values(i, s):
                g, q = i * BODY + s, s % QPG
                mt, u = q % TB, s // QPG % 2
                pe.wait_ge(p_ready, g * R + R)
                if q == 0:
                    pe.wait_ge(v_cp, i * 2 + s // QPG + 1)
                if mt == 0 and s:
                    pe.wait_ge(o_evac, i * 4 + s // TB)
                for r in range(R):
                    last = mm(PS[STRIP * r:STRIP * (r + 1), 7, :], VG[:, u, mt, r // 2, :], PR[:, s % PRING, r, :],
                              start=mt == 0, stop=mt == TB - 1)
                last.then_inc(av_done, 1)

            def quad(i, s, with_scores=True):
                items = quad_items(s)
                cut = (len(items) + 1) // 2
                if with_scores:
                    scores(i, s, 0)
                    scores(i, s, 1)
                m_items(i, items[:cut])
                if with_scores:
                    scores(i, s, 2)
                    scores(i, s, 3)
                m_items(i, items[cut:])

            for s in range(-LEAD, 0):
                quad(0, s, False)
            for s in range(HEAD_Q):
                quad(0, s)
                if s:
                    weighted_values(0, s - 1)
            with pe.Fori(0, LOOPS) as i:
                for s in range(HEAD_Q, HEAD_Q + BODY):
                    quad(i, s)
                    weighted_values(i, s - 1)
            for s in range(NQ - BODY + HEAD_Q, NQ):
                quad(0, s)
                weighted_values(0, s - 1)
            weighted_values(0, NQ - 1)
            for s in range(NQ, NQ + 4):
                quad(0, s, False)

            for c in range(NCH):
                pe.wait_ge(rms_on, c // 2 + 1)
                ring(("oT", c), A_ITEM, a_full, a_free, transposes([XC[:, 4 * c + j, :] for j in range(4)]))
            for c in range(NCH):
                pe.wait_ge(a_free, A_ITEM["oT", c] + 1)
                tokens(XT, WT[:, 3, :], c)(4 + D_ITEM["proj", c] % 4).then_inc(d_full, 1)

            def split3(dst, ah, al, bh, bl, first, last):
                mm(dst, ah, bh, start=first, stop=False)
                mm(dst, ah, bl, start=False, stop=False)
                return mm(dst, al, bh, start=False, stop=last)

            def experts(k):
                ln_transposed(2 * k + 1)
                for h in range(2):
                    pe.wait_ge(a_free, A_ITEM["xT", 2 * k + 1, 2 * h + 1] + 1)
                    n = D_ITEM["aff", k, h]
                    if h == 0:
                        pe.wait_ge(d_free, n - 2 * NCH)
                    for j in range(8):
                        t = 8 * h + j
                        last = mm(PS[:, 4 + n % 4, j * E:(j + 1) * E], XT[:, t * P:(t + 1) * P], CT[:], start=True, stop=True)
                    last.then_inc(d_full, 1)
                for c in range(NCH):
                    pe.wait_ge(ch_ok, k + 1)
                    ring(("cwT", k, c), A_ITEM, a_full, a_free, transposes([CH[:, 4 * c + j, :] for j in range(4)]))
                pe.wait_ge(a_free, A_ITEM["cwT", k, NCH - 1] + 1)
                pe.wait_ge(xh_ok, k + 1)
                pe.wait_ge(xl_ok, k + 1)
                pe.wait_ge(d_free, D_ITEM["aff", k, 1] - 2 * NCH + 1)

                with pe.Fori(0, NCH) as c:
                    base, hbase = c * UNITS + k * NCH * UNITS, c * PAIRS + k * NCH * PAIRS
                    cols = bass.ds(c * BANK, BANK)
                    for j in range(UNITS + LAG):
                        if j < UNITS:
                            wh, wl = (WUH[:, j * P:(j + 1) * P], WUL[:, j * P:(j + 1) * P]) if j < PAIRS else (WSUH[:], WSUL[:])
                            if j >= 3:
                                pe.wait_ge(silu_ok, base + (j - 2))
                            split3(PS[:, j % 3, :], wh, wl, XH[:, cols], XL[:, cols], True, True).then_inc(z_full, 1)
                        if j < PAIRS:
                            if j >= 2:
                                pe.wait_ge(hf_ok, hbase + (j - 1))
                            mm(PS[:, 3 + j % 2, :], SEL[:, j * P:(j + 1) * P], CWT[:, cols], start=True, stop=True).then_inc(c_full, 1)
                        if j >= LAG:
                            d = j - LAG
                            wh, wl = (WDH[:, d * DIM:(d + 1) * DIM], WDL[:, d * DIM:(d + 1) * DIM]) if d < PAIRS else (WSDH[:], WSDL[:])
                            pe.wait_ge(hh_ok, base + (d + 1))
                            pe.wait_ge(hl_ok, base + (d + 1))
                            split3(PS[:, 5, :], wh, wl, HH[:, d % 3, :], HL[:, d % 3, :], d == 0,
                                   d == UNITS - 1).then_inc(down_ok, 1)
                    pe.wait_ge(y_evac, c + (k * NCH + 1))
                    for j in range(4):
                        last = nc.tensor.transpose(PS[:, 6, j * P:(j + 1) * P], YS[:, j * P:(j + 1) * P], ident[:])
                    last.then_inc(t_full, 1)

            experts(0)

            two = slice(0, BATCH * DIM)
            ln_transposed(2)
            for b in range(BATCH):
                for j in range(TB):
                    t = XC[:, b * TB + j, :]
                    last = mm(PS[:, 4, b * DIM:(b + 1) * DIM], t, t, start=j == 0, stop=j == TB - 1)
            last.then_inc(b_pe, 1)
            pe.wait_ge(b_dve, 1)
            for b in range(BATCH):
                last = mm(PS[:, 5, b * DIM:(b + 1) * DIM], GRAM[:, b, :], WB[:, 1, :], start=True, stop=True)
            last.then_inc(b_pe, 1)
            pe.wait_ge(b_dve, 2)
            mm(PS[:, 6, two], WB[:, 0, :], GK[:].rearrange("p b c -> p (b c)"), start=True, stop=True).then_inc(b_pe, 1)
            pe.wait_ge(b_dve, 3)
            pe.wait_ge(blk_ok, 1)
            mm(PS[:, 7, 0:BATCH * HEADS_B], BLK[:], QKR[:], start=True, stop=True).then_inc(b_pe, 1)
            pe.wait_ge(b_dve, 5)
            for b in range(BATCH):
                last = nc.tensor.transpose(PS[:, 4, b * DIM:(b + 1) * DIM], MIXT[:, b, :], ident[:])
            last.then_inc(b_pe, 1)
            pe.wait_ge(b_dve, 6)
            mm(PS[:, 5, two], WVT[:], MIX[:].rearrange("p b c -> p (b c)"), start=True, stop=True).then_inc(b_pe, 1)
            pe.wait_ge(b_dve, 7)
            for c in range(NCH):
                ring(("vp", c), A_ITEM, a_full, a_free, chunk(VMIX[:, c // 2, :], c))
            for c in range(NCH):
                if c % 2 == 0:
                    pe.wait_ge(mix_r[c // 2], 16 * S0)
                tokens(RT[:].rearrange("p b n -> p (b n)"), WB[:, 3, :], c)(4 + D_ITEM["out_b", c] % 4).then_inc(d_full, 1)
            experts(1)


_INS = ["L0_attn_a_x", "L0_attn_a_w_qkv", "L0_attn_a_w_proj", "L0_attn_a_b_proj", "L0_attn_a_lambda_q1",
        "L0_attn_a_lambda_k1", "L0_attn_a_lambda_q2", "L0_attn_a_lambda_k2", "L0_attn_a_sub_norm_w",
        "L0_attn_b_Wq", "L0_attn_b_Wk", "L0_attn_b_Wv", "L0_attn_b_Wo", "L0_attn_b_bo", "L0_ffn_centroids",
        "L0_ffn_expert_biases", "L0_ffn_Ws_up", "L0_ffn_Ws_down", "L0_ffn_W_up", "L0_ffn_W_down"]
_OUTS = [((BATCH, SEQ, DIM), "float32")]


def kernel(**inputs):
    import numpy as _np
    import concourse.bacc as _bacc
    from concourse import mybir as _mybir
    from concourse.bass_utils import run_bass_kernel_spmd as _run

    nc = _bacc.Bacc("TRN2", target_bir_lowering=False, num_devices=1)
    arrays, args = {}, []
    for name in _INS:
        a = _np.ascontiguousarray(inputs[name])
        arrays[f"in_{name}_dram"] = a
        args.append(nc.dram_tensor(f"in_{name}_dram", a.shape, _mybir.dt.from_np(a.dtype), kind="ExternalInput").ap())
    for i, (shape, dtype) in enumerate(_OUTS):
        dt = _mybir.dt.from_np(_np.dtype(dtype))
        args.append(nc.dram_tensor(f"out_{i}_dram", shape, dt, kind="ExternalOutput").ap())
    hybrid_layer(nc, *args)
    r = _run(nc, [arrays], core_ids=[0])
    return r.results[0]["out_0_dram"]
```

```python
from contextlib import ExitStack

import numpy as np

import concourse.bass as bass
from concourse import mybir

F32 = mybir.dt.float32
F32R = mybir.dt.float32r
BF16 = mybir.dt.bfloat16
ALU = mybir.AluOpType
ACT = mybir.ActivationFunctionType
AX_X = mybir.AxisListType.X

P = 128
BATCH, SEQ, DIM = 2, 1024, 128
NT = BATCH * SEQ // P
TB = SEQ // P
TOK = BATCH * SEQ
BANK = 512
NCH = TOK // BANK
LN_EPS = 1e-5

HEADS_A = 16
HD_A = DIM // HEADS_A // 2
SUBS = 2 * HEADS_A
R = 4
GPB = SUBS // R
NG = BATCH * GPB
VD = 2 * HD_A
SCALE_A = HD_A ** -0.5
LAMBDA_INIT = 0.8 - 0.6 * float(np.exp(-0.3 * 0))
EPS_A = 1e-5
Q_SLOTS = (0, 0, 0, 1, 1, 2)
K_SLOTS = (0, 1, 2, 0, 1, 0)
SHIFT_ROW = HD_A * len(Q_SLOTS)
STRIP = 32

QPG = 2 * TB
NQ = NG * QPG
LEAD = 20
BODY = 2 * QPG
HEAD_Q = 4
LOOPS = (NQ - BODY) // BODY
PRING = 4

HEADS_B = 16
HD_B = DIM // HEADS_B
SCALE_B = float(1.0 / np.sqrt(HD_B))
S0 = HEADS_B
S1 = SEQ // S0

E, F, TOPK = 64, 64, 8
PAIRS = E // 2
UNITS = PAIRS + 1
LAG = 3


def max_pass_items():
    index = {}
    for g in range(-LEAD, NQ + 4):
        for key in quad_items(g):
            index[key] = len(index)
    return index


def quad_items(g):
    items = []
    if 0 <= g + LEAD < NQ:
        items.append(("max", g + LEAD, 0))
    if (g + 3) % QPG == 0 and 0 <= (g + 3) // QPG < NG:
        items.append(("shift", (g + 3) // QPG))
    if g >= 10 and (g - 10) % TB == 0 and (g - 10) // TB < 2 * NG:
        items.append(("out", (g - 10) // TB // 2, (g - 10) // TB % 2))
    if 0 <= g + LEAD < NQ:
        items.append(("max", g + LEAD, 1))
    return items


ITEM = max_pass_items()
ITEMS_PER_BODY = 2 * BODY + 2 + 4


def ring_order(names):
    return {n: i for i, n in enumerate(names)}


A_ITEM = ring_order(["wT", "centT"] + [("xT", c) for c in range(NCH)] + [("va", c) for c in range(NCH)])
D_ITEM = ring_order([("qk", j, c) for c in range(NCH) for j in range(2)])

SIDE = {
    NQ - 19: [("rms_squares", 0)], NQ - 18: [("rms_sums", 0), ("rms_root", 0), ("rms_scale", 0)],
    NQ - 14: [("heads_T", 0)], NQ - 13: [("proj", 0), ("stats", ("f", 0))],
    NQ - 12: [("root", ("f", 0)), ("norm", ("f", 0))], NQ - 10: [("x_T", ("f", 0))],
    NQ - 8: [("affinity", 0), ("top", 0)], NQ - 6: [("gate", 0)], NQ - 3: [("gate_T", 0)],
    (0, 2): [("rms_squares", 1)], (0, 3): [("heads_T", 1), ("rms_sums", 1)], (0, 4): [("rms_root", 1)],
    (0, 5): [("proj", 1), ("stats", ("f", 1))], (0, 6): [("root", ("f", 1)), ("rms_scale", 1)],
    (0, 8): [("norm", ("f", 1))], (0, 11): [("x_T", ("f", 1))], (0, 14): [("affinity", 1)], (0, 15): [("top", 1)],
    (0, 18): [("gate", 1)], (0, 23): [("gate_T", 1)],
}
for n in (1, 2, 4):
    c = n - 1
    SIDE.update({
        (n, 1): [("heads_T", n + 1)] if n < NCH else [],
        (n, 3): [("proj", n + 1)] if n < NCH else [],
        (n, 4): [("stats", ("f", n + 1))],
        (n, 6): [("y_T", n - 1)],
        (n, 8): [("stats", ("b", c))],
        (n, 9): [("root", ("f", n + 1)), ("root", ("b", c))],
        (n, 10): [("norm", ("f", n + 1))], (n, 11): [("norm", ("b", c))],
        (n, 13): [("x_T", ("f", n + 1))], (n, 15): [("x_T", ("b", c))],
        (n, 17): [("affinity", n + 1)], (n, 18): [("top", n + 1)], (n, 20): [("gate", n + 1)],
        (n, 25): [("gate_T", n + 1)],
    })
for n, b in ((2, 0), (4, 1)):
    SIDE.update({
        (n, 19): [("gram", b)], (n, 21): [("gram_k", b)], (n, 23): [("q_k", b)], (n, 26): [("energy", b)],
        (n, 27): [("soft_exp", b)], (n, 28): [("soft_mix", b)],
        (n, 30): [("mix_T", b)], (n, 32): [("v_mix", b)],
        (n + 1, 2): [("v_all", 2 * b)], (n + 1, 3): [("v_all", 2 * b + 1)],
        (n + 1, 6): [("y_T", n)],
        (n + 1, 11): [("out_b", 2 * b)], (n + 1, 12): [("out_b", 2 * b + 1), ("stats", ("f", 2 * b + NCH))],
        (n + 1, 13): ([("stats", ("b", 2))] if b == 0 else []),
        (n + 1, 14): [("root", ("f", 2 * b + NCH))] + ([("root", ("b", 2))] if b == 0 else []),
        (n + 1, 15): [("norm", ("f", 2 * b + NCH))], (n + 1, 16): ([("norm", ("b", 2))] if b == 0 else []),
        (n + 1, 17): [("x_T", ("f", 2 * b + NCH))], (n + 1, 19): ([("x_T", ("b", 2))] if b == 0 else []),
        (n + 1, 20): [("affinity", 2 * b + NCH)], (n + 1, 21): [("top", 2 * b + NCH)],
        (n + 1, 22): [("gate", 2 * b + NCH)], (n + 1, 27): [("gate_T", 2 * b + NCH)],
    })
SIDE.update({
    (6, 1): [("stats", ("f", 7))], (6, 2): [("root", ("f", 7))], (6, 3): [("norm", ("f", 7))],
    (6, 5): [("x_T", ("f", 7))], (6, 6): [("y_T", 5)],
    (6, 9): [("affinity", 7)], (6, 10): [("top", 7)], (6, 14): [("gate", 7)], (6, 20): [("gate_T", 7)],
    (7, 6): [("y_T", 6)],
    (8, 0): [("y_T", 7)],
})
SIDE_STEPS = sorted([k for k in SIDE if isinstance(k, int)]) + sorted([k for k in SIDE if not isinstance(k, int)])
SIDE_ITEM = ring_order([st for k in SIDE_STEPS for st in SIDE[k] if st[0] in (
    "heads_T", "proj", "x_T", "affinity", "gate_T", "y_T", "gram", "gram_k", "q_k", "energy", "mix_T", "v_mix",
    "v_all", "out_b")])
LN = ring_order([st[1] for k in SIDE_STEPS for st in SIDE[k] if st[0] == "stats"])
TAIL_BANK, SIDE_BANK = 1, 7


def chunk_of(key):
    return key[1] % NCH


def hybrid_layer(nc, x, w_qkv, w_proj, b_proj, lam_q1, lam_k1, lam_q2, lam_k2, sub_w,
                 w_q, w_k, w_v, w_o, b_o, cent, e_bias, ws_up, ws_down, w_up, w_down, out):
    ctx = ExitStack()
    with ctx:
        used = {}

        def sb(name, shape, dt=F32, where=ctx):
            used[where] = used.get(where, 0) + int(np.prod(shape[1:])) * (2 if dt == BF16 else 4)
            return where.enter_context(nc.sbuf_tensor(name, shape, dt))

        def sem(name):
            return ctx.enter_context(nc.semaphore(name))

        X = sb("X", [P, NT, DIM])
        XC = sb("XC", [P, NT, DIM])
        SQ = sb("SQ", [P, NT, DIM])
        XT = sb("XT", [P, TOK])
        ln_s = sb("ln_s", [P, NT]); ln_m = sb("ln_m", [P, NT]); ln_v = sb("ln_v", [P, NT])
        ln_sd = sb("ln_sd", [P, NT]); ln_r = sb("ln_r", [P, NT]); ln_t = sb("ln_t", [P, NT])
        WUH = sb("WUH", [P, E * F], F32R); WUL = sb("WUL", [P, E * F], F32R)
        WDH = sb("WDH", [P, PAIRS * DIM], F32R); WDL = sb("WDL", [P, PAIRS * DIM], F32R)
        WSUH = sb("WSUH", [P, P], F32R); WSUL = sb("WSUL", [P, P], F32R)
        WSDH = sb("WSDH", [P, DIM], F32R); WSDL = sb("WSDL", [P, DIM], F32R)
        SEL = sb("SEL", [P, PAIRS * P], F32R)
        ident = sb("ident", [P, P]); identb = sb("identb", [P, P], BF16)
        WQKV = sb("WQKV", [P, 3, DIM]); WPRJ = sb("WPRJ", [P, DIM]); CENT = sb("CENT", [E, DIM])
        WT = sb("WT", [P, 4, DIM])
        CT = sb("CT", [P, E]); WVT = sb("WVT", [P, DIM])
        T8 = sb("T8", [P, HD_B]); H16 = sb("H16", [P, HEADS_B])
        BLK = sb("BLK", [P, DIM])
        WB = sb("WB", [P, 4, DIM])
        BPROJ = sb("BPROJ", [P, DIM]); BO = sb("BO", [P, DIM]); EBIAS = sb("EBIAS", [P, E])
        SUBW = sb("SUBW", [P, 2, VD])
        LAM = sb("LAM", [P, 4, HD_A]); lam_p = sb("lam_p", [P, 2, HD_A]); lam_s = sb("lam_s", [P, 2])
        ln_st = sb("ln_st", [P, 2, 4, 6]); ln_mv = sb("ln_mv", [P, 2, 4, 2]); ln_ve = sb("ln_ve", [P, 2, 4])
        ln_root = sb("ln_root", [P, 2, 4]); ln_inv = sb("ln_inv", [P, 2, 4]); ln_tmp = sb("ln_tmp", [P, 2, 4])
        rms_r = sb("rms_r", [P, TB * GPB * 2])
        top8 = sb("top8", [P, 4, TOPK]); wsum = sb("wsum", [P, 4]); wrec = sb("wrec", [P, 4])
        lam_e = sb("lam_e", [P, 2]); neg_lam = sb("neg_lam", [P, 1])

        VALL = XC[:].rearrange("p t c -> p (t c)").rearrange("p (g t v) -> p g t v", g=NG, t=TB)
        O = XT[:].rearrange("p (g t v) -> p g t v", g=NG, t=TB)

        kept = used[ctx]

        prep = ExitStack()
        RAWU = sb("RAWU", [P, E * F], where=prep); RAWD = sb("RAWD", [P, PAIRS * DIM], where=prep)
        PARTS = sb("PARTS", [P, 3, 2, TOK], BF16, where=prep)
        R1 = XC[:, 0:2 * BANK // DIM, :].rearrange("p t c -> p (t c)").rearrange("p (j n) -> p j n", j=2)
        SELF = SQ
        RAWSU = sb("RAWSU", [P, P], where=prep); RAWSD = sb("RAWSD", [P, DIM], where=prep)
        ZEROS = sb("ZEROS", [P, SEQ], BF16, where=prep); ONES = sb("ONES", [P, SEQ], BF16, where=prep)
        prep.close()

        attn = ExitStack()
        PR = sb("PR", [P, PRING, R, BANK], where=attn)
        KB = sb("KB", [P, 2, R, SEQ], BF16, where=attn)
        QB = sb("QB", [P, 2, SEQ], BF16, where=attn)
        VG = sb("VG", [P, 2, TB, 2, STRIP], where=attn)
        OTS = sb("OTS", [P, 2, BANK], where=attn)
        SHP = sb("SHP", [P, 2, 3 * R * TB], BF16, where=attn)
        SHT = sb("SHT", [3 * R * TB, 2, P], BF16, where=attn)
        ZERO = sb("ZERO", [P, R * TB], where=attn)
        front = used[attn]
        QA = sb("QA", [P, 2, R, SEQ], BF16, where=attn)
        KA = sb("KA", [P, 2, SEQ], BF16, where=attn)
        NEGMAX = sb("NEGMAX", [P, 2, R * TB], where=attn); SHR = sb("SHR", [P, R * TB], where=attn)
        RD = sb("RD", [P, 4 * R], where=attn); TM = sb("TM", [P, 4 * R, VD], where=attn)
        attn.close()

        SI = sb("SI", [P, 3, BANK]); HF = sb("HF", [P, 3, BANK])
        HH = sb("HH", [P, 3, BANK], F32R); HL = sb("HL", [P, 3, BANK], F32R)
        YS = sb("YS", [P, BANK])
        GRAM = sb("GRAM", [P, BATCH, DIM]); GK = sb("GK", [P, BATCH, DIM])
        QK = sb("QK", [P, DIM]); QKR = sb("QKR", [P, HEADS_B])
        EN = sb("EN", [P, HEADS_B]); en_m = sb("en_m", [P, 1]); en_s = sb("en_s", [P, 1]); en_r = sb("en_r", [P, 1])
        MIXT = sb("MIXT", [P, DIM]); MIX = sb("MIX", [P, DIM]); VMIX = sb("VMIX", [P, BATCH, DIM])
        VP = sb("VP", [P, BATCH, S0, S1]); RT = sb("RT", [P, BATCH, SEQ])
        sb("gap", [P, (front - (used[ctx] - kept)) // 4])
        XH = sb("XH", [P, TOK], F32R); XL = sb("XL", [P, TOK], F32R)
        CWT = sb("CWT", [P, 2, BANK], F32R)
        HSQ, CH = SQ[:, 0:TB, :], SQ[:, TB:TB + 4, :]
        AFF, BI, EX, BR = (SQ[:, j:j + 2, :].rearrange("p t c -> p (t c)").rearrange("p (t e) -> p t e", e=E)
                           for j in (TB + 4, TB + 6, 0, 2))
        rms_s, rms_sd, rms_t = (SQ[:, TB + 4 + j, :] for j in range(3))

        PS = ctx.enter_context(nc.psum_tensor("PS", [P, 8, BANK], F32))

        q_stack = nc.dram_tensor("q_stack", (NG, R, STRIP, SEQ), BF16, kind="Internal").ap()
        k_stack = nc.dram_tensor("k_stack", (NG, R, STRIP, SEQ), BF16, kind="Internal").ap()
        mixed_d = nc.dram_tensor("mixed_d", (BATCH, S0, HEADS_B, HD_B, S1), F32, kind="Internal").ap()
        shift_d = nc.dram_tensor("shift_d", (2, 3, R, SEQ), BF16, kind="Internal").ap()

        ld_x, ld_w, ld_mix, ld_exp, ld_b = (sem(n) for n in ("ld_x", "ld_w", "ld_mix", "ld_exp", "ld_b"))
        ident_ok, identb_ok, const_ok, sel_f, sel_r = (sem(n) for n in ("ident_ok", "identb_ok", "const_ok", "sel_f", "sel_r"))
        a_full, a_free, d_full, d_free = (sem(n) for n in ("a_full", "a_free", "d_full", "d_free"))
        dve_step = sem("dve_step")
        pool_step = sem("pool_step")
        xc_ok, sq_ok, ve_ok, sd_ok, xn_ok = (sem(n) for n in ("xc_ok", "sq_ok", "ve_ok", "sd_ok", "xn_ok"))
        lam_in, lam_exp = sem("lam_in"), sem("lam_exp")
        qk_hi, qk_r1, qk_mid, qk_lo = (sem(n) for n in ("qk_hi", "qk_r1", "qk_mid", "qk_lo"))
        st_w = [sem(f"st_w{b}") for b in range(BATCH)]
        w_hi, w_lo = sem("w_hi"), sem("w_lo")
        xb_ok = sem("xb_ok")
        qa_ld = [sem(f"qa_ld{u}") for u in range(2)]
        kb_ld = [sem(f"kb_ld{u}") for u in range(2)]
        m_full, m_free, s_full, p_ready = (sem(n) for n in ("m_full", "m_free", "s_full", "p_ready"))
        av_done, o_evac, o_done, v_cp = (sem(n) for n in ("av_done", "o_evac", "o_done", "v_cp"))
        rd_ok, zeroed = sem("rd_ok"), sem("zeroed")
        sh_split, sh_w, sh_r = sem("sh_split"), sem("sh_w"), sem("sh_r")
        rms_sq, rms_var, rms_sd_ok, rms_r_ok, rms_step, heads_ok = (
            sem(n) for n in ("rms_sq", "rms_var", "rms_sd_ok", "rms_r_ok", "rms_step", "heads_ok"))
        side_full, side_free = sem("side_full"), sem("side_free")
        ln_var, ln_std, ln_xn = sem("ln_var"), sem("ln_std"), sem("ln_xn")
        x_biased = sem("x_biased")
        xh_ok, xl_ok = sem("xh_ok"), sem("xl_ok")
        ex_ok, ch_ok = sem("ex_ok"), sem("ch_ok")
        z_full, silu_ok, c_full, hf_ok = (sem(n) for n in ("z_full", "silu_ok", "c_full", "hf_ok"))
        hh_ok, hl_ok, down_ok = sem("hh_ok"), sem("hl_ok"), sem("down_ok")
        y_evac = sem("y_evac")
        blk_ok, en_in, en_exp, mix_in = (sem(n) for n in ("blk_ok", "en_in", "en_exp", "mix_in"))
        mix_w = [sem(f"mix_w{b}") for b in range(BATCH)]
        mix_r = [sem(f"mix_r{b}") for b in range(BATCH)]
        stored = sem("stored")

        block = ctx.enter_context(nc.Block())

        @block.sync
        def _(sp):
            sp.dma_start(X[:], x.rearrange("b (n p) c -> p (b n) c", p=P)).then_inc(ld_x, 16)
            sp.dma_start(WQKV[:], w_qkv.rearrange("(j p) c -> p j c", p=P)).then_inc(ld_w, 16)
            sp.dma_start(WPRJ[:], w_proj).then_inc(ld_w, 16)
            sp.dma_start(CENT[:], cent).then_inc(ld_w, 16)
            for j, v in enumerate((lam_q1, lam_k1, lam_q2, lam_k2)):
                sp.dma_start(LAM[:, j, :], v.partition_broadcast(P)).then_inc(ld_mix, 16)
            sp.dma_start(BPROJ[:], b_proj.partition_broadcast(P)).then_inc(ld_mix, 16)
            sp.dma_start(BO[:], b_o.partition_broadcast(P)).then_inc(ld_mix, 16)
            sp.dma_start(EBIAS[:], e_bias.partition_broadcast(P)).then_inc(ld_mix, 16)
            for j in range(2):
                sp.dma_start(SUBW[:, j, :], sub_w.partition_broadcast(P)).then_inc(ld_mix, 16)

            for b in range(BATCH):
                sp.wait_ge(qk_mid, 4 * (b + 1))
                sp.wait_ge(qk_lo, 4 * (b + 1))
                if b == 0:
                    sp.wait_ge(const_ok, 2)
                gs = slice(b * GPB, (b + 1) * GPB)
                for j, (stack, slots) in enumerate(((q_stack, Q_SLOTS), (k_stack, K_SLOTS))):
                    def rows(lo):
                        return stack[gs, :, lo:lo + HD_A, :].rearrange("g r d n -> (g r) d n")
                    for c, part in enumerate(slots):
                        sp.dma_start(rows(HD_A * c), PARTS[:, part, j, b * SEQ:(b + 1) * SEQ]).then_inc(st_w[b], 16)
                    fill = ZEROS if j == 0 else ONES
                    sp.dma_start(rows(SHIFT_ROW), fill[:]).then_inc(st_w[b], 16)
                    sp.dma_start(rows(SHIFT_ROW + HD_A), ZEROS[:]).then_inc(st_w[b], 16)

            def load(stack, tile, u, g, there):
                if not isinstance(g, int) or g in (0, GPB):
                    b = 0 if isinstance(g, int) and g < GPB else 1
                    sp.wait_ge(st_w[b], STW)
                if tile is QB or tile is KA:
                    src = stack[bass.ds(g, 1), :, :, :].rearrange("o r s n -> (o r s) n")
                    sp.dma_start(tile[:, u, :], src).then_inc(there, 16)
                    return
                for r in range(R):
                    src = stack[bass.ds(g, 1), r, :, :].rearrange("o s n -> (o s) n")
                    sp.dma_start(tile[STRIP * r:STRIP * (r + 1), u, r, :], src).then_inc(there, 16)

            STW = 16 * 2 * (len(Q_SLOTS) + 2)
            sp.wait_ge(zeroed, 1)
            for u in range(2):
                load(q_stack, QA, u, u, qa_ld[u])
                load(k_stack, KA, u, u, qa_ld[u])
            sp.wait_ge(st_w[1], STW)
            sp.wait_ge(zeroed, 2)
            load(q_stack, QB, 0, 0, sh_w)
            load(k_stack, KB, 0, 0, kb_ld[0])

            def shift_rows(i, s):
                u = s % 2
                sp.wait_ge(m_free, i * ITEMS_PER_BODY + (ITEM["shift", s] + 1))
                sp.dma_start(shift_d[u].rearrange("a r (t n) -> (a r t) n", n=P), SHT[:, u, :]).then_inc(sh_w, 16)
                sp.wait_ge(sh_w, i * 64 + 32 * (s + 1))
                for r in range(R):
                    lo = STRIP * r + SHIFT_ROW
                    sp.dma_start(QB[lo:lo + 3, u, :], shift_d[u, :, r, :]).then_inc(sh_r, 16)

            def group_loads(i, s, more=True):
                u = s % 2
                if s >= 2:
                    sp.wait_ge(s_full, i * (R * BODY) + R * QPG * (s - 1))
                if s:
                    load(q_stack, QB, u, i * 2 + s, sh_w)
                    load(k_stack, KB, u, i * 2 + s, kb_ld[u])
                shift_rows(i, s)
                if more:
                    sp.wait_ge(m_full, i * ITEMS_PER_BODY + (ITEM["max", QPG * s + QPG - 1, 1] + 1))
                    load(q_stack, QA, u, i * 2 + (s + 2), qa_ld[u])
                    load(k_stack, KA, u, i * 2 + (s + 2), qa_ld[u])

            group_loads(0, 0)
            group_loads(0, 1)
            with sp.Fori(0, NG // 2 - 2) as i:
                for s in (2, 3):
                    group_loads(i, s)
            for s in (NG - 2, NG - 1):
                group_loads(0, s, False)
            for b in range(BATCH):
                sp.wait_ge(side_free, SIDE_ITEM["v_all", 2 * b + 1] + 1)
                sp.dma_start(mixed_d[b].rearrange("i a d j -> (a d) i j"), VP[:, b, :, :]).then_inc(mix_w[b], 16)
                sp.wait_ge(mix_w[b], 16)
                for i in range(S0):
                    sp.dma_start(RT[HD_B * i:HD_B * (i + 1), b, :].rearrange("d (a j) -> d a j", j=S1),
                                 mixed_d[b, i].rearrange("a d j -> d a j")).then_inc(mix_r[b], 16)
            rows_out = out.rearrange("b (n p) c -> p (b n) c", p=P)
            for c in range(NCH):
                sp.wait_ge(side_free, SIDE_ITEM["y_T", NCH + c] + 1)
                sp.dma_start(rows_out[:, 4 * c:4 * c + 4, :], X[:, 4 * c:4 * c + 4, :]).then_inc(stored, 16)
            sp.wait_ge(stored, 16 * NCH)

        @block.gpsimd
        def _(pool):
            nsteps = [0]

            def link(ins):
                nsteps[0] += 1
                ins.then_inc(pool_step, 1)
                pool.wait_ge(pool_step, nsteps[0])

            link(nc.gpsimd.memset(ident[:], 0.0))
            nc.gpsimd.affine_select(out=ident[:], in_=ident[:], compare_op=ALU.not_equal, fill=1.0, base=0,
                                    pattern=[[-1, P]], channel_multiplier=1).then_inc(ident_ok, 1)
            pool.dma_start(RAWU[:].rearrange("d (e f) -> d e f", f=F), w_up.rearrange("e d f -> d e f")).then_inc(ld_exp, 16)
            pool.dma_start(RAWD[:].rearrange("p (j d) -> p j d", d=DIM),
                           w_down.rearrange("(j e) f d -> (e f) j d", e=2)).then_inc(ld_exp, 16)
            link(nc.gpsimd.memset(RAWSU[:], 0.0))
            link(nc.gpsimd.memset(RAWSD[:], 0.0))
            pool.dma_start(RAWSU[:, 0:F], ws_up).then_inc(ld_exp, 16)
            pool.dma_start(RAWSD[0:F, :], ws_down).then_inc(ld_exp, 16)
            for j, w in enumerate((w_q, w_k, w_v, w_o)):
                pool.dma_start(WB[:, j, :], w).then_inc(ld_b, 16)
            pool.wait_ge(ident_ok, 1)
            nc.gpsimd.tensor_copy(identb[:], ident[:]).then_inc(identb_ok, 1)
            nc.gpsimd.memset(ZEROS[:], 0.0).then_inc(const_ok, 1)
            nc.gpsimd.memset(ONES[:], 1.0).then_inc(const_ok, 1)
            nc.gpsimd.memset(QA[:].bitcast(F32), 0.0).then_inc(zeroed, 1)
            pool.wait_ge(ld_mix, 16 * 9)
            pool.wait_ge(xc_ok, 1)
            nc.gpsimd.tensor_tensor(X[:], X[:], BPROJ[:].unsqueeze(1).to_broadcast([P, NT, DIM]), op=ALU.add).then_inc(xb_ok, 1)
            pool.wait_ge(sq_ok, 1)
            pool.wait_ge(ve_ok, 1)
            for h in range(2):
                sel = SELF[:].rearrange("p t c -> p (t c)").rearrange("p (j e f) -> p j e f", e=2, f=F)
                if h:
                    pool.wait_ge(sel_r, 1)
                link(nc.gpsimd.memset(SELF[:], 0.0))
                for base in (0, -E):
                    ins = nc.gpsimd.affine_select(out=sel, in_=sel, compare_op=ALU.not_equal, fill=1.0,
                                                  base=base - h * PAIRS, pattern=[[-2, PAIRS // 2], [-1, 2], [0, F]],
                                                  channel_multiplier=1)
                    if base == 0:
                        link(ins)
                ins.then_inc(sel_f, 1)

            pool.wait_ge(w_lo, 4)
            for b in range(BATCH):
                pool.wait_ge(st_w[b], 16 * 2 * (len(Q_SLOTS) + 2))
            nc.gpsimd.memset(KB[:].bitcast(F32), 0.0).then_inc(zeroed, 1)
            link(nc.gpsimd.memset(ZERO[:], 0.0))
            link(nc.gpsimd.memset(VG[:], 0.0))
            link(nc.gpsimd.memset(VG[:, :, :, :, VD:VD + 1], 1.0))

            def values(u, g):
                pool.wait_ge(a_free, A_ITEM["va", NCH - 1] + 1)
                nc.gpsimd.tensor_copy(
                    VG[:, u, :, :, 0:VD],
                    VALL[:, bass.ds(g, 1), :, :].rearrange("p o t (h d) -> p (o t) h d", d=VD)).then_inc(v_cp, 1)

            def shift_parts(i, s):
                pool.wait_ge(m_free, i * ITEMS_PER_BODY + (ITEM["max", QPG * s + QPG - 1, 1] + 1))
                u, w = s % 2, R * TB
                nc.gpsimd.tensor_tensor(SHP[:, u, 0:w], NEGMAX[:, u, :], ZERO[:], op=ALU.add).then_inc(sh_split, 1)
                pool.wait_ge(sh_split, i * 8 + (4 * s + 1))
                nc.gpsimd.tensor_tensor(SHR[:], NEGMAX[:, u, :], SHP[:, u, 0:w], op=ALU.subtract).then_inc(sh_split, 1)
                pool.wait_ge(sh_split, i * 8 + (4 * s + 2))
                nc.gpsimd.tensor_tensor(SHP[:, u, w:2 * w], SHR[:], ZERO[:], op=ALU.add).then_inc(sh_split, 1)
                pool.wait_ge(sh_split, i * 8 + (4 * s + 3))
                nc.gpsimd.tensor_tensor(SHP[:, u, 2 * w:3 * w], SHR[:], SHP[:, u, w:2 * w], op=ALU.subtract).then_inc(sh_split, 1)
                pool.wait_ge(sh_split, i * 8 + (4 * s + 4))

            values(0, 0)
            values(1, 1)
            shift_parts(0, 0)
            with pool.Fori(0, LOOPS) as i:
                for s in (1, 2):
                    shift_parts(i, s)
                    pool.wait_ge(av_done, i * BODY + QPG * s)
                    values((s + 1) % 2, i * 2 + (s + 1))
            shift_parts(0, NG - 1)

            for where in SIDE_STEPS:
                for stage, arg in SIDE[where]:
                    if stage == "rms_scale":
                        heads = O[:, arg * GPB:(arg + 1) * GPB, :, :]
                        flat = heads.rearrange("p g t (h v) -> p (g t h) v", v=VD)
                        pool.wait_ge(rms_r_ok, arg + 1)
                        nc.gpsimd.tensor_tensor(flat, flat, rms_r[:].unsqueeze(2).to_broadcast([P, TB * GPB * 2, VD]),
                                                op=ALU.mult).then_inc(rms_step, 1)
                        pool.wait_ge(rms_step, arg + 1)
                        nc.gpsimd.tensor_tensor(
                            XC[:, arg * TB:(arg + 1) * TB, :].rearrange("p t (g v) -> p t g v", v=2 * VD),
                            heads.rearrange("p g t v -> p t g v"),
                            SUBW[:].rearrange("p j v -> p (j v)").unsqueeze(1).unsqueeze(1).to_broadcast([P, TB, GPB, 2 * VD]),
                            op=ALU.mult).then_inc(heads_ok, 1)
                    elif stage == "x_T" and arg[0] == "f":
                        cols = slice(chunk_of(arg) * BANK, (chunk_of(arg) + 1) * BANK)
                        pool.wait_ge(xh_ok, arg[1] + 1)
                        nc.gpsimd.tensor_tensor(XL[:, cols], XT[:, cols], XH[:, cols].bitcast(F32), op=ALU.subtract).then_inc(xl_ok, 1)
                    elif stage == "x_T":
                        tiles = X[:, 4 * arg[1]:4 * arg[1] + 4, :]
                        pool.wait_ge(ln_xn, LN[arg] + 1)
                        nc.gpsimd.tensor_tensor(tiles, tiles, BO[:].unsqueeze(1).to_broadcast([P, 4, DIM]), op=ALU.add).then_inc(x_biased, 1)

        @block.scalar
        def _(act):
            def evac(key, dst, src):
                n = A_ITEM[key]
                act.wait_ge(a_full, n + 1)
                nc.scalar.activation(dst, src(n % 4), ACT.Copy).then_inc(a_free, 1)

            evac("wT", WT[:].rearrange("p j c -> p (j c)"), lambda n: PS[:, n, :])
            n = A_ITEM["centT"]
            act.wait_ge(a_full, n + 1)
            nc.scalar.activation(CT[:], PS[:, n % 4, 0:E], ACT.Copy)
            nc.scalar.activation(WVT[:], PS[:, n % 4, E:E + DIM], ACT.Copy).then_inc(a_free, 1)
            act.wait_ge(lam_in, 1)
            nc.scalar.activation(lam_e[:], lam_s[:], ACT.Exp).then_inc(lam_exp, 1)
            act.wait_ge(xc_ok, 1)
            nc.scalar.activation(SQ[:], XC[:], ACT.Square).then_inc(sq_ok, 1)
            act.wait_ge(ve_ok, 1)
            nc.scalar.activation(ln_sd[:], ln_v[:], ACT.Sqrt).then_inc(sd_ok, 1)
            for c in range(NCH):
                evac(("xT", c), XT[:, c * BANK:(c + 1) * BANK], lambda n: PS[:, n, :])
            for c in range(NCH):
                for j in range(2):
                    n, cols = D_ITEM["qk", j, c], slice(c * BANK, (c + 1) * BANK)
                    act.wait_ge(d_full, n + 1)
                    nc.scalar.activation(PARTS[:, 0, j, cols], PS[:, 4 + n % 4, :], ACT.Copy).then_inc(qk_hi, 1)
                    act.wait_ge(qk_r1, n + 1)
                    nc.scalar.activation(PARTS[:, 1, j, cols], R1[:, n % 2, :], ACT.Copy).then_inc(qk_mid, 1)
            act.wait_ge(qk_lo, 2 * NCH)
            for c in range(NCH):
                b, h = c // 2, c % 2
                evac(("va", c), VALL[:, b * GPB:(b + 1) * GPB, h * 4:(h + 1) * 4, :].rearrange("p g t v -> p t g v"),
                     lambda n: PS[:, n, :].rearrange("p (t g v) -> p t g v", t=4, g=GPB))
            act.wait_ge(ld_exp, 64)
            for dst, src in ((WUH, RAWU), (WDH, RAWD), (WSUH, RAWSU), (WSDH, RAWSD)):
                nc.scalar.activation(dst[:], src[:], ACT.Copy).then_inc(w_hi, 1)
            for h in range(2):
                act.wait_ge(sel_f, h + 1)
                half = PAIRS // 2 * P
                nc.scalar.activation(SEL[:, h * half:(h + 1) * half], SELF[:].rearrange("p t c -> p (t c)"), ACT.Copy).then_inc(sel_r, 1)
            act.wait_ge(w_lo, 4)
            for b in range(BATCH):
                act.wait_ge(st_w[b], 16 * 2 * (len(Q_SLOTS) + 2))

            def exp_quad(i, s):
                g = i * BODY + s
                if s >= HEAD_Q:
                    act.wait_ge(av_done, g - (PRING - 1))
                for r in range(R):
                    n = R * s + r
                    act.wait_ge(s_full, g * R + (r + 1))
                    nc.scalar.activation(PR[:, s % PRING, r, :], PS[:, 4 + n % 3, :], ACT.Exp, scale=SCALE_A).then_inc(p_ready, 1)
                    if r == 1 and s >= 9 and (s - 9) % TB == 0:
                        evac_out(i, s)

            def evac_out(i, s):
                g, half = (s - 9) // QPG, (s - 9) // TB % 2
                act.wait_ge(av_done, i * BODY + (s - 1))
                before = ITEM["out", g - 1, half] + 1 if g else ITEM["out", g + 1, half] + 1 - ITEMS_PER_BODY
                assert before > 0
                act.wait_ge(m_full, i * ITEMS_PER_BODY + before)
                nc.scalar.activation(OTS[:, half, :], PS[:, 7, :], ACT.Copy).then_inc(o_evac, 1)

            def side_evac(item, dst, src, func=ACT.Copy):
                act.wait_ge(side_full, SIDE_ITEM[item] + 1)
                nc.scalar.activation(dst, src, func).then_inc(side_free, 1)

            def side(where):
                bank = TAIL_BANK if isinstance(where, int) else SIDE_BANK
                for item in SIDE.get(where, ()):
                    stage, arg = item
                    if stage == "rms_squares":
                        act.wait_ge(o_done, 2 * GPB * (arg + 1) + 1)
                        if arg:
                            act.wait_ge(rms_r_ok, arg)
                        nc.scalar.activation(HSQ.rearrange("p t c -> p (t c)"),
                                             O[:, arg * GPB:(arg + 1) * GPB, :, :].rearrange("p g t v -> p (g t v)"),
                                             ACT.Square).then_inc(rms_sq, 1)
                    elif stage == "rms_root":
                        act.wait_ge(rms_var, arg + 1)
                        nc.scalar.activation(rms_sd, rms_s, ACT.Sqrt).then_inc(rms_sd_ok, 1)
                    elif stage == "heads_T":
                        side_evac(item, XT[:, arg * BANK:(arg + 1) * BANK], PS[:, bank, :])
                    elif stage == "root":
                        n = LN[arg]
                        act.wait_ge(ln_var, n + 1)
                        nc.scalar.activation(ln_root[:, n % 2, :], ln_ve[:, n % 2, :], ACT.Sqrt).then_inc(ln_std, 1)
                    elif stage == "x_T":
                        cols = slice(chunk_of(arg) * BANK, (chunk_of(arg) + 1) * BANK)
                        act.wait_ge(side_full, SIDE_ITEM[item] + 1)
                        if arg[0] == "b" or arg[1] >= NCH:
                            act.wait_ge(xl_ok, arg[1] % NCH + 1)
                        if arg[0] == "b":
                            nc.scalar.activation(XT[:, cols], PS[:, bank, :], ACT.Copy).then_inc(side_free, 1)
                        else:
                            nc.scalar.activation(XT[:, cols], PS[:, bank, :], ACT.Copy)
                            nc.scalar.activation(XH[:, cols], PS[:, bank, :], ACT.Copy).then_inc(xh_ok, 1)
                            act.wait_ge(xh_ok, arg[1] + 1)
                            act.sem_inc(side_free, 1)
                    elif stage == "affinity":
                        side_evac(item, AFF, PS[:, bank, 0:4 * E].rearrange("p (t e) -> p t e", e=E))
                        act.wait_ge(side_free, SIDE_ITEM[item] + 1)
                        nc.scalar.activation(EX, AFF, ACT.Sigmoid).then_inc(ex_ok, 1)
                    elif stage == "gate_T":
                        side_evac(item, CWT[:, arg % 2, :], PS[:, bank, :])
                    elif stage == "soft_exp":
                        act.wait_ge(en_in, arg + 1)
                        nc.scalar.activation(EN[:], EN[:], ACT.Exp, scale=SCALE_B).then_inc(en_exp, 1)
                    elif stage == "v_all":
                        b, h = divmod(arg, 2)
                        side_evac(item, VP[:, b, :, h * (S1 // 2):(h + 1) * (S1 // 2)],
                                  PS[:, bank, :].rearrange("p (j i) -> p i j", i=S0))

            for s in range(HEAD_Q):
                exp_quad(0, s)
            with act.Fori(0, LOOPS) as i:
                for s in range(HEAD_Q, HEAD_Q + BODY):
                    exp_quad(i, s)
            for s in range(NQ - BODY + HEAD_Q, NQ):
                exp_quad(0, s)
                side(s)
            evac_out(0, NQ + 1)

            def high(g):
                n, j = divmod(g, UNITS)
                if g >= 3:
                    act.wait_ge(down_ok, g - 2)
                if j < PAIRS:
                    act.wait_ge(hf_ok, n * PAIRS + j + 1)
                else:
                    act.wait_ge(silu_ok, g + 1)
                nc.scalar.activation(HH[:, j % 3, :], HF[:, j % 3, :], ACT.Copy).then_inc(hh_ok, 1)

            def chunk_sum(n):
                act.wait_ge(down_ok, (n + 1) * UNITS)
                nc.scalar.activation(YS[:], PS[:, 5 + n % 2, :], ACT.Copy).then_inc(y_evac, 1)

            for n in range(2 * NCH):
                for j in range(UNITS):
                    g = n * UNITS + j
                    act.wait_ge(z_full, g + 1)
                    if j < PAIRS and g >= 3 and j != 2:
                        act.wait_ge(hf_ok, n * PAIRS + j - 2 if j >= 3 else (n - 1) * PAIRS + 31 + j)
                    if j == PAIRS:
                        act.wait_ge(hl_ok, g - 2)
                        act.wait_ge(hh_ok, g - 2)
                    nc.scalar.activation((SI if j < PAIRS else HF)[:, j % 3, :], PS[:, j % 3, :], ACT.Silu).then_inc(silu_ok, 1)
                    if g:
                        high(g - 1)
                    if n and j == 4:
                        chunk_sum(n - 1)
                    side((n, j))
            high(2 * NCH * UNITS - 1)
            chunk_sum(2 * NCH - 1)
            side((2 * NCH, 0))

        @block.vector
        def _(dve):
            nsteps = [0]

            def link(ins):
                nsteps[0] += 1
                ins.then_inc(dve_step, 1)
                dve.wait_ge(dve_step, nsteps[0])

            def newton(r, t, v):
                link(nc.vector.tensor_tensor(t, r, r, op=ALU.mult))
                link(nc.vector.tensor_tensor(t, t, v, op=ALU.mult))
                link(nc.vector.tensor_scalar(t, t, -0.5, 1.5, ALU.mult, ALU.add))
                link(nc.vector.tensor_tensor(r, r, t, op=ALU.mult))

            def layernorm():
                link(nc.vector.tensor_reduce(ln_s[:], X[:], axis=AX_X, op=ALU.add))
                link(nc.vector.tensor_scalar(ln_m[:], ln_s[:], 1.0 / DIM, None, ALU.mult))
                nc.vector.tensor_tensor(XC[:], X[:], ln_m[:].unsqueeze(2).to_broadcast([P, NT, DIM]), op=ALU.subtract).then_inc(xc_ok, 1)
                dve.wait_ge(sq_ok, 1)
                link(nc.vector.tensor_reduce(ln_s[:], SQ[:], axis=AX_X, op=ALU.add))
                nc.vector.tensor_scalar(ln_v[:], ln_s[:], 1.0 / DIM, LN_EPS, ALU.mult, ALU.add).then_inc(ve_ok, 1)
                dve.wait_ge(sd_ok, 1)
                link(nc.vector.reciprocal(ln_r[:], ln_sd[:]))
                newton(ln_r[:], ln_t[:], ln_v[:])
                for c in range(NCH):
                    t = XC[:, 4 * c:4 * c + 4, :]
                    nc.vector.tensor_tensor(t, t, ln_r[:, 4 * c:4 * c + 4].unsqueeze(2).to_broadcast([P, 4, DIM]), op=ALU.mult).then_inc(xn_ok, 1)

            dve.wait_ge(ident_ok, 1)
            link(nc.vector.tensor_reduce(T8[:], ident[:].rearrange("p (a d) -> p d a", d=HD_B), axis=AX_X, op=ALU.add))
            link(nc.vector.tensor_reduce(H16[:], ident[:].rearrange("p (a d) -> p a d", d=HD_B), axis=AX_X, op=ALU.add))
            nc.vector.tensor_copy(BLK[:].rearrange("p (a d) -> p a d", d=HD_B),
                                  H16[:].unsqueeze(2).to_broadcast([P, HEADS_B, HD_B])).then_inc(blk_ok, 1)
            dve.wait_ge(ld_mix, 16 * 9)
            for j in range(2):
                link(nc.vector.tensor_tensor(lam_p[:, j, :], LAM[:, 2 * j, :], LAM[:, 2 * j + 1, :], op=ALU.mult))
            nc.vector.tensor_reduce(lam_s[:], lam_p[:], axis=AX_X, op=ALU.add).then_inc(lam_in, 1)
            link(nc.vector.tensor_scalar(SUBW[:], SUBW[:], 1.0 - LAMBDA_INIT, None, ALU.mult))
            dve.wait_ge(ld_x, 16)
            layernorm()
            dve.wait_ge(lam_exp, 1)
            link(nc.vector.tensor_tensor(neg_lam[:], lam_e[:, 1:2], lam_e[:, 0:1], op=ALU.subtract))
            link(nc.vector.tensor_scalar(neg_lam[:], neg_lam[:], -LAMBDA_INIT, None, ALU.add))
            for c in range(NCH):
                for j in range(2):
                    n, cols = D_ITEM["qk", j, c], slice(c * BANK, (c + 1) * BANK)
                    dve.wait_ge(qk_hi, n + 1)
                    nc.vector.tensor_tensor(R1[:, n % 2, :], PS[:, 4 + n % 4, :], PARTS[:, 0, j, cols], op=ALU.subtract).then_inc(qk_r1, 1)
                    dve.wait_ge(qk_r1, n + 1)
                    dve.wait_ge(qk_mid, n + 1)
                    nc.vector.tensor_tensor(PARTS[:, 2, j, cols], R1[:, n % 2, :], PARTS[:, 1, j, cols], op=ALU.subtract).then_inc(qk_lo, 1)
                    dve.wait_ge(qk_lo, n + 1)
            for n, (dst, src, hi) in enumerate(((WUL, RAWU, WUH), (WDL, RAWD, WDH), (WSUL, RAWSU, WSUH), (WSDL, RAWSD, WSDH))):
                dve.wait_ge(w_hi, n + 1)
                nc.vector.tensor_tensor(dst[:], src[:], hi[:].bitcast(F32), op=ALU.subtract).then_inc(w_lo, 1)
            nc.vector.memset(TM[:], 0.0).then_inc(o_done, 1)
            def slot(it):
                return 2 * (it % 2)

            def max_quad(i, s):
                at = i * ITEMS_PER_BODY
                for key in quad_items(s):
                    it = ITEM[key]
                    e = slot(it)
                    dve.wait_ge(m_full, at + (it + 1))
                    if key[0] == "max":
                        ga, a = key[1] // QPG, 2 * (key[1] % QPG) + key[2]
                        if a == 0 and (ga >= 2):
                            dve.wait_ge(sh_split, i * 8 + 4 * (ga - 1))
                        nc.vector.tensor_reduce(NEGMAX[:, ga % 2, a:a + 1], PS[:, e:e + 2, :].rearrange("p b n -> p (b n)"),
                                                axis=AX_X, op=ALU.max, negate=True).then_inc(m_free, 1)
                    elif key[0] == "shift":
                        ga = key[1]
                        if ga >= 2:
                            dve.wait_ge(sh_w, i * 64 + 32 * (ga - 1))
                        nc.vector.tensor_copy(SHT[:, ga % 2, :], PS[0:3 * R * TB, e, 0:P // 2].bitcast(BF16)).then_inc(m_free, 1)
                    else:
                        gg, half = key[1], key[2]
                        n = 2 * gg + half
                        rows = PS[:, e, :].rearrange("p (m v) -> p m v", v=STRIP)
                        dve.wait_ge(o_done, i * 4 + (n + 1))
                        ob = i * 8 + 2 * n
                        nc.vector.reciprocal(RD[:], rows[:, :, VD]).then_inc(rd_ok, 1)
                        dve.wait_ge(rd_ok, ob + 1)
                        second = RD[:].rearrange("p (m s) -> p m s", s=2)[:, :, 1]
                        nc.vector.tensor_scalar(second, second, neg_lam[:], None, ALU.mult).then_inc(rd_ok, 1)
                        dve.wait_ge(rd_ok, ob + 2)
                        nc.vector.tensor_tensor(TM[:], rows[:, :, 0:VD], RD[:].unsqueeze(2).to_broadcast([P, 4 * R, VD]),
                                                op=ALU.mult).then_inc(m_free, 1)
                        dve.wait_ge(m_free, at + (it + 1))
                        tm = TM[:].rearrange("p (t h s) v -> p t h s v", h=2, s=2)
                        dst = O[:, bass.ds(i * 2 + gg, 1), 4 * half:4 * half + 4, :]
                        nc.vector.tensor_tensor(dst.rearrange("p o t (h v) -> p (o t) h v", v=VD),
                                                tm[:, :, :, 0, :], tm[:, :, :, 1, :], op=ALU.add).then_inc(o_done, 1)

            for s in range(-LEAD, HEAD_Q):
                max_quad(0, s)
            with dve.Fori(0, LOOPS) as i:
                for s in range(HEAD_Q, HEAD_Q + BODY):
                    max_quad(i, s)
            def low(g):
                if g >= 3:
                    dve.wait_ge(down_ok, g - 2)
                dve.wait_ge(hh_ok, g + 1)
                j = g % UNITS
                nc.vector.tensor_tensor(HL[:, j % 3, :], HF[:, j % 3, :], HH[:, j % 3, :].bitcast(F32), op=ALU.subtract).then_inc(hl_ok, 1)

            def side(where):
                bank = TAIL_BANK if isinstance(where, int) else SIDE_BANK
                for item in SIDE.get(where, ()):
                    stage, arg = item
                    if item in SIDE_ITEM and stage in ("proj", "out_b", "y_T", "gram", "gram_k", "q_k", "energy", "mix_T", "v_mix"):
                        dve.wait_ge(side_full, SIDE_ITEM[item] + 1)
                    if stage == "rms_sums":
                        dve.wait_ge(rms_sq, arg + 1)
                        link(nc.vector.tensor_reduce(rms_s, HSQ.rearrange("p t c -> p (t c)").rearrange("p (m v) -> p m v", v=VD),
                                                     axis=AX_X, op=ALU.add))
                        nc.vector.tensor_scalar(rms_s, rms_s, 1.0 / VD, EPS_A, ALU.mult, ALU.add).then_inc(rms_var, 1)
                    elif stage == "rms_scale":
                        dve.wait_ge(rms_sd_ok, arg + 1)
                        link(nc.vector.reciprocal(rms_r[:], rms_sd))
                        newton(rms_r[:], rms_t, rms_s)
                        dve.wait_ge(v_cp, NG)
                        dve.sem_inc(rms_r_ok, 1)
                    elif stage in ("proj", "out_b"):
                        tiles = X[:, 4 * arg:4 * arg + 4, :].rearrange("p t c -> p (t c)")
                        if stage == "proj":
                            dve.wait_ge(xb_ok, 1)
                        else:
                            dve.wait_ge(x_biased, arg + 1)
                        nc.vector.tensor_tensor(tiles, tiles, PS[:, bank, :], op=ALU.add).then_inc(side_free, 1)
                    elif stage == "y_T":
                        tiles = X[:, 4 * (arg % NCH):4 * (arg % NCH) + 4, :].rearrange("p t c -> p (t c)")
                        nc.vector.tensor_tensor(tiles, tiles, PS[:, bank, :], op=ALU.add).then_inc(side_free, 1)
                    elif stage == "stats":
                        n, c = LN[arg], chunk_of(arg)
                        before = {"f": ("proj", c) if arg[1] < NCH else ("out_b", c), "b": ("y_T", c)}[arg[0]]
                        dve.wait_ge(side_free, SIDE_ITEM[before] + 1)
                        for t in range(4):
                            last = nc.vector.bn_stats(ln_st[:, n % 2, t, :], X[:, 4 * c + t, :])
                        link(last)
                        for t in range(4):
                            last = nc.vector.bn_aggr(ln_mv[:, n % 2, t, :], ln_st[:, n % 2, t, :])
                        link(last)
                        nc.vector.tensor_scalar(ln_ve[:, n % 2, :], ln_mv[:, n % 2, :, 1], LN_EPS, None, ALU.add).then_inc(ln_var, 1)
                    elif stage == "norm":
                        n, c = LN[arg], chunk_of(arg)
                        dve.wait_ge(ln_std, n + 1)
                        link(nc.vector.reciprocal(ln_inv[:, n % 2, :], ln_root[:, n % 2, :]))
                        newton(ln_inv[:, n % 2, :], ln_tmp[:, n % 2, :], ln_ve[:, n % 2, :])
                        for t in range(4):
                            last = nc.vector.tensor_scalar(XC[:, 4 * c + t, :], X[:, 4 * c + t, :], ln_mv[:, n % 2, t, 0:1],
                                                           ln_inv[:, n % 2, t:t + 1], ALU.subtract, ALU.mult)
                        last.then_inc(ln_xn, 1)
                    elif stage == "top":
                        dve.wait_ge(side_free, SIDE_ITEM["affinity", arg] + 1)
                        link(nc.vector.tensor_tensor(BI, AFF, EBIAS[:].unsqueeze(1).to_broadcast([P, 4, E]), op=ALU.add))
                        for t in range(4):
                            last = nc.vector.max(top8[:, t, :], BI[:, t, :])
                        link(last)
                        for t in range(4):
                            last = nc.vector.match_replace(BR[:, t, :], top8[:, t, :], BI[:, t, :], -3.0e38)
                        link(last)
                        link(nc.vector.tensor_tensor(BR, BR, BI, op=ALU.not_equal))
                    elif stage == "gate":
                        dve.wait_ge(ex_ok, arg + 1)
                        link(nc.vector.tensor_tensor(EX, EX, BR, op=ALU.mult))
                        link(nc.vector.tensor_reduce(wsum[:], EX, axis=AX_X, op=ALU.add))
                        link(nc.vector.tensor_scalar(wsum[:], wsum[:], 1e-8, None, ALU.add))
                        link(nc.vector.reciprocal(wrec[:], wsum[:]))
                        link(nc.vector.tensor_tensor(EX, EX, wrec[:].unsqueeze(2).to_broadcast([P, 4, E]), op=ALU.mult))
                        link(nc.vector.tensor_copy(CH[:, :, 0:E].bitcast(F32R), EX))
                        nc.vector.tensor_tensor(CH[:, :, E:2 * E], EX, CH[:, :, 0:E], op=ALU.subtract).then_inc(ch_ok, 1)
                    elif stage == "gram":
                        nc.vector.tensor_copy(GRAM[:, arg, :], PS[:, bank, 0:DIM]).then_inc(side_free, 1)
                    elif stage == "gram_k":
                        nc.vector.tensor_copy(GK[:, arg, :], PS[:, bank, 0:DIM]).then_inc(side_free, 1)
                    elif stage == "q_k":
                        by_head = "p (h d) -> p h d"
                        link(nc.vector.tensor_tensor(QK[:].rearrange(by_head, d=HD_B), PS[:, bank, 0:DIM].rearrange(by_head, d=HD_B),
                                                     T8[:].unsqueeze(1).to_broadcast([P, HEADS_B, HD_B]), op=ALU.mult))
                        nc.vector.tensor_reduce(QKR[:], QK[:].rearrange(by_head, d=HD_B), axis=AX_X, op=ALU.add).then_inc(side_free, 1)
                    elif stage == "energy":
                        link(nc.vector.tensor_reduce(en_m[:], PS[:, bank, 0:HEADS_B], axis=AX_X, op=ALU.max))
                        nc.vector.tensor_scalar(EN[:], PS[:, bank, 0:HEADS_B], en_m[:], None, ALU.subtract).then_inc(side_free, 1)
                        dve.wait_ge(side_free, SIDE_ITEM[item] + 1)
                        dve.sem_inc(en_in, 1)
                    elif stage == "soft_mix":
                        dve.wait_ge(en_exp, arg + 1)
                        link(nc.vector.tensor_reduce(en_s[:], EN[:], axis=AX_X, op=ALU.add))
                        link(nc.vector.reciprocal(en_r[:], en_s[:]))
                        link(nc.vector.tensor_scalar(EN[:], EN[:], en_r[:], None, ALU.mult))
                        nc.vector.tensor_tensor(MIXT[:].rearrange("p (h d) -> p h d", d=HD_B),
                                                EN[:].unsqueeze(2).to_broadcast([P, HEADS_B, HD_B]),
                                                T8[:].unsqueeze(1).to_broadcast([P, HEADS_B, HD_B]), op=ALU.mult).then_inc(mix_in, 1)
                    elif stage == "mix_T":
                        nc.vector.tensor_copy(MIX[:], PS[:, bank, 0:DIM]).then_inc(side_free, 1)
                    elif stage == "v_mix":
                        nc.vector.tensor_copy(VMIX[:, arg, :], PS[:, bank, 0:DIM]).then_inc(side_free, 1)

            for s in range(NQ - BODY + HEAD_Q, NQ + 4):
                max_quad(0, s)
                side(s)
            dve.wait_ge(o_done, 2 * NG + 1)
            for n in range(2 * NCH):
                for j in range(UNITS):
                    g, h = n * UNITS + j, n * PAIRS + j
                    if j < PAIRS:
                        dve.wait_ge(silu_ok, g + 1)
                        dve.wait_ge(c_full, h + 1)
                        if g >= 3:
                            dve.wait_ge(hh_ok, g - 2)
                            dve.wait_ge(hl_ok, g - 2)
                        nc.vector.tensor_tensor(HF[:, j % 3, :], SI[:, j % 3, :], PS[:, 3 + j % 2, :], op=ALU.mult).then_inc(hf_ok, 1)
                    if g:
                        dve.wait_ge(hf_ok, n * PAIRS + j if j <= PAIRS else n * PAIRS)
                        low(g - 1)
                    side((n, j))
            low(2 * NCH * UNITS - 1)
            side((2 * NCH, 0))

        @block.tensor
        def _(pe):
            mm = nc.tensor.matmul

            def ring(key, items, full, free, put):
                n = items[key]
                if n >= 4:
                    pe.wait_ge(free, n - 3)
                put((0 if items is A_ITEM else 4) + n % 4).then_inc(full, 1)

            def transposes(tiles):
                def put(n):
                    for j, t in enumerate(tiles):
                        last = nc.tensor.transpose(PS[:, n, j * P:j * P + t.shape[0]], t, ident[0:t.shape[0], 0:t.shape[0]])
                    return last
                return put

            pe.wait_ge(ident_ok, 1)
            pe.wait_ge(ld_w, 48)
            ring("wT", A_ITEM, a_full, a_free, transposes([WQKV[:, j, :] for j in range(3)] + [WPRJ[:]]))
            pe.wait_ge(ld_b, 64)

            def centroids(n):
                nc.tensor.transpose(PS[:, n, 0:E], CENT[:], ident[0:E, 0:E])
                return nc.tensor.transpose(PS[:, n, E:E + DIM], WB[:, 2, :], ident[:])

            ring("centT", A_ITEM, a_full, a_free, centroids)
            for c in range(NCH):
                pe.wait_ge(xn_ok, c + 1)
                ring(("xT", c), A_ITEM, a_full, a_free, transposes([XC[:, 4 * c + j, :] for j in range(4)]))

            def chunk(w, c):
                return lambda n: mm(PS[:, n, :], w, XT[:, c * BANK:(c + 1) * BANK], start=True, stop=True)

            def tokens(src, w, c):
                def put(n):
                    for j in range(4):
                        t = 4 * c + j
                        last = mm(PS[:, n, j * P:(j + 1) * P], src[:, t * P:(t + 1) * P], w, start=True, stop=True)
                    return last
                return put

            for c in range(NCH):
                pe.wait_ge(a_free, A_ITEM["xT", c] + 1)
                for j in range(2):
                    ring(("qk", j, c), D_ITEM, d_full, qk_r1, chunk(WT[:, j, :], c))
            for c in range(NCH):
                ring(("va", c), A_ITEM, a_full, a_free, tokens(XT, WT[:, 2, :], c))
            pe.wait_ge(qk_r1, 2 * NCH)
            pe.wait_ge(a_free, A_ITEM["va", NCH - 1] + 1)
            pe.wait_ge(identb_ok, 1)

            def m_items(i, which):
                at = i * ITEMS_PER_BODY
                for key in which:
                    it = ITEM[key]
                    e = 2 * (it % 2)
                    if it >= 2:
                        pe.wait_ge(m_free, at + (it - 1))
                    if key[0] == "max":
                        ga, a = key[1] // QPG, 2 * (key[1] % QPG) + key[2]
                        r, nt, u = a // TB, a % TB, ga % 2
                        if a == 0:
                            pe.wait_ge(qa_ld[u], i * (16 * (R + 1)) + 16 * (R + 1) * (ga // 2 + 1))
                        for h in range(2):
                            last = mm(PS[:, e + h, :], QA[:, u, r, nt * P:(nt + 1) * P], KA[:, u, h * BANK:(h + 1) * BANK],
                                      start=True, stop=True)
                    elif key[0] == "shift":
                        ga = key[1]
                        pe.wait_ge(sh_split, i * 8 + 4 * (ga + 1))
                        last = nc.tensor.transpose(PS[0:3 * R * TB, e, 0:P // 2].bitcast(BF16), SHP[:, ga % 2, :], identb[:])
                    else:
                        gg, half = key[1], key[2]
                        pe.wait_ge(o_evac, i * 4 + 2 * gg + half + 1)
                        for j in range(4):
                            last = nc.tensor.transpose(PS[:, e, j * P:(j + 1) * P], OTS[:, half, j * P:(j + 1) * P], ident[:])
                    last.then_inc(m_full, 1)

            def scores(i, s, r):
                g, n, q = i * BODY + s, R * s + r, s % QPG
                half, mt, u = q // TB, q % TB, s // QPG % 2
                if q == 0 and r == 0:
                    grp = s // QPG
                    pe.wait_ge(kb_ld[u], i * (16 * R) + 16 * R * (grp // 2 + 1))
                    pe.wait_ge(sh_r, i * 128 + 64 * (grp + 1))
                if n >= 3:
                    pe.wait_ge(p_ready, g * R + (r - 1 if n in (R * HEAD_Q, R * HEAD_Q + 1) else r - 2))
                mm(PS[:, 4 + n % 3, :], KB[:, u, r, mt * P:(mt + 1) * P], QB[:, u, half * BANK:(half + 1) * BANK],
                   start=True, stop=True).then_inc(s_full, 1)

            def weighted_values(i, s):
                g, q = i * BODY + s, s % QPG
                mt, u = q % TB, s // QPG % 2
                pe.wait_ge(p_ready, g * R + R)
                if q == 0:
                    pe.wait_ge(v_cp, i * 2 + s // QPG + 1)
                if mt == 0 and s:
                    pe.wait_ge(o_evac, i * 4 + s // TB)
                for r in range(R):
                    last = mm(PS[STRIP * r:STRIP * (r + 1), 7, :], VG[:, u, mt, r // 2, :], PR[:, s % PRING, r, :],
                              start=mt == 0, stop=mt == TB - 1)
                last.then_inc(av_done, 1)

            def quad(i, s, with_scores=True):
                items = quad_items(s)
                cut = (len(items) + 1) // 2
                if with_scores:
                    scores(i, s, 0)
                    scores(i, s, 1)
                m_items(i, items[:cut])
                if with_scores:
                    scores(i, s, 2)
                    scores(i, s, 3)
                m_items(i, items[cut:])

            def side(where):
                bank = TAIL_BANK if isinstance(where, int) else SIDE_BANK
                for item in SIDE.get(where, ()):
                    stage, arg = item
                    if item not in SIDE_ITEM:
                        continue
                    if SIDE_ITEM[item]:
                        pe.wait_ge(side_free, SIDE_ITEM[item])
                    else:
                        pe.wait_ge(m_free, ITEM["max", NQ - 1, 1] + 1)
                    if stage == "heads_T":
                        pe.wait_ge(heads_ok, arg // 2 + 1)
                        last = transposes([XC[:, 4 * arg + j, :] for j in range(4)])(bank)
                    elif stage == "proj":
                        last = tokens(XT, WT[:, 3, :], arg)(bank)
                    elif stage == "x_T":
                        c = chunk_of(arg)
                        pe.wait_ge(ln_xn, LN[arg] + 1)
                        last = transposes([XC[:, 4 * c + j, :] for j in range(4)])(bank)
                    elif stage == "affinity":
                        for j in range(4):
                            t = 4 * (arg % NCH) + j
                            last = mm(PS[:, bank, j * E:(j + 1) * E], XT[:, t * P:(t + 1) * P], CT[:], start=True, stop=True)
                    elif stage == "gate_T":
                        pe.wait_ge(ch_ok, arg + 1)
                        last = transposes([CH[:, j, :] for j in range(4)])(bank)
                    elif stage == "y_T":
                        pe.wait_ge(y_evac, arg + 1)
                        last = transposes([YS[:, j * P:(j + 1) * P] for j in range(4)])(bank)
                    elif stage == "gram":
                        for j in range(TB):
                            t = XC[:, arg * TB + j, :]
                            last = mm(PS[:, bank, 0:DIM], t, t, start=j == 0, stop=j == TB - 1)
                    elif stage == "gram_k":
                        last = mm(PS[:, bank, 0:DIM], GRAM[:, arg, :], WB[:, 1, :], start=True, stop=True)
                    elif stage == "q_k":
                        last = mm(PS[:, bank, 0:DIM], WB[:, 0, :], GK[:, arg, :], start=True, stop=True)
                    elif stage == "energy":
                        pe.wait_ge(blk_ok, 1)
                        last = mm(PS[:, bank, 0:HEADS_B], BLK[:], QKR[:], start=True, stop=True)
                    elif stage == "mix_T":
                        pe.wait_ge(mix_in, arg + 1)
                        last = nc.tensor.transpose(PS[:, bank, 0:DIM], MIXT[:], ident[:])
                    elif stage == "v_mix":
                        last = mm(PS[:, bank, 0:DIM], WVT[:], MIX[:], start=True, stop=True)
                    elif stage == "v_all":
                        last = chunk(VMIX[:, arg // 2, :], arg)(bank)
                    elif stage == "out_b":
                        pe.wait_ge(mix_r[arg // 2], 16 * S0)
                        last = tokens(RT[:].rearrange("p b n -> p (b n)"), WB[:, 3, :], arg)(bank)
                    last.then_inc(side_full, 1)

            for s in range(-LEAD, 0):
                quad(0, s, False)
            for s in range(HEAD_Q):
                quad(0, s)
                if s:
                    weighted_values(0, s - 1)
            with pe.Fori(0, LOOPS) as i:
                for s in range(HEAD_Q, HEAD_Q + BODY):
                    quad(i, s)
                    weighted_values(i, s - 1)
            for s in range(NQ - BODY + HEAD_Q, NQ):
                quad(0, s)
                side(s)
                weighted_values(0, s - 1)
            weighted_values(0, NQ - 1)
            for s in range(NQ, NQ + 4):
                quad(0, s, False)

            def split3(dst, ah, al, bh, bl, first, last):
                mm(dst, ah, bh, start=first, stop=False)
                mm(dst, ah, bl, start=False, stop=False)
                return mm(dst, al, bh, start=False, stop=last)

            def up(n, j):
                g, h, cols = n * UNITS + j, n * PAIRS + j, slice(n % NCH * BANK, (n % NCH + 1) * BANK)
                wh, wl = (WUH[:, j * P:(j + 1) * P], WUL[:, j * P:(j + 1) * P]) if j < PAIRS else (WSUH[:], WSUL[:])
                if g >= 3:
                    pe.wait_ge(silu_ok, g - 2)
                split3(PS[:, j % 3, :], wh, wl, XH[:, cols], XL[:, cols], True, True).then_inc(z_full, 1)
                if j < PAIRS:
                    if h >= 2:
                        pe.wait_ge(hf_ok, h - 1)
                    mm(PS[:, 3 + j % 2, :], SEL[:, j * P:(j + 1) * P], CWT[:, n % 2, :], start=True, stop=True).then_inc(c_full, 1)

            def down(g):
                n, j = divmod(g, UNITS)
                wh, wl = (WDH[:, j * DIM:(j + 1) * DIM], WDL[:, j * DIM:(j + 1) * DIM]) if j < PAIRS else (WSDH[:], WSDL[:])
                if j == 0 and n >= 2:
                    pe.wait_ge(y_evac, n - 1)
                pe.wait_ge(hh_ok, g + 1)
                pe.wait_ge(hl_ok, g + 1)
                split3(PS[:, 5 + n % 2, :], wh, wl, HH[:, j % 3, :], HL[:, j % 3, :], j == 0, j == UNITS - 1).then_inc(down_ok, 1)

            pe.wait_ge(m_free, len(ITEM))
            pe.wait_ge(o_evac, 2 * NG)
            for n in range(2 * NCH):
                pe.wait_ge(xl_ok, n + 1)
                pe.wait_ge(side_free, SIDE_ITEM["gate_T", n] + 1)
                for j in range(UNITS):
                    up(n, j)
                    side((n, j))
                    if n * UNITS + j >= LAG:
                        down(n * UNITS + j - LAG)
            for g in range(2 * NCH * UNITS - LAG, 2 * NCH * UNITS):
                down(g)
            side((2 * NCH, 0))


_INS = ["L0_attn_a_x", "L0_attn_a_w_qkv", "L0_attn_a_w_proj", "L0_attn_a_b_proj", "L0_attn_a_lambda_q1",
        "L0_attn_a_lambda_k1", "L0_attn_a_lambda_q2", "L0_attn_a_lambda_k2", "L0_attn_a_sub_norm_w",
        "L0_attn_b_Wq", "L0_attn_b_Wk", "L0_attn_b_Wv", "L0_attn_b_Wo", "L0_attn_b_bo", "L0_ffn_centroids",
        "L0_ffn_expert_biases", "L0_ffn_Ws_up", "L0_ffn_Ws_down", "L0_ffn_W_up", "L0_ffn_W_down"]
_OUTS = [((BATCH, SEQ, DIM), "float32")]


def kernel(**inputs):
    import numpy as _np
    import concourse.bacc as _bacc
    from concourse import mybir as _mybir
    from concourse.bass_utils import run_bass_kernel_spmd as _run

    nc = _bacc.Bacc("TRN2", target_bir_lowering=False, num_devices=1)
    arrays, args = {}, []
    for name in _INS:
        a = _np.ascontiguousarray(inputs[name])
        arrays[f"in_{name}_dram"] = a
        args.append(nc.dram_tensor(f"in_{name}_dram", a.shape, _mybir.dt.from_np(a.dtype), kind="ExternalInput").ap())
    for i, (shape, dtype) in enumerate(_OUTS):
        dt = _mybir.dt.from_np(_np.dtype(dtype))
        args.append(nc.dram_tensor(f"out_{i}_dram", shape, dt, kind="ExternalOutput").ap())
    hybrid_layer(nc, *args)
    r = _run(nc, [arrays], core_ids=[0])
    return r.results[0]["out_0_dram"]
```

```python
from contextlib import ExitStack

import numpy as np

import concourse.bass as bass
from concourse import mybir

F32 = mybir.dt.float32
F32R = mybir.dt.float32r
BF16 = mybir.dt.bfloat16
ALU = mybir.AluOpType
ACT = mybir.ActivationFunctionType
AX_X = mybir.AxisListType.X

P = 128
BATCH, SEQ, DIM = 2, 1024, 128
NT = BATCH * SEQ // P
TB = SEQ // P
TOK = BATCH * SEQ
BANK = 512
NCH = TOK // BANK
LN_EPS = 1e-5

HEADS_A = 16
HD_A = DIM // HEADS_A // 2
SUBS = 2 * HEADS_A
R = 4
GPB = SUBS // R
NG = BATCH * GPB
VD = 2 * HD_A
SCALE_A = HD_A ** -0.5
LAMBDA_INIT = 0.8 - 0.6 * float(np.exp(-0.3 * 0))
EPS_A = 1e-5
Q_SLOTS = (0, 0, 0, 1, 2, 1)
K_SLOTS = (2, 1, 0, 0, 0, 1)
SHIFT_ROW = HD_A * len(Q_SLOTS)
STRIP = 32
STACK_WRITES = 16 * 2 * (len(Q_SLOTS) + 1)

QPG = 2 * TB
NQ = NG * QPG
LEAD = 20
BODY = 2 * QPG
HEAD_Q = 4
LOOPS = (NQ - BODY) // BODY
PRING = 4

HEADS_B = 16
HD_B = DIM // HEADS_B
SCALE_B = float(1.0 / np.sqrt(HD_B))
S0 = HEADS_B
S1 = SEQ // S0

E, F, TOPK = 64, 64, 8
PAIRS = E // 2
UNITS = PAIRS + 1
LAG = 4
HPLACES = LAG + 1


def max_pass_items():
    index = {}
    for g in range(-LEAD, NQ + 4):
        for key in quad_items(g):
            index[key] = len(index)
    return index


def quad_items(g):
    items = []
    if 0 <= g + LEAD < NQ:
        items.append(("max", g + LEAD, 0))
    if (g + 3) % QPG == 0 and 0 <= (g + 3) // QPG < NG:
        items.append(("shift", (g + 3) // QPG))
    if g >= 10 and (g - 10) % TB == 0 and (g - 10) // TB < 2 * NG:
        items.append(("out", (g - 10) // TB // 2, (g - 10) // TB % 2))
    if 0 <= g + LEAD < NQ:
        items.append(("max", g + LEAD, 1))
    return items


ITEM = max_pass_items()
ITEMS_PER_BODY = 2 * BODY + 2 + 4


def ring_order(names):
    return {n: i for i, n in enumerate(names)}


A_ITEM = ring_order(["wT"] + [("xT", c) for c in range(NCH)] + [("va", c) for c in range(NCH)] + ["centT"])
D_ITEM = ring_order([("qk", j, c) for c in range(NCH) for j in range(2)])

SIDE = {
    NQ - 28: [("rms_squares", 0), ("rms_sums", 0)], NQ - 26: [("rms_root", 0)], NQ - 25: [("rms_scale", 0)],
    NQ - 19: [("heads_T", 0)], NQ - 17: [("proj", 0), ("stats", ("f", 0))], NQ - 16: [("norm", ("f", 0))],
    NQ - 13: [("x_T", ("f", 0))], NQ - 10: [("affinity", 0)], NQ - 9: [("top", 0)], NQ - 8: [("sum", 0)], NQ - 4: [("gate_T", 0)],
    (0, 4): [("heads_T", 1)], (0, 6): [("proj", 1)], (0, 7): [("stats", ("f", 1))],
    (0, 9): [("norm", ("f", 1))], (0, 12): [("x_T", ("f", 1))], (0, 15): [("affinity", 1)], (0, 17): [("top", 1)],
    (0, 20): [("sum", 1)], (0, 24): [("rms_squares", 1)], (0, 25): [("rms_sums", 1), ("gate_T", 1)],
    (0, 27): [("rms_root", 1)], (0, 28): [("rms_scale", 1)],
}
for n in (1, 2, 4):
    SIDE.update({
        (n, 2): [("heads_T", n + 1)] if n < NCH else [],
        (n, 4): [("proj", n + 1)] if n < NCH else [],
        (n, 5): [("stats", ("f", n + 1))],
        (n, 7): [("norm", ("f", n + 1))],
        (n, 8): [("y_T", n - 1)],
        (n, 9): [("stats", ("b", n - 1))],
        (n, 11): [("x_T", ("f", n + 1)), ("norm", ("b", n - 1))],
        (n, 14): [("affinity", n + 1)], (n, 16): [("x_T", ("b", n - 1)), ("top", n + 1)],
        (n, 19): [("sum", n + 1)], (n, 24): [("gate_T", n + 1)],
    })
for n, b in ((2, 0), (4, 1)):
    SIDE.update({
        (n, 18): [("gram", b)], (n, 20): [("gram_k", b)], (n, 22): [("q_k", b)], (n, 25): [("energy", b)],
        (n, 26): [("soft_exp", b)], (n, 27): [("soft_mix", b)],
        (n, 30): [("mix_T", b)], (n + 1, 0): [("v_mix", b)],
        (n + 1, 2): [("v_all", 2 * b)], (n + 1, 3): [("v_all", 2 * b + 1)],
        (n + 1, 7): [("y_T", n)],
        (n + 1, 13): [("out_b", 2 * b)], (n + 1, 14): [("stats", ("f", 2 * b + NCH))],
        (n + 1, 15): [("out_b", 2 * b + 1)],
        (n + 1, 16): [("norm", ("f", 2 * b + NCH))],
        (n + 1, 18): [("x_T", ("f", 2 * b + NCH))] + ([("stats", ("b", 2))] if b == 0 else []),
        (n + 1, 20): [("norm", ("b", 2))] if b == 0 else [],
        (n + 1, 21): [("affinity", 2 * b + NCH)],
        (n + 1, 23): [("top", 2 * b + NCH)] + ([("x_T", ("b", 2))] if b == 0 else []),
        (n + 1, 25): [("sum", 2 * b + NCH)], (n + 1, 29): [("gate_T", 2 * b + NCH)],
    })
SIDE.update({
    (6, 1): [("stats", ("f", 7))], (6, 3): [("norm", ("f", 7))],
    (6, 6): [("x_T", ("f", 7))], (6, 8): [("y_T", 5)],
    (6, 10): [("affinity", 7)], (6, 12): [("top", 7)], (6, 15): [("sum", 7)], (6, 20): [("gate_T", 7)],
    (7, 8): [("y_T", 6)],
    (8, 0): [("y_T", 7)],
})
SIDE_STEPS = sorted([k for k in SIDE if isinstance(k, int)]) + sorted([k for k in SIDE if not isinstance(k, int)])
SIDE_ITEM = ring_order([st for k in SIDE_STEPS for st in SIDE[k] if st[0] in (
    "heads_T", "proj", "x_T", "affinity", "gate_T", "y_T", "gram", "gram_k", "q_k", "energy", "mix_T", "v_mix",
    "v_all", "out_b")])
LN = ring_order([("a", c) for c in range(NCH)] + [st[1] for k in SIDE_STEPS for st in SIDE[k] if st[0] == "stats"])


def score_banks():
    first, wide = R * (NQ - BODY + HEAD_Q), R * (NQ - LEAD + 1)
    bank = {n: 4 + n % 3 for n in range(first - 3, wide)}
    for n in range(wide, R * NQ):
        bank[n] = 3 if n == wide else bank[n - 4]
    before = {n: max((m for m in bank if m < n and bank[m] == bank[n]), default=None) for n in bank}
    return bank, before


SCORE_BANK, TILE_BEFORE = score_banks()
TAIL_BANK, SIDE_BANK = 1, 7
DOWN_BANK = 6


def chunk_of(key):
    return key[1] % NCH


def hybrid_layer(nc, x, w_qkv, w_proj, b_proj, lam_q1, lam_k1, lam_q2, lam_k2, sub_w,
                 w_q, w_k, w_v, w_o, b_o, cent, e_bias, ws_up, ws_down, w_up, w_down, out):
    ctx = ExitStack()
    with ctx:
        used = {}

        def sb(name, shape, dt=F32, where=ctx):
            used[where] = used.get(where, 0) + int(np.prod(shape[1:])) * (2 if dt == BF16 else 4)
            return where.enter_context(nc.sbuf_tensor(name, shape, dt))

        def sem(name):
            return ctx.enter_context(nc.semaphore(name))

        X = sb("X", [P, NT, DIM])
        XC = sb("XC", [P, NT, DIM])
        SQ = sb("SQ", [P, NT, DIM])
        XT = sb("XT", [P, TOK])
        WUH = sb("WUH", [P, E * F], F32R); WUL = sb("WUL", [P, E * F], F32R)
        WDH = sb("WDH", [P, PAIRS * DIM], F32R); WDL = sb("WDL", [P, PAIRS * DIM], F32R)
        WSUH = sb("WSUH", [P, P], F32R); WSUL = sb("WSUL", [P, P], F32R)
        WSDH = sb("WSDH", [P, DIM], F32R); WSDL = sb("WSDL", [P, DIM], F32R)
        SEL = sb("SEL", [P, PAIRS * P], F32R)
        ident = sb("ident", [P, P]); identb = sb("identb", [P, P], BF16)
        WQKV = sb("WQKV", [P, 3, DIM]); WPRJ = sb("WPRJ", [P, DIM]); CENT = sb("CENT", [E, DIM])
        WT = sb("WT", [P, 4, DIM])
        CT = sb("CT", [P, E]); WVT = sb("WVT", [P, DIM])
        T8 = sb("T8", [P, HD_B]); H16 = sb("H16", [P, HEADS_B])
        BLK = sb("BLK", [P, DIM])
        WB = sb("WB", [P, 4, DIM])
        BPROJ = sb("BPROJ", [P, DIM]); BO = sb("BO", [P, DIM]); EBIAS = sb("EBIAS", [P, E])
        SUBW = sb("SUBW", [P, 2, VD])
        LAM = sb("LAM", [P, 4, HD_A]); lam_p = sb("lam_p", [P, 2, HD_A]); lam_s = sb("lam_s", [P, 2])
        ln_st = sb("ln_st", [P, 2, 4, 6]); ln_mv = sb("ln_mv", [P, 2, 4, 2]); ln_ve = sb("ln_ve", [P, 2, 4])
        ln_inv = sb("ln_inv", [P, 2, 4]); ln_tmp = sb("ln_tmp", [P, 2, 4])
        rms_r = sb("rms_r", [P, TB * GPB * 2])
        POWER = sb("POWER", [P, 1])
        top8 = sb("top8", [P, 4, TOPK]); wsum = sb("wsum", [P, 4]); wrec = sb("wrec", [P, 4])
        lam_e = sb("lam_e", [P, 2]); neg_lam = sb("neg_lam", [P, 1])

        VALL = XC[:].rearrange("p t c -> p (t c)").rearrange("p (g t v) -> p g t v", g=NG, t=TB)
        O = XT[:].rearrange("p (g t v) -> p g t v", g=NG, t=TB)

        kept = used[ctx]

        prep = ExitStack()
        RAWU = sb("RAWU", [P, E * F], where=prep); RAWD = sb("RAWD", [P, PAIRS * DIM], where=prep)
        PARTS = sb("PARTS", [P, 3, 2, TOK], BF16, where=prep)
        R1 = SQ[:, 0:2 * BANK // DIM, :].rearrange("p t c -> p (t c)").rearrange("p (j n) -> p j n", j=2)
        SELF = SQ
        RAWSU = sb("RAWSU", [P, P], where=prep); RAWSD = sb("RAWSD", [P, DIM], where=prep)
        ZEROS = sb("ZEROS", [P, SEQ], BF16, where=prep); ONES = sb("ONES", [P, SEQ], BF16, where=prep)
        prep.close()

        attn = ExitStack()
        PR = sb("PR", [P, PRING, R, BANK], where=attn)
        KB = sb("KB", [P, 2, R, SEQ], BF16, where=attn)
        QB = sb("QB", [P, 2, SEQ], BF16, where=attn)
        VG = sb("VG", [P, 2, TB, 2, STRIP], where=attn)
        OTS = sb("OTS", [P, 2, BANK], where=attn)
        SHP = sb("SHP", [P, 2, 3 * R * TB], BF16, where=attn)
        SHT = sb("SHT", [3 * R * TB, 2, P], BF16, where=attn)
        ZERO = sb("ZERO", [P, R * TB], where=attn)
        front = used[attn]
        QA = sb("QA", [P, 2, R, SEQ], BF16, where=attn)
        KA = sb("KA", [P, 2, SEQ], BF16, where=attn)
        NEGMAX = sb("NEGMAX", [P, 2, R * TB], where=attn); SHR = sb("SHR", [P, R * TB], where=attn)
        RD = sb("RD", [P, 4 * R], where=attn); TM = sb("TM", [P, 4 * R, VD], where=attn)
        attn.close()

        SI = sb("SI", [P, 3, BANK]); HF = sb("HF", [P, HPLACES, BANK])
        HH = sb("HH", [P, HPLACES, BANK], F32R); HL = sb("HL", [P, HPLACES, BANK], F32R)
        YS = sb("YS", [P, BANK])
        GRAM = sb("GRAM", [P, BATCH, DIM]); GK = sb("GK", [P, BATCH, DIM])
        QK = sb("QK", [P, DIM]); QKR = sb("QKR", [P, HEADS_B])
        EN = sb("EN", [P, HEADS_B]); en_m = sb("en_m", [P, 1]); en_s = sb("en_s", [P, 1]); en_r = sb("en_r", [P, 1])
        MIXT = sb("MIXT", [P, DIM]); MIX = sb("MIX", [P, DIM]); VMIX = sb("VMIX", [P, BATCH, DIM])
        VP = sb("VP", [P, BATCH, S0, S1]); RT = sb("RT", [P, BATCH, SEQ])
        sb("gap", [P, (front - (used[ctx] - kept)) // 4])
        XH = sb("XH", [P, TOK], F32R); XL = sb("XL", [P, TOK], F32R)
        CWT = sb("CWT", [P, 2, BANK], F32R)
        HSQ, CH = SQ[:, 0:TB, :], SQ[:, TB:TB + 4, :]
        AFF, BI, EX, BR = (SQ[:, j:j + 2, :].rearrange("p t c -> p (t c)").rearrange("p (t e) -> p t e", e=E)
                           for j in (TB + 4, TB + 6, 0, 2))
        rms_s, rms_sd, rms_t = (SQ[:, TB + 4 + j, :] for j in range(3))

        PS = ctx.enter_context(nc.psum_tensor("PS", [P, 8, BANK], F32))

        q_stack = nc.dram_tensor("q_stack", (NG, R, STRIP, SEQ), BF16, kind="Internal").ap()
        k_stack = nc.dram_tensor("k_stack", (NG, R, STRIP, SEQ), BF16, kind="Internal").ap()
        mixed_d = nc.dram_tensor("mixed_d", (BATCH, S0, HEADS_B, HD_B, S1), F32, kind="Internal").ap()
        shift_d = nc.dram_tensor("shift_d", (2, 3, R, SEQ), BF16, kind="Internal").ap()

        ld_x = [sem(f"ld_x{c}") for c in range(NCH)]
        ld_w, ld_mix, ld_exp, ld_b = (sem(n) for n in ("ld_w", "ld_mix", "ld_exp", "ld_b"))
        ld_up = sem("ld_up")
        ident_ok, identb_ok, const_ok = (sem(n) for n in ("ident_ok", "identb_ok", "const_ok"))
        a_full, a_free, d_full = sem("a_full"), sem("a_free"), sem("d_full")
        dve_step = sem("dve_step")
        pool_step = sem("pool_step")
        lam_in, lam_exp = sem("lam_in"), sem("lam_exp")
        qk_hi, qk_r1, qk_mid, qk_lo = (sem(n) for n in ("qk_hi", "qk_r1", "qk_mid", "qk_lo"))
        st_w = [sem(f"st_w{b}") for b in range(BATCH)]
        w_hi, w_lo = sem("w_hi"), sem("w_lo")
        xb_ok = sem("xb_ok")
        qa_ld = [sem(f"qa_ld{u}") for u in range(2)]
        kb_ld = [sem(f"kb_ld{u}") for u in range(2)]
        m_full, m_free, s_full, p_ready = (sem(n) for n in ("m_full", "m_free", "s_full", "p_ready"))
        av_done, o_evac, o_done, v_cp = (sem(n) for n in ("av_done", "o_evac", "o_done", "v_cp"))
        rd_ok, qa_zeroed, kb_zeroed = sem("rd_ok"), sem("qa_zeroed"), sem("kb_zeroed")
        sh_split, sh_w, sh_r = sem("sh_split"), sem("sh_w"), sem("sh_r")
        rms_sq, rms_var, rms_sd_ok, rms_r_ok, rms_step, heads_ok = (
            sem(n) for n in ("rms_sq", "rms_var", "rms_sd_ok", "rms_r_ok", "rms_step", "heads_ok"))
        side_full, side_free = sem("side_full"), sem("side_free")
        ln_var, ln_r_ok, ln_xn = sem("ln_var"), sem("ln_r_ok"), sem("ln_xn")
        bi_ok, top_ok, picked, wrec_ok, route_step = (sem(n) for n in ("bi_ok", "top_ok", "picked", "wrec_ok", "route_step"))
        x_biased = sem("x_biased")
        xh_ok, xl_ok = sem("xh_ok"), sem("xl_ok")
        ex_ok, ch_ok = sem("ex_ok"), sem("ch_ok")
        z_full, silu_ok, c_full, hf_ok = (sem(n) for n in ("z_full", "silu_ok", "c_full", "hf_ok"))
        hh_ok, hl_ok, down_ok = sem("hh_ok"), sem("hl_ok"), sem("down_ok")
        y_evac = sem("y_evac")
        blk_ok, en_in, en_exp, mix_in = (sem(n) for n in ("blk_ok", "en_in", "en_exp", "mix_in"))
        mix_w = [sem(f"mix_w{b}") for b in range(BATCH)]
        mix_r = [sem(f"mix_r{b}") for b in range(BATCH)]
        stored = sem("stored")

        block = ctx.enter_context(nc.Block())

        @block.sync
        def _(sp):
            x_rows = x.rearrange("b (n p) c -> p (b n) c", p=P)
            for c in range(NCH):
                sp.dma_start(X[:, 4 * c:4 * c + 4, :], x_rows[:, 4 * c:4 * c + 4, :]).then_inc(ld_x[c], 16)
                if c == 0:
                    sp.dma_start(WQKV[:], w_qkv.rearrange("(j p) c -> p j c", p=P)).then_inc(ld_w, 16)
                    sp.dma_start(WPRJ[:], w_proj).then_inc(ld_w, 16)

            sp.wait_ge(const_ok, 2)

            def fill_shift_rows(b):
                for stack, fill in ((q_stack, ZEROS), (k_stack, ONES)):
                    rows = stack[b * GPB:(b + 1) * GPB, :, SHIFT_ROW:STRIP, :].rearrange("g r s n -> (g r) (s n)")
                    sp.dma_start(rows, fill[:].unsqueeze(1).to_broadcast([P, 2, SEQ])).then_inc(st_w[b], 16)

            def write_parts(b, part):
                for j, (stack, slots) in enumerate(((q_stack, Q_SLOTS), (k_stack, K_SLOTS))):
                    src = PARTS[:, part, j, b * SEQ:(b + 1) * SEQ]
                    places = [c for c, a in enumerate(slots) if a == part]
                    for c in places:
                        rows = stack[b * GPB:(b + 1) * GPB, :, HD_A * c:HD_A * (c + 1), :].rearrange("g r d n -> (g r) d n")
                        sp.dma_start(rows, src).then_inc(st_w[b], 16)

            def write_stacks(b):
                n = 2 * (NCH // BATCH) * (b + 1)
                for part, made in enumerate((qk_hi, qk_mid, qk_lo)):
                    sp.wait_ge(made, n)
                    write_parts(b, part)

            fill_shift_rows(0)
            write_stacks(0)

            def load(stack, tile, u, g, there):
                if tile is QB or tile is KA:
                    src = stack[bass.ds(g, 1), :, :, :].rearrange("o r s n -> (o r s) n")
                    sp.dma_start(tile[:, u, :], src).then_inc(there, 16)
                    return
                for r in range(R):
                    src = stack[bass.ds(g, 1), r, :, :].rearrange("o s n -> (o s) n")
                    sp.dma_start(tile[STRIP * r:STRIP * (r + 1), u, r, :], src).then_inc(there, 16)

            sp.wait_ge(st_w[0], STACK_WRITES)
            sp.wait_ge(qa_zeroed, 1)
            load(q_stack, QA, 0, 0, qa_ld[0])
            load(k_stack, KA, 0, 0, qa_ld[0])
            fill_shift_rows(1)
            write_stacks(1)
            load(q_stack, QA, 1, 1, qa_ld[1])
            load(k_stack, KA, 1, 1, qa_ld[1])
            sp.wait_ge(st_w[1], STACK_WRITES)
            load(q_stack, QB, 0, 0, sh_w)
            sp.wait_ge(kb_zeroed, 1)
            load(k_stack, KB, 0, 0, kb_ld[0])

            def shift_rows(i, s):
                u = s % 2
                sp.wait_ge(m_free, i * ITEMS_PER_BODY + (ITEM["shift", s] + 1))
                sp.dma_start(shift_d[u].rearrange("a r (t n) -> (a r t) n", n=P), SHT[:, u, :]).then_inc(sh_w, 16)
                sp.wait_ge(sh_w, i * 64 + 32 * (s + 1))
                for r in range(R):
                    lo = STRIP * r + SHIFT_ROW
                    sp.dma_start(QB[lo:lo + 3, u, :], shift_d[u, :, r, :]).then_inc(sh_r, 16)

            def group_loads(i, s, more=True):
                u = s % 2
                if s >= 2:
                    sp.wait_ge(s_full, i * (R * BODY) + R * QPG * (s - 1))
                if s:
                    load(q_stack, QB, u, i * 2 + s, sh_w)
                    load(k_stack, KB, u, i * 2 + s, kb_ld[u])
                shift_rows(i, s)
                if more:
                    sp.wait_ge(m_full, i * ITEMS_PER_BODY + (ITEM["max", QPG * s + QPG - 1, 1] + 1))
                    load(q_stack, QA, u, i * 2 + (s + 2), qa_ld[u])
                    load(k_stack, KA, u, i * 2 + (s + 2), qa_ld[u])

            group_loads(0, 0)
            group_loads(0, 1)
            with sp.Fori(0, NG // 2 - 2) as i:
                for s in (2, 3):
                    group_loads(i, s)
            for s in (NG - 2, NG - 1):
                group_loads(0, s, False)
            for b in range(BATCH):
                sp.wait_ge(side_free, SIDE_ITEM["v_all", 2 * b + 1] + 1)
                sp.dma_start(mixed_d[b].rearrange("i a d j -> (a d) i j"), VP[:, b, :, :]).then_inc(mix_w[b], 16)
                sp.wait_ge(mix_w[b], 16)
                for i in range(S0):
                    sp.dma_start(RT[HD_B * i:HD_B * (i + 1), b, :].rearrange("d (a j) -> d a j", j=S1),
                                 mixed_d[b, i].rearrange("a d j -> d a j")).then_inc(mix_r[b], 16)
            rows_out = out.rearrange("b (n p) c -> p (b n) c", p=P)
            for c in range(NCH):
                sp.wait_ge(side_free, SIDE_ITEM["y_T", NCH + c] + 1)
                sp.dma_start(rows_out[:, 4 * c:4 * c + 4, :], X[:, 4 * c:4 * c + 4, :]).then_inc(stored, 16)
            sp.wait_ge(stored, 16 * NCH)

        @block.gpsimd
        def _(pool):
            nsteps = [0]

            def link(ins):
                nsteps[0] += 1
                ins.then_inc(pool_step, 1)
                pool.wait_ge(pool_step, nsteps[0])

            link(nc.gpsimd.memset(ident[:], 0.0))
            nc.gpsimd.affine_select(out=ident[:], in_=ident[:], compare_op=ALU.not_equal, fill=1.0, base=0,
                                    pattern=[[-1, P]], channel_multiplier=1).then_inc(ident_ok, 1)
            pool.wait_ge(ident_ok, 1)
            nc.gpsimd.tensor_copy(identb[:], ident[:]).then_inc(identb_ok, 1)
            nc.gpsimd.memset(ZEROS[:], 0.0).then_inc(const_ok, 1)
            nc.gpsimd.memset(ONES[:], 1.0).then_inc(const_ok, 1)
            link(nc.gpsimd.memset(POWER[:], -0.5))
            link(nc.gpsimd.memset(RAWSU[:], 0.0))
            nc.gpsimd.memset(RAWSD[:], 0.0).then_inc(const_ok, 1)

            def newton(r, t, v, done):
                link(nc.gpsimd.tensor_tensor(t, r, r, op=ALU.mult))
                link(nc.gpsimd.tensor_tensor(t, t, v, op=ALU.mult))
                link(nc.gpsimd.tensor_scalar(t, t, -0.5, 1.5, ALU.mult, ALU.add))
                nc.gpsimd.tensor_tensor(r, r, t, op=ALU.mult).then_inc(done, 1)

            def root_inverse(r, t, v, done):
                link(nc.gpsimd.tensor_tensor(r, v, POWER[:].to_broadcast(list(v.shape)), op=ALU.pow))
                newton(r, t, v, done)

            def root_of(key):
                n = LN[key]
                pool.wait_ge(ln_var, n + 1)
                root_inverse(ln_inv[:, n % 2, :], ln_tmp[:, n % 2, :], ln_ve[:, n % 2, :], ln_r_ok)

            for c in range(NCH):
                root_of(("a", c))
            pool.wait_ge(ld_mix, 16 * 9)
            pool.wait_ge(ln_xn, NCH)
            nc.gpsimd.tensor_tensor(X[:], X[:], BPROJ[:].unsqueeze(1).to_broadcast([P, NT, DIM]), op=ALU.add).then_inc(xb_ok, 1)

            def low_weights(n, dst, src, hi):
                pool.wait_ge(w_hi, n + 1)
                nc.gpsimd.tensor_tensor(dst[:], src[:], hi[:].bitcast(F32), op=ALU.subtract).then_inc(w_lo, 1)

            low_weights(0, WDL, RAWD, WDH)
            low_weights(1, WUL, RAWU, WUH)
            for b in range(BATCH):
                pool.wait_ge(st_w[b], STACK_WRITES)
            nc.gpsimd.memset(KB[:].bitcast(F32), 0.0).then_inc(kb_zeroed, 1)
            link(nc.gpsimd.memset(VG[:], 0.0))
            link(nc.gpsimd.memset(VG[:, :, :, :, VD:VD + 1], 1.0))

            def values(u, g):
                pool.wait_ge(a_free, A_ITEM["va", NCH - 1] + 1)
                nc.gpsimd.tensor_copy(
                    VG[:, u, :, :, 0:VD],
                    VALL[:, bass.ds(g, 1), :, :].rearrange("p o t (h d) -> p (o t) h d", d=VD)).then_inc(v_cp, 1)

            def shift_parts(i, s):
                pool.wait_ge(m_free, i * ITEMS_PER_BODY + (ITEM["max", QPG * s + QPG - 1, 1] + 1))
                u, w = s % 2, R * TB
                nc.gpsimd.tensor_tensor(SHP[:, u, 0:w], NEGMAX[:, u, :], ZERO[:], op=ALU.add).then_inc(sh_split, 1)
                pool.wait_ge(sh_split, i * 8 + (4 * s + 1))
                nc.gpsimd.tensor_tensor(SHR[:], NEGMAX[:, u, :], SHP[:, u, 0:w], op=ALU.subtract).then_inc(sh_split, 1)
                pool.wait_ge(sh_split, i * 8 + (4 * s + 2))
                nc.gpsimd.tensor_tensor(SHP[:, u, w:2 * w], SHR[:], ZERO[:], op=ALU.add).then_inc(sh_split, 1)
                pool.wait_ge(sh_split, i * 8 + (4 * s + 3))
                nc.gpsimd.tensor_tensor(SHP[:, u, 2 * w:3 * w], SHR[:], SHP[:, u, w:2 * w], op=ALU.subtract).then_inc(sh_split, 1)
                pool.wait_ge(sh_split, i * 8 + (4 * s + 4))

            values(0, 0)
            values(1, 1)
            for n, (dst, src, hi) in enumerate(((WSUL, RAWSU, WSUH), (WSDL, RAWSD, WSDH))):
                low_weights(n + 2, dst, src, hi)
            pool.wait_ge(w_lo, 4)
            link(nc.gpsimd.memset(ZERO[:], 0.0))
            shift_parts(0, 0)
            pool.wait_ge(qk_lo, 2 * NCH)
            sel = SELF[:].rearrange("p t c -> p (t c)").rearrange("p (j e f) -> p j e f", e=2, f=F)
            half = PAIRS // 2 * P
            for h in range(2):
                link(nc.gpsimd.memset(SELF[:], 0.0))
                for base in (0, -E):
                    link(nc.gpsimd.affine_select(out=sel, in_=sel, compare_op=ALU.not_equal, fill=1.0,
                                                 base=base - h * PAIRS, pattern=[[-2, PAIRS // 2], [-1, 2], [0, F]],
                                                 channel_multiplier=1))
                link(nc.gpsimd.tensor_copy(SEL[:, h * half:(h + 1) * half], SELF[:].rearrange("p t c -> p (t c)")))
            with pool.Fori(0, LOOPS) as i:
                for s in (1, 2):
                    shift_parts(i, s)
                    pool.wait_ge(av_done, i * BODY + QPG * s)
                    values((s + 1) % 2, i * 2 + (s + 1))
            for where in SIDE_STEPS:
                if where == NQ - 19:
                    shift_parts(0, NG - 1)
                for stage, arg in SIDE[where]:
                    if stage == "rms_scale":
                        heads = O[:, arg * GPB:(arg + 1) * GPB, :, :]
                        flat = heads.rearrange("p g t (h v) -> p (g t h) v", v=VD)
                        pool.wait_ge(rms_r_ok, arg + 1)
                        newton(rms_r[:], rms_t, rms_s, rms_step)
                        pool.wait_ge(v_cp, NG)
                        pool.wait_ge(rms_step, 2 * arg + 1)
                        nc.gpsimd.tensor_tensor(flat, flat, rms_r[:].unsqueeze(2).to_broadcast([P, TB * GPB * 2, VD]),
                                                op=ALU.mult).then_inc(rms_step, 1)
                        pool.wait_ge(rms_step, 2 * arg + 2)
                        nc.gpsimd.tensor_tensor(
                            XC[:, arg * TB:(arg + 1) * TB, :].rearrange("p t (g v) -> p t g v", v=2 * VD),
                            heads.rearrange("p g t v -> p t g v"),
                            SUBW[:].rearrange("p j v -> p (j v)").unsqueeze(1).unsqueeze(1).to_broadcast([P, TB, GPB, 2 * VD]),
                            op=ALU.mult).then_inc(heads_ok, 1)
                    elif stage == "x_T" and arg[0] == "f":
                        cols = slice(chunk_of(arg) * BANK, (chunk_of(arg) + 1) * BANK)
                        pool.wait_ge(xh_ok, arg[1] + 1)
                        nc.gpsimd.tensor_tensor(XL[:, cols], XT[:, cols], XH[:, cols].bitcast(F32), op=ALU.subtract).then_inc(xl_ok, 1)
                    elif stage == "stats":
                        root_of(arg)
                    elif stage == "affinity":
                        pool.wait_ge(side_free, SIDE_ITEM["affinity", arg] + 1)
                        nc.gpsimd.tensor_tensor(BI, AFF, EBIAS[:].unsqueeze(1).to_broadcast([P, 4, E]), op=ALU.add).then_inc(bi_ok, 1)
                    elif stage == "top":
                        pool.wait_ge(top_ok, arg + 1)
                        pool.wait_ge(ex_ok, arg + 1)
                        nc.gpsimd.tensor_tensor(EX, EX, BR, op=ALU.mult).then_inc(picked, 1)
                    elif stage == "sum":
                        pool.wait_ge(wrec_ok, arg + 1)
                        nc.gpsimd.tensor_tensor(EX, EX, wrec[:].unsqueeze(2).to_broadcast([P, 4, E]), op=ALU.mult).then_inc(route_step, 1)
                        pool.wait_ge(route_step, 2 * arg + 1)
                        nc.gpsimd.tensor_copy(CH[:, :, 0:E].bitcast(F32R), EX).then_inc(route_step, 1)
                        pool.wait_ge(route_step, 2 * arg + 2)
                        nc.gpsimd.tensor_tensor(CH[:, :, E:2 * E], EX, CH[:, :, 0:E], op=ALU.subtract).then_inc(ch_ok, 1)
                    elif stage == "x_T":
                        tiles = X[:, 4 * arg[1]:4 * arg[1] + 4, :]
                        pool.wait_ge(ln_xn, LN[arg] + 1)
                        nc.gpsimd.tensor_tensor(tiles, tiles, BO[:].unsqueeze(1).to_broadcast([P, 4, DIM]), op=ALU.add).then_inc(x_biased, 1)

        @block.scalar
        def _(act):
            def evac(key, dst, src):
                n = A_ITEM[key]
                act.wait_ge(a_full, n + 1)
                nc.scalar.activation(dst, src(n % 4), ACT.Copy).then_inc(a_free, 1)

            evac("wT", WT[:].rearrange("p j c -> p (j c)"), lambda n: PS[:, n, :])

            def load_up(part):
                es = slice(part * E // 4, (part + 1) * E // 4)
                act.dma_start(RAWU[:].rearrange("d (e f) -> d e f", f=F)[:, es, :],
                              w_up[es, :, :].rearrange("e d f -> d e f")).then_inc(ld_up, 16)

            act.dma_start(RAWD[:].rearrange("p (j d) -> p j d", d=DIM),
                          w_down.rearrange("(j e) f d -> (e f) j d", e=2)).then_inc(ld_exp, 16)
            load_up(0)
            load_up(1)
            for j, v in enumerate((lam_q1, lam_k1, lam_q2, lam_k2)):
                act.dma_start(LAM[:, j, :], v.partition_broadcast(P)).then_inc(ld_mix, 16)
            act.dma_start(BPROJ[:], b_proj.partition_broadcast(P)).then_inc(ld_mix, 16)
            act.dma_start(BO[:], b_o.partition_broadcast(P)).then_inc(ld_mix, 16)
            act.dma_start(EBIAS[:], e_bias.partition_broadcast(P)).then_inc(ld_mix, 16)
            for j in range(2):
                act.dma_start(SUBW[:, j, :], sub_w.partition_broadcast(P)).then_inc(ld_mix, 16)

            def high_and_middle(c):
                cols = slice(c * BANK, (c + 1) * BANK)
                for j in range(2):
                    n = D_ITEM["qk", j, c]
                    act.wait_ge(d_full, n + 1)
                    nc.scalar.activation(PARTS[:, 0, j, cols], PS[:, 4 + n % 4, :], ACT.Copy).then_inc(qk_hi, 1)
                for j in range(2):
                    n = D_ITEM["qk", j, c]
                    act.wait_ge(qk_r1, n + 1)
                    nc.scalar.activation(PARTS[:, 1, j, cols], R1[:, n % 2, :], ACT.Copy).then_inc(qk_mid, 1)

            for c in range(NCH):
                evac(("xT", c), XT[:, c * BANK:(c + 1) * BANK], lambda n: PS[:, n, :])
                if c:
                    high_and_middle(c - 1)
            high_and_middle(NCH - 1)
            act.dma_start(CENT[:], cent).then_inc(ld_b, 16)
            for j, w in enumerate((w_q, w_k, w_v, w_o)):
                act.dma_start(WB[:, j, :], w).then_inc(ld_b, 16)
            act.wait_ge(const_ok, 3)
            act.dma_start(RAWSU[:, 0:F], ws_up).then_inc(ld_exp, 16)
            act.dma_start(RAWSD[0:F, :], ws_down).then_inc(ld_exp, 16)
            for c in range(NCH):
                b, h = c // 2, c % 2
                evac(("va", c), VALL[:, b * GPB:(b + 1) * GPB, h * 4:(h + 1) * 4, :].rearrange("p g t v -> p t g v"),
                     lambda n: PS[:, n, :].rearrange("p (t g v) -> p t g v", t=4, g=GPB))
            n = A_ITEM["centT"]
            act.wait_ge(a_full, n + 1)
            nc.scalar.activation(CT[:], PS[:, n % 4, 0:E], ACT.Copy)
            nc.scalar.activation(WVT[:], PS[:, n % 4, E:E + DIM], ACT.Copy).then_inc(a_free, 1)
            act.wait_ge(qa_ld[0], 16 * (R + 1))
            load_up(2)
            load_up(3)
            act.wait_ge(ld_exp, 48)
            for n, (dst, src) in enumerate(((WDH, RAWD), (WUH, RAWU), (WSUH, RAWSU), (WSDH, RAWSD))):
                if n == 1:
                    act.wait_ge(ld_up, 16 * 4)
                nc.scalar.activation(dst[:], src[:], ACT.Copy).then_inc(w_hi, 1)
            act.wait_ge(lam_in, 1)
            nc.scalar.activation(lam_e[:], lam_s[:], ACT.Exp).then_inc(lam_exp, 1)
            act.wait_ge(w_lo, 4)
            for b in range(BATCH):
                act.wait_ge(st_w[b], STACK_WRITES)

            def exp_quad(i, s):
                g = i * BODY + s
                if s >= HEAD_Q:
                    act.wait_ge(av_done, g - (PRING - 1))
                for r in range(R):
                    n = R * s + r
                    act.wait_ge(s_full, g * R + (r + 1))
                    nc.scalar.activation(PR[:, s % PRING, r, :], PS[:, SCORE_BANK.get(n, 4 + n % 3), :], ACT.Exp, scale=SCALE_A).then_inc(p_ready, 1)
                    if r == 0 and s >= 9 and (s - 9) % TB == 0:
                        evac_out(i, s)

            def evac_out(i, s):
                g, half = (s - 9) // QPG, (s - 9) // TB % 2
                act.wait_ge(av_done, i * BODY + (s - 1))
                before = ITEM["out", g - 1, half] + 1 if g else ITEM["out", g + 1, half] + 1 - ITEMS_PER_BODY
                assert before > 0
                act.wait_ge(m_full, i * ITEMS_PER_BODY + before)
                nc.scalar.activation(OTS[:, half, :], PS[:, 7, :], ACT.Copy).then_inc(o_evac, 1)

            def side_evac(item, dst, src, func=ACT.Copy):
                act.wait_ge(side_full, SIDE_ITEM[item] + 1)
                nc.scalar.activation(dst, src, func).then_inc(side_free, 1)

            def side(where):
                bank = TAIL_BANK if isinstance(where, int) else SIDE_BANK
                for item in SIDE.get(where, ()):
                    stage, arg = item
                    if stage == "rms_squares":
                        act.wait_ge(o_done, 2 * GPB * (arg + 1) + 1)
                        if arg:
                            act.wait_ge(ch_ok, NCH // 2)
                        nc.scalar.activation(HSQ.rearrange("p t c -> p (t c)"),
                                             O[:, arg * GPB:(arg + 1) * GPB, :, :].rearrange("p g t v -> p (g t v)"),
                                             ACT.Square).then_inc(rms_sq, 1)
                    elif stage == "rms_root":
                        act.wait_ge(rms_var, arg + 1)
                        nc.scalar.activation(rms_sd, rms_s, ACT.Sqrt).then_inc(rms_sd_ok, 1)
                    elif stage == "heads_T":
                        side_evac(item, XT[:, arg * BANK:(arg + 1) * BANK], PS[:, bank, :])
                    elif stage == "x_T":
                        cols = slice(chunk_of(arg) * BANK, (chunk_of(arg) + 1) * BANK)
                        act.wait_ge(side_full, SIDE_ITEM[item] + 1)
                        if arg[0] == "b" or arg[1] >= NCH:
                            act.wait_ge(xl_ok, arg[1] % NCH + 1)
                        if arg[0] == "b":
                            nc.scalar.activation(XT[:, cols], PS[:, bank, :], ACT.Copy).then_inc(side_free, 1)
                        else:
                            nc.scalar.activation(XT[:, cols], PS[:, bank, :], ACT.Copy)
                            nc.scalar.activation(XH[:, cols], PS[:, bank, :], ACT.Copy).then_inc(xh_ok, 1)
                            act.wait_ge(xh_ok, arg[1] + 1)
                            act.sem_inc(side_free, 1)
                    elif stage == "affinity":
                        side_evac(item, AFF, PS[:, bank, 0:4 * E].rearrange("p (t e) -> p t e", e=E))
                        act.wait_ge(side_free, SIDE_ITEM[item] + 1)
                        nc.scalar.activation(EX, AFF, ACT.Sigmoid).then_inc(ex_ok, 1)
                    elif stage == "gate_T":
                        side_evac(item, CWT[:, arg % 2, :], PS[:, bank, :])
                    elif stage == "soft_exp":
                        act.wait_ge(en_in, arg + 1)
                        nc.scalar.activation(EN[:], EN[:], ACT.Exp, scale=SCALE_B).then_inc(en_exp, 1)
                    elif stage == "v_all":
                        b, h = divmod(arg, 2)
                        side_evac(item, VP[:, b, :, h * (S1 // 2):(h + 1) * (S1 // 2)],
                                  PS[:, bank, :].rearrange("p (j i) -> p i j", i=S0))

            for s in range(HEAD_Q):
                exp_quad(0, s)
            with act.Fori(0, LOOPS) as i:
                for s in range(HEAD_Q, HEAD_Q + BODY):
                    exp_quad(i, s)
            for s in range(NQ - BODY + HEAD_Q, NQ):
                exp_quad(0, s)
                side(s)
            evac_out(0, NQ + 1)

            def high(g):
                n, j = divmod(g, UNITS)
                if g >= HPLACES:
                    act.wait_ge(down_ok, g - HPLACES + 1)
                if j < PAIRS:
                    act.wait_ge(hf_ok, n * PAIRS + j + 1)
                else:
                    act.wait_ge(silu_ok, g + 1)
                nc.scalar.activation(HH[:, g % HPLACES, :], HF[:, g % HPLACES, :], ACT.Copy).then_inc(hh_ok, 1)

            def chunk_sum(n):
                act.wait_ge(down_ok, (n + 1) * UNITS)
                nc.scalar.activation(YS[:], PS[:, DOWN_BANK, :], ACT.Copy).then_inc(y_evac, 1)

            for n in range(2 * NCH):
                for j in range(UNITS):
                    g = n * UNITS + j
                    if n and j == LAG:
                        chunk_sum(n - 1)
                    act.wait_ge(z_full, g + 1)
                    if j < PAIRS and g >= 3 and j != 2:
                        act.wait_ge(hf_ok, n * PAIRS + j - 2 if j >= 3 else (n - 1) * PAIRS + 31 + j)
                    if j == PAIRS:
                        act.wait_ge(hl_ok, g - HPLACES + 1)
                        act.wait_ge(hh_ok, g - HPLACES + 1)
                    nc.scalar.activation(SI[:, j % 3, :] if j < PAIRS else HF[:, g % HPLACES, :], PS[:, j % 3, :], ACT.Silu).then_inc(silu_ok, 1)
                    if g:
                        high(g - 1)
                    side((n, j))
            high(2 * NCH * UNITS - 1)
            chunk_sum(2 * NCH - 1)
            side((2 * NCH, 0))

        @block.vector
        def _(dve):
            nsteps = [0]

            def link(ins):
                nsteps[0] += 1
                ins.then_inc(dve_step, 1)
                dve.wait_ge(dve_step, nsteps[0])

            def stats(key):
                n, c = LN[key], chunk_of(key)
                for t in range(4):
                    last = nc.vector.bn_stats(ln_st[:, n % 2, t, :], X[:, 4 * c + t, :])
                link(last)
                for t in range(4):
                    last = nc.vector.bn_aggr(ln_mv[:, n % 2, t, :], ln_st[:, n % 2, t, :])
                link(last)
                nc.vector.tensor_scalar(ln_ve[:, n % 2, :], ln_mv[:, n % 2, :, 1], LN_EPS, None, ALU.add).then_inc(ln_var, 1)

            def norm(key):
                n, c = LN[key], chunk_of(key)
                dve.wait_ge(ln_r_ok, n + 1)
                for t in range(4):
                    last = nc.vector.tensor_scalar(XC[:, 4 * c + t, :], X[:, 4 * c + t, :], ln_mv[:, n % 2, t, 0:1],
                                                   ln_inv[:, n % 2, t:t + 1], ALU.subtract, ALU.mult)
                last.then_inc(ln_xn, 1)

            def rest_and_low(c):
                cols = slice(c * BANK, (c + 1) * BANK)
                for j in range(2):
                    n = D_ITEM["qk", j, c]
                    dve.wait_ge(qk_hi, n + 1)
                    nc.vector.tensor_tensor(R1[:, n % 2, :], PS[:, 4 + n % 4, :], PARTS[:, 0, j, cols], op=ALU.subtract).then_inc(qk_r1, 1)
                for j in range(2):
                    n = D_ITEM["qk", j, c]
                    dve.wait_ge(qk_r1, n + 1)
                    dve.wait_ge(qk_mid, n + 1)
                    nc.vector.tensor_tensor(PARTS[:, 2, j, cols], R1[:, n % 2, :], PARTS[:, 1, j, cols], op=ALU.subtract).then_inc(qk_lo, 1)
                dve.wait_ge(qk_lo, 2 * (c + 1))

            nc.vector.memset(QA[:].bitcast(F32), 0.0).then_inc(qa_zeroed, 1)
            for c in range(NCH):
                dve.wait_ge(ld_x[c], 16)
                stats(("a", c))
                if c:
                    norm(("a", c - 1))
            norm(("a", NCH - 1))
            for c in range(NCH):
                rest_and_low(c)
            nc.vector.memset(TM[:], 0.0).then_inc(o_done, 1)
            dve.wait_ge(ld_mix, 16 * 9)
            for j in range(2):
                link(nc.vector.tensor_tensor(lam_p[:, j, :], LAM[:, 2 * j, :], LAM[:, 2 * j + 1, :], op=ALU.mult))
            nc.vector.tensor_reduce(lam_s[:], lam_p[:], axis=AX_X, op=ALU.add).then_inc(lam_in, 1)
            link(nc.vector.tensor_scalar(SUBW[:], SUBW[:], 1.0 - LAMBDA_INIT, None, ALU.mult))
            dve.wait_ge(ident_ok, 1)
            link(nc.vector.tensor_reduce(T8[:], ident[:].rearrange("p (a d) -> p d a", d=HD_B), axis=AX_X, op=ALU.add))
            link(nc.vector.tensor_reduce(H16[:], ident[:].rearrange("p (a d) -> p a d", d=HD_B), axis=AX_X, op=ALU.add))
            nc.vector.tensor_copy(BLK[:].rearrange("p (a d) -> p a d", d=HD_B),
                                  H16[:].unsqueeze(2).to_broadcast([P, HEADS_B, HD_B])).then_inc(blk_ok, 1)
            def slot(it):
                return 2 * (it % 2)

            def max_quad(i, s):
                at = i * ITEMS_PER_BODY
                for key in quad_items(s):
                    it = ITEM[key]
                    e = slot(it)
                    dve.wait_ge(m_full, at + (it + 1))
                    if key[0] == "max":
                        ga, a = key[1] // QPG, 2 * (key[1] % QPG) + key[2]
                        if a == 0 and (ga >= 2):
                            dve.wait_ge(sh_split, i * 8 + 4 * (ga - 1))
                        nc.vector.tensor_reduce(NEGMAX[:, ga % 2, a:a + 1], PS[:, e:e + 2, :].rearrange("p b n -> p (b n)"),
                                                axis=AX_X, op=ALU.max, negate=True).then_inc(m_free, 1)
                    elif key[0] == "shift":
                        ga = key[1]
                        if ga >= 2:
                            dve.wait_ge(sh_w, i * 64 + 32 * (ga - 1))
                        nc.vector.tensor_copy(SHT[:, ga % 2, :], PS[0:3 * R * TB, e, 0:P // 2].bitcast(BF16)).then_inc(m_free, 1)
                    else:
                        gg, half = key[1], key[2]
                        n = 2 * gg + half
                        rows = PS[:, e, :].rearrange("p (m v) -> p m v", v=STRIP)
                        dve.wait_ge(o_done, i * 4 + (n + 1))
                        ob = i * 8 + 2 * n
                        nc.vector.reciprocal(RD[:], rows[:, :, VD]).then_inc(rd_ok, 1)
                        dve.wait_ge(rd_ok, ob + 1)
                        second = RD[:].rearrange("p (m s) -> p m s", s=2)[:, :, 1]
                        nc.vector.tensor_scalar(second, second, neg_lam[:], None, ALU.mult).then_inc(rd_ok, 1)
                        dve.wait_ge(rd_ok, ob + 2)
                        nc.vector.tensor_tensor(TM[:], rows[:, :, 0:VD], RD[:].unsqueeze(2).to_broadcast([P, 4 * R, VD]),
                                                op=ALU.mult).then_inc(m_free, 1)
                        dve.wait_ge(m_free, at + (it + 1))
                        tm = TM[:].rearrange("p (t h s) v -> p t h s v", h=2, s=2)
                        dst = O[:, bass.ds(i * 2 + gg, 1), 4 * half:4 * half + 4, :]
                        nc.vector.tensor_tensor(dst.rearrange("p o t (h v) -> p (o t) h v", v=VD),
                                                tm[:, :, :, 0, :], tm[:, :, :, 1, :], op=ALU.add).then_inc(o_done, 1)

            for s in range(-LEAD, HEAD_Q):
                if s == 0:
                    dve.wait_ge(lam_exp, 1)
                    link(nc.vector.tensor_tensor(neg_lam[:], lam_e[:, 1:2], lam_e[:, 0:1], op=ALU.subtract))
                    link(nc.vector.tensor_scalar(neg_lam[:], neg_lam[:], -LAMBDA_INIT, None, ALU.add))
                max_quad(0, s)
            with dve.Fori(0, LOOPS) as i:
                for s in range(HEAD_Q, HEAD_Q + BODY):
                    max_quad(i, s)
            def low(g):
                if g >= HPLACES:
                    dve.wait_ge(down_ok, g - HPLACES + 1)
                dve.wait_ge(hh_ok, g + 1)
                place = g % HPLACES
                nc.vector.tensor_tensor(HL[:, place, :], HF[:, place, :], HH[:, place, :].bitcast(F32), op=ALU.subtract).then_inc(hl_ok, 1)

            def side(where):
                bank = TAIL_BANK if isinstance(where, int) else SIDE_BANK
                for item in SIDE.get(where, ()):
                    stage, arg = item
                    if item in SIDE_ITEM and stage in ("proj", "out_b", "y_T", "gram", "gram_k", "q_k", "energy", "mix_T", "v_mix"):
                        dve.wait_ge(side_full, SIDE_ITEM[item] + 1)
                    if stage == "rms_sums":
                        dve.wait_ge(rms_sq, arg + 1)
                        link(nc.vector.tensor_reduce(rms_s, HSQ.rearrange("p t c -> p (t c)").rearrange("p (m v) -> p m v", v=VD),
                                                     axis=AX_X, op=ALU.add))
                        nc.vector.tensor_scalar(rms_s, rms_s, 1.0 / VD, EPS_A, ALU.mult, ALU.add).then_inc(rms_var, 1)
                    elif stage == "rms_scale":
                        dve.wait_ge(rms_sd_ok, arg + 1)
                        nc.vector.reciprocal(rms_r[:], rms_sd).then_inc(rms_r_ok, 1)
                    elif stage in ("proj", "out_b"):
                        tiles = X[:, 4 * arg:4 * arg + 4, :].rearrange("p t c -> p (t c)")
                        if stage == "proj":
                            dve.wait_ge(xb_ok, 1)
                        else:
                            dve.wait_ge(x_biased, arg + 1)
                        nc.vector.tensor_tensor(tiles, tiles, PS[:, bank, :], op=ALU.add).then_inc(side_free, 1)
                    elif stage == "y_T":
                        tiles = X[:, 4 * (arg % NCH):4 * (arg % NCH) + 4, :].rearrange("p t c -> p (t c)")
                        nc.vector.tensor_tensor(tiles, tiles, PS[:, bank, :], op=ALU.add).then_inc(side_free, 1)
                    elif stage == "stats":
                        c = chunk_of(arg)
                        before = {"f": ("proj", c) if arg[1] < NCH else ("out_b", c), "b": ("y_T", c)}[arg[0]]
                        dve.wait_ge(side_free, SIDE_ITEM[before] + 1)
                        stats(arg)
                    elif stage == "norm":
                        norm(arg)
                    elif stage == "top":
                        dve.wait_ge(bi_ok, arg + 1)
                        for t in range(4):
                            last = nc.vector.max(top8[:, t, :], BI[:, t, :])
                        link(last)
                        for t in range(4):
                            last = nc.vector.match_replace(BR[:, t, :], top8[:, t, :], BI[:, t, :], -3.0e38)
                        link(last)
                        nc.vector.tensor_tensor(BR, BR, BI, op=ALU.not_equal).then_inc(top_ok, 1)
                    elif stage == "sum":
                        dve.wait_ge(picked, arg + 1)
                        link(nc.vector.tensor_reduce(wsum[:], EX, axis=AX_X, op=ALU.add))
                        link(nc.vector.tensor_scalar(wsum[:], wsum[:], 1e-8, None, ALU.add))
                        nc.vector.reciprocal(wrec[:], wsum[:]).then_inc(wrec_ok, 1)
                    elif stage == "gram":
                        nc.vector.tensor_copy(GRAM[:, arg, :], PS[:, bank, 0:DIM]).then_inc(side_free, 1)
                    elif stage == "gram_k":
                        nc.vector.tensor_copy(GK[:, arg, :], PS[:, bank, 0:DIM]).then_inc(side_free, 1)
                    elif stage == "q_k":
                        by_head = "p (h d) -> p h d"
                        link(nc.vector.tensor_tensor(QK[:].rearrange(by_head, d=HD_B), PS[:, bank, 0:DIM].rearrange(by_head, d=HD_B),
                                                     T8[:].unsqueeze(1).to_broadcast([P, HEADS_B, HD_B]), op=ALU.mult))
                        nc.vector.tensor_reduce(QKR[:], QK[:].rearrange(by_head, d=HD_B), axis=AX_X, op=ALU.add).then_inc(side_free, 1)
                    elif stage == "energy":
                        link(nc.vector.tensor_reduce(en_m[:], PS[:, bank, 0:HEADS_B], axis=AX_X, op=ALU.max))
                        nc.vector.tensor_scalar(EN[:], PS[:, bank, 0:HEADS_B], en_m[:], None, ALU.subtract).then_inc(side_free, 1)
                        dve.wait_ge(side_free, SIDE_ITEM[item] + 1)
                        dve.sem_inc(en_in, 1)
                    elif stage == "soft_mix":
                        dve.wait_ge(en_exp, arg + 1)
                        link(nc.vector.tensor_reduce(en_s[:], EN[:], axis=AX_X, op=ALU.add))
                        link(nc.vector.reciprocal(en_r[:], en_s[:]))
                        link(nc.vector.tensor_scalar(EN[:], EN[:], en_r[:], None, ALU.mult))
                        nc.vector.tensor_tensor(MIXT[:].rearrange("p (h d) -> p h d", d=HD_B),
                                                EN[:].unsqueeze(2).to_broadcast([P, HEADS_B, HD_B]),
                                                T8[:].unsqueeze(1).to_broadcast([P, HEADS_B, HD_B]), op=ALU.mult).then_inc(mix_in, 1)
                    elif stage == "mix_T":
                        nc.vector.tensor_copy(MIX[:], PS[:, bank, 0:DIM]).then_inc(side_free, 1)
                    elif stage == "v_mix":
                        nc.vector.tensor_copy(VMIX[:, arg, :], PS[:, bank, 0:DIM]).then_inc(side_free, 1)

            for s in range(NQ - BODY + HEAD_Q, NQ + 4):
                max_quad(0, s)
                side(s)
            dve.wait_ge(o_done, 2 * NG + 1)
            for n in range(2 * NCH):
                for j in range(UNITS):
                    g, h = n * UNITS + j, n * PAIRS + j
                    if j < PAIRS:
                        dve.wait_ge(silu_ok, g + 1)
                        dve.wait_ge(c_full, h + 1)
                        if g >= HPLACES:
                            dve.wait_ge(hh_ok, g - HPLACES + 1)
                            dve.wait_ge(hl_ok, g - HPLACES + 1)
                        nc.vector.tensor_tensor(HF[:, g % HPLACES, :], SI[:, j % 3, :], PS[:, 3 + h % 3, :], op=ALU.mult).then_inc(hf_ok, 1)
                    if g:
                        dve.wait_ge(hf_ok, n * PAIRS + j if j <= PAIRS else n * PAIRS)
                        low(g - 1)
                    side((n, j))
            low(2 * NCH * UNITS - 1)
            side((2 * NCH, 0))

        @block.tensor
        def _(pe):
            mm = nc.tensor.matmul

            def ring(key, items, full, free, put):
                n = items[key]
                if n >= 4:
                    pe.wait_ge(free, n - 3)
                put((0 if items is A_ITEM else 4) + n % 4).then_inc(full, 1)

            def transposes(tiles):
                def put(n):
                    for j, t in enumerate(tiles):
                        last = nc.tensor.transpose(PS[:, n, j * P:j * P + t.shape[0]], t, ident[0:t.shape[0], 0:t.shape[0]])
                    return last
                return put

            pe.wait_ge(ident_ok, 1)
            pe.wait_ge(ld_w, 32)
            ring("wT", A_ITEM, a_full, a_free, transposes([WQKV[:, j, :] for j in range(3)] + [WPRJ[:]]))

            def chunk(w, c):
                return lambda n: mm(PS[:, n, :], w, XT[:, c * BANK:(c + 1) * BANK], start=True, stop=True)

            def tokens(src, w, c):
                def put(n):
                    for j in range(4):
                        t = 4 * c + j
                        last = mm(PS[:, n, j * P:(j + 1) * P], src[:, t * P:(t + 1) * P], w, start=True, stop=True)
                    return last
                return put

            def queries_and_keys(c):
                pe.wait_ge(a_free, A_ITEM["xT", c] + 1)
                for j in range(2):
                    ring(("qk", j, c), D_ITEM, d_full, qk_r1, chunk(WT[:, j, :], c))

            for c in range(NCH):
                pe.wait_ge(ln_xn, LN["a", c] + 1)
                ring(("xT", c), A_ITEM, a_full, a_free, transposes([XC[:, 4 * c + j, :] for j in range(4)]))
                if c:
                    queries_and_keys(c - 1)
            queries_and_keys(NCH - 1)
            for c in range(NCH):
                ring(("va", c), A_ITEM, a_full, a_free, tokens(XT, WT[:, 2, :], c))

            def centroids(n):
                nc.tensor.transpose(PS[:, n, 0:E], CENT[:], ident[0:E, 0:E])
                return nc.tensor.transpose(PS[:, n, E:E + DIM], WB[:, 2, :], ident[:])

            pe.wait_ge(ld_b, 16 * 5)
            ring("centT", A_ITEM, a_full, a_free, centroids)
            pe.wait_ge(qk_r1, 2 * NCH)
            pe.wait_ge(a_free, A_ITEM["centT"] + 1)
            pe.wait_ge(identb_ok, 1)

            def m_items(i, which):
                at = i * ITEMS_PER_BODY
                for key in which:
                    it = ITEM[key]
                    e = 2 * (it % 2)
                    if it >= 2:
                        pe.wait_ge(m_free, at + (it - 1))
                    if key[0] == "max":
                        ga, a = key[1] // QPG, 2 * (key[1] % QPG) + key[2]
                        r, nt, u = a // TB, a % TB, ga % 2
                        if a == 0:
                            pe.wait_ge(qa_ld[u], i * (16 * (R + 1)) + 16 * (R + 1) * (ga // 2 + 1))
                        for h in range(2):
                            last = mm(PS[:, e + h, :], QA[:, u, r, nt * P:(nt + 1) * P], KA[:, u, h * BANK:(h + 1) * BANK],
                                      start=True, stop=True)
                    elif key[0] == "shift":
                        ga = key[1]
                        pe.wait_ge(sh_split, i * 8 + 4 * (ga + 1))
                        last = nc.tensor.transpose(PS[0:3 * R * TB, e, 0:P // 2].bitcast(BF16), SHP[:, ga % 2, :], identb[:])
                    else:
                        gg, half = key[1], key[2]
                        pe.wait_ge(o_evac, i * 4 + 2 * gg + half + 1)
                        for j in range(4):
                            last = nc.tensor.transpose(PS[:, e, j * P:(j + 1) * P], OTS[:, half, j * P:(j + 1) * P], ident[:])
                    last.then_inc(m_full, 1)

            def scores(i, s, r):
                g, n, q = i * BODY + s, R * s + r, s % QPG
                half, mt, u = q // TB, q % TB, s // QPG % 2
                if q == 0 and r == 0:
                    grp = s // QPG
                    pe.wait_ge(kb_ld[u], i * (16 * R) + 16 * R * (grp // 2 + 1))
                    pe.wait_ge(sh_r, i * 128 + 64 * (grp + 1))
                if n in SCORE_BANK:
                    if TILE_BEFORE[n] is None:
                        pe.wait_ge(m_free, ITEM["max", NQ - 1, 1] + 1)
                    else:
                        pe.wait_ge(p_ready, TILE_BEFORE[n] + 1)
                elif n >= 3:
                    pe.wait_ge(p_ready, g * R + (r - 1 if n in (R * HEAD_Q, R * HEAD_Q + 1) else r - 2))
                mm(PS[:, SCORE_BANK.get(n, 4 + n % 3), :], KB[:, u, r, mt * P:(mt + 1) * P], QB[:, u, half * BANK:(half + 1) * BANK],
                   start=True, stop=True).then_inc(s_full, 1)

            def weighted_values(i, s):
                g, q = i * BODY + s, s % QPG
                mt, u = q % TB, s // QPG % 2
                pe.wait_ge(p_ready, g * R + R)
                if q == 0:
                    pe.wait_ge(v_cp, i * 2 + s // QPG + 1)
                if mt == 0 and s:
                    pe.wait_ge(o_evac, i * 4 + s // TB)
                for r in range(R):
                    last = mm(PS[STRIP * r:STRIP * (r + 1), 7, :], VG[:, u, mt, r // 2, :], PR[:, s % PRING, r, :],
                              start=mt == 0, stop=mt == TB - 1)
                last.then_inc(av_done, 1)

            def quad(i, s, with_scores=True, values=None):
                items = quad_items(s)
                cut = (len(items) + 1) // 2
                if with_scores:
                    scores(i, s, 0)
                    scores(i, s, 1)
                m_items(i, items[:cut])
                if with_scores:
                    scores(i, s, 2)
                    scores(i, s, 3)
                if len(items) < 3:
                    m_items(i, items[cut:])
                if s >= NQ - BODY + HEAD_Q:
                    side(s)
                if values is not None:
                    weighted_values(i, values)
                if len(items) == 3:
                    m_items(i, items[cut:])

            def side(where):
                bank = TAIL_BANK if isinstance(where, int) else SIDE_BANK
                for item in SIDE.get(where, ()):
                    stage, arg = item
                    if item not in SIDE_ITEM:
                        continue
                    if SIDE_ITEM[item]:
                        pe.wait_ge(side_free, SIDE_ITEM[item])
                    else:
                        pe.wait_ge(m_free, ITEM["max", NQ - 1, 1] + 1)
                    if stage == "heads_T":
                        pe.wait_ge(heads_ok, arg // 2 + 1)
                        last = transposes([XC[:, 4 * arg + j, :] for j in range(4)])(bank)
                    elif stage == "proj":
                        last = tokens(XT, WT[:, 3, :], arg)(bank)
                    elif stage == "x_T":
                        c = chunk_of(arg)
                        pe.wait_ge(ln_xn, LN[arg] + 1)
                        last = transposes([XC[:, 4 * c + j, :] for j in range(4)])(bank)
                    elif stage == "affinity":
                        for j in range(4):
                            t = 4 * (arg % NCH) + j
                            last = mm(PS[:, bank, j * E:(j + 1) * E], XT[:, t * P:(t + 1) * P], CT[:], start=True, stop=True)
                    elif stage == "gate_T":
                        pe.wait_ge(ch_ok, arg + 1)
                        last = transposes([CH[:, j, :] for j in range(4)])(bank)
                    elif stage == "y_T":
                        pe.wait_ge(y_evac, arg + 1)
                        last = transposes([YS[:, j * P:(j + 1) * P] for j in range(4)])(bank)
                    elif stage == "gram":
                        for j in range(TB):
                            t = XC[:, arg * TB + j, :]
                            last = mm(PS[:, bank, 0:DIM], t, t, start=j == 0, stop=j == TB - 1)
                    elif stage == "gram_k":
                        last = mm(PS[:, bank, 0:DIM], GRAM[:, arg, :], WB[:, 1, :], start=True, stop=True)
                    elif stage == "q_k":
                        last = mm(PS[:, bank, 0:DIM], WB[:, 0, :], GK[:, arg, :], start=True, stop=True)
                    elif stage == "energy":
                        pe.wait_ge(blk_ok, 1)
                        last = mm(PS[:, bank, 0:HEADS_B], BLK[:], QKR[:], start=True, stop=True)
                    elif stage == "mix_T":
                        pe.wait_ge(mix_in, arg + 1)
                        last = nc.tensor.transpose(PS[:, bank, 0:DIM], MIXT[:], ident[:])
                    elif stage == "v_mix":
                        last = mm(PS[:, bank, 0:DIM], WVT[:], MIX[:], start=True, stop=True)
                    elif stage == "v_all":
                        last = chunk(VMIX[:, arg // 2, :], arg)(bank)
                    elif stage == "out_b":
                        pe.wait_ge(mix_r[arg // 2], 16 * S0)
                        last = tokens(RT[:].rearrange("p b n -> p (b n)"), WB[:, 3, :], arg)(bank)
                    last.then_inc(side_full, 1)

            for s in range(-LEAD, 0):
                quad(0, s, False)
            for s in range(HEAD_Q):
                quad(0, s, values=s - 1 if s else None)
            with pe.Fori(0, LOOPS) as i:
                for s in range(HEAD_Q, HEAD_Q + BODY):
                    quad(i, s, values=s - 1)
            for s in range(NQ - BODY + HEAD_Q, NQ):
                quad(0, s, values=s - 1)
            weighted_values(0, NQ - 1)

            def split3(dst, ah, al, bh, bl, first, last):
                mm(dst, ah, bh, start=first, stop=False)
                mm(dst, ah, bl, start=False, stop=False)
                return mm(dst, al, bh, start=False, stop=last)

            def up(n, j):
                g, h, cols = n * UNITS + j, n * PAIRS + j, slice(n % NCH * BANK, (n % NCH + 1) * BANK)
                wh, wl = (WUH[:, j * P:(j + 1) * P], WUL[:, j * P:(j + 1) * P]) if j < PAIRS else (WSUH[:], WSUL[:])
                if g >= 3:
                    pe.wait_ge(silu_ok, g - 2)
                split3(PS[:, j % 3, :], wh, wl, XH[:, cols], XL[:, cols], True, True).then_inc(z_full, 1)
                if j < PAIRS:
                    if h >= 3:
                        pe.wait_ge(hf_ok, h - 2)
                    mm(PS[:, 3 + h % 3, :], SEL[:, j * P:(j + 1) * P], CWT[:, n % 2, :], start=True, stop=True).then_inc(c_full, 1)

            def down(g):
                n, j = divmod(g, UNITS)
                wh, wl = (WDH[:, j * DIM:(j + 1) * DIM], WDL[:, j * DIM:(j + 1) * DIM]) if j < PAIRS else (WSDH[:], WSDL[:])
                if j == 0 and n:
                    pe.wait_ge(y_evac, n)
                pe.wait_ge(hh_ok, g + 1)
                pe.wait_ge(hl_ok, g + 1)
                split3(PS[:, DOWN_BANK, :], wh, wl, HH[:, g % HPLACES, :], HL[:, g % HPLACES, :], j == 0, j == UNITS - 1).then_inc(down_ok, 1)

            def operands(n):
                pe.wait_ge(xl_ok, n + 1)
                pe.wait_ge(side_free, SIDE_ITEM["gate_T", n] + 1)

            assert ITEM["out", NG - 1, 1] % 2 == 1
            operands(0)
            pe.wait_ge(m_free, ITEM["out", NG - 1, 1])
            up(0, 0)
            for s in range(NQ, NQ + 4):
                quad(0, s, False)
            for n in range(2 * NCH):
                if n:
                    operands(n)
                for j in range(UNITS):
                    if (n, j) == (0, 2):
                        pe.wait_ge(m_free, len(ITEM))
                    if (n, j) != (0, 0):
                        up(n, j)
                    side((n, j))
                    for g in ([n * UNITS + j - LAG] if j > LAG + 1 or (n and j < LAG) else
                              [n * UNITS, n * UNITS + 1] if j == LAG + 1 else []):
                        down(g)
            for g in range(2 * NCH * UNITS - LAG, 2 * NCH * UNITS):
                down(g)
            side((2 * NCH, 0))


_INS = ["L0_attn_a_x", "L0_attn_a_w_qkv", "L0_attn_a_w_proj", "L0_attn_a_b_proj", "L0_attn_a_lambda_q1",
        "L0_attn_a_lambda_k1", "L0_attn_a_lambda_q2", "L0_attn_a_lambda_k2", "L0_attn_a_sub_norm_w",
        "L0_attn_b_Wq", "L0_attn_b_Wk", "L0_attn_b_Wv", "L0_attn_b_Wo", "L0_attn_b_bo", "L0_ffn_centroids",
        "L0_ffn_expert_biases", "L0_ffn_Ws_up", "L0_ffn_Ws_down", "L0_ffn_W_up", "L0_ffn_W_down"]
_OUTS = [((BATCH, SEQ, DIM), "float32")]


def kernel(**inputs):
    import numpy as _np
    import concourse.bacc as _bacc
    from concourse import mybir as _mybir
    from concourse.bass_utils import run_bass_kernel_spmd as _run

    nc = _bacc.Bacc("TRN2", target_bir_lowering=False, num_devices=1)
    arrays, args = {}, []
    for name in _INS:
        a = _np.ascontiguousarray(inputs[name])
        arrays[f"in_{name}_dram"] = a
        args.append(nc.dram_tensor(f"in_{name}_dram", a.shape, _mybir.dt.from_np(a.dtype), kind="ExternalInput").ap())
    for i, (shape, dtype) in enumerate(_OUTS):
        dt = _mybir.dt.from_np(_np.dtype(dtype))
        args.append(nc.dram_tensor(f"out_{i}_dram", shape, dt, kind="ExternalOutput").ap())
    hybrid_layer(nc, *args)
    r = _run(nc, [arrays], core_ids=[0])
    return r.results[0]["out_0_dram"]
```
